# Optimizing a Trainium2 kernel written in Bass

```python
import numpy as np
import jax
import jax.numpy as jnp

def _softmax(x, axis=-1):
    return jax.nn.softmax(x, axis=axis)

def _gelu(x):
    return jax.nn.gelu(x, approximate=True)

def _silu(x):
    return jax.nn.silu(x)

def _sigmoid(x):
    return jax.nn.sigmoid(x)

def _layernorm(x, axis=-1, eps=1e-05):
    m = jnp.mean(x, axis=axis, keepdims=True)
    v = jnp.var(x, axis=axis, keepdims=True)
    return (x - m) / jnp.sqrt(v + eps)

def _scatter_add(tgt, idx, src, axis=0):
    return tgt.at[idx].add(src)

def _segment_sum(src, seg, n):
    return jax.ops.segment_sum(src, seg, n)
kernel_name = 'mk_xattn_ffn_d1_seqx_r8_7d4d0a'

def setup_inputs(seed: int=0):
    np.random.seed(seed)
    _w = jnp.asarray

    def _rec_inputs():
        import jax
        import jax.numpy as jnp
        _rk = jax.random.key(seed)
        x = -0.0002928 + 1 * jax.random.normal(jax.random.fold_in(_rk, 1), (32, 128, 128), jnp.float32)
        _lenS = 128 - jax.random.randint(jax.random.fold_in(_rk, 7), (32,), 0, max(1, 128 // 4) + 1, jnp.int32)
        _lenS2 = 128 - jax.random.randint(jax.random.fold_in(_rk, 8), (32,), 0, max(1, 128 // 4) + 1, jnp.int32)
        _ctx_1024P = jax.random.normal(jax.random.fold_in(_rk, 11), (32, 16, 128), jnp.float32)
        _ctx_1024c = jax.random.dirichlet(jax.random.fold_in(_rk, 511), 0.3 * jnp.ones((16,), jnp.float32), (32, 128))
        _ctx_1024t = jnp.einsum('bsk,bkd->bsd', _ctx_1024c, _ctx_1024P)
        _ctx_1024t = _ctx_1024t * jax.lax.rsqrt(jnp.mean(jnp.square(_ctx_1024t)) + 1e-12) * 0.953939
        ctx_1024 = -1.39393e-06 + 0.999914 * (_ctx_1024t + 0.3 * jax.random.normal(jax.random.fold_in(_rk, 611), (32, 128, 128), jnp.float32))
        return (x, ctx_1024)
    x, ctx_1024 = _rec_inputs()

    def _L0_xattn_setup():
        import jax, jax.numpy as jnp
        import numpy as np
        HEADS = 16
        DIM_HEAD = 64
        key = jax.random.key(seed)
        k1, k2, k3, k4 = jax.random.split(key, 4)
        b, sq, skv, dim = (2, 256, 256, 128)
        inner = HEADS * DIM_HEAD
        return {'x_q': jax.random.normal(k1, (b, sq, dim), dtype=jnp.float32), 'x_kv': jax.random.normal(k2, (b, skv, dim), dtype=jnp.float32), 'W_qkv': jax.random.normal(k3, (dim, 3 * inner), dtype=jnp.float32) * dim ** (-0.5), 'W_out': jax.random.normal(k4, (inner, dim), dtype=jnp.float32) * inner ** (-0.5), 'b_out': jnp.zeros((dim,), dtype=jnp.float32)}
    _L0_xattn_all = _L0_xattn_setup()
    _L0_xattn_in = {k: v for k, v in _L0_xattn_all.items() if k in ('W_qkv', 'W_out', 'b_out')}
    del _L0_xattn_all

    def _L0_ffn_setup():
        import jax, jax.numpy as jnp
        import numpy as np
        B, S, H = (1, 128, 128)
        E = 128
        NEXP = 16
        TOPK = 2
        ALPHA = 1.702
        LIMIT = 7.0

        def _moe_forward(x, Wg, bg, Wgu, bgu, Wd, bd):
            b, s, h = x.shape
            xt = x.reshape(-1, h)
            logits = xt @ Wg.T + bg
            top_vals, top_idx = jax.lax.top_k(logits, TOPK)
            rw = jax.nn.softmax(top_vals.astype(jnp.float32), axis=-1).astype(xt.dtype)
            onehot = jax.nn.one_hot(top_idx, NEXP, dtype=xt.dtype)
            cw = jnp.einsum('tk,tke->te', rw, onehot)
            gu = jnp.einsum('th,ehf->tef', xt, Wgu) + bgu[None]
            gate = gu[..., ::2]
            up = gu[..., 1::2]
            gate = jnp.minimum(gate, LIMIT)
            up = jnp.clip(up, -LIMIT, LIMIT)
            glu = gate * jax.nn.sigmoid(gate * ALPHA)
            gated = (up + 1.0) * glu
            out_e = jnp.einsum('tef,efh->teh', gated, Wd) + bd[None]
            out = jnp.einsum('teh,te->th', out_e, cw)
            return out.reshape(b, s, h)
        key = jax.random.key(seed)
        ks = jax.random.split(key, 8)
        hidden_states = jax.random.normal(ks[0], (B, S, H), dtype=jnp.float32)
        Wg = jax.random.normal(ks[1], (NEXP, H), dtype=jnp.float32) / np.sqrt(H)
        bg = jax.random.normal(ks[2], (NEXP,), dtype=jnp.float32) * 0.01
        Wgu = jax.random.normal(ks[3], (NEXP, H, 2 * E), dtype=jnp.float32) / np.sqrt(H)
        bgu = jax.random.normal(ks[4], (NEXP, 2 * E), dtype=jnp.float32) * 0.01
        Wd = jax.random.normal(ks[5], (NEXP, E, H), dtype=jnp.float32) / np.sqrt(E)
        bd = jax.random.normal(ks[6], (NEXP, H), dtype=jnp.float32) * 0.01
        return {'hidden_states': hidden_states, 'Wg': Wg, 'bg': bg, 'Wgu': Wgu, 'bgu': bgu, 'Wd': Wd, 'bd': bd}
    _L0_ffn_all = _L0_ffn_setup()
    _L0_ffn_in = {k: v for k, v in _L0_ffn_all.items() if k in ('Wg', 'bg', 'Wgu', 'bgu', 'Wd', 'bd')}
    del _L0_ffn_all
    return {'x': x, 'ctx_1024': ctx_1024, 'L0_xattn_W_qkv': _L0_xattn_in['W_qkv'], 'L0_xattn_W_out': _L0_xattn_in['W_out'], 'L0_xattn_b_out': _L0_xattn_in['b_out'], 'L0_ffn_Wg': _L0_ffn_in['Wg'], 'L0_ffn_bg': _L0_ffn_in['bg'], 'L0_ffn_Wgu': _L0_ffn_in['Wgu'], 'L0_ffn_bgu': _L0_ffn_in['bgu'], 'L0_ffn_Wd': _L0_ffn_in['Wd'], 'L0_ffn_bd': _L0_ffn_in['bd']}

def reference(x, ctx_1024, L0_xattn_W_qkv, L0_xattn_W_out, L0_xattn_b_out, L0_ffn_Wg, L0_ffn_bg, L0_ffn_Wgu, L0_ffn_bgu, L0_ffn_Wd, L0_ffn_bd):
    import jax
    import jax.numpy as jnp

    def _L0_xattn_ref(x_q, x_kv, W_qkv, W_out, b_out):
        import jax, jax.numpy as jnp
        import numpy as np
        HEADS = 16
        DIM_HEAD = 64
        b, sq, dim = x_q.shape
        skv = x_kv.shape[1]
        inner = HEADS * DIM_HEAD
        scale = DIM_HEAD ** (-0.5)
        qkv = jnp.concatenate([x_q, x_kv], axis=1) @ W_qkv
        q, k, v = jnp.split(qkv, 3, axis=-1)
        q = q[:, :sq].reshape(b, sq, HEADS, DIM_HEAD).transpose(0, 2, 1, 3)
        k = k[:, sq:].reshape(b, skv, HEADS, DIM_HEAD).transpose(0, 2, 1, 3)
        v = v[:, sq:].reshape(b, skv, HEADS, DIM_HEAD).transpose(0, 2, 1, 3)
        dots = jnp.einsum('bhqd,bhkd->bhqk', q, k) * scale
        attn = jax.nn.softmax(dots, axis=-1)
        out = jnp.einsum('bhqk,bhkd->bhqd', attn, v)
        out = out.transpose(0, 2, 1, 3).reshape(b, sq, inner)
        return out @ W_out + b_out

    def _L0_ffn_ref(hidden_states, Wg, bg, Wgu, bgu, Wd, bd):
        import jax, jax.numpy as jnp
        import numpy as np
        B, S, H = (1, 128, 128)
        E = 128
        NEXP = 16
        TOPK = 2
        ALPHA = 1.702
        LIMIT = 7.0

        def _moe_forward(x, Wg, bg, Wgu, bgu, Wd, bd):
            b, s, h = x.shape
            xt = x.reshape(-1, h)
            logits = xt @ Wg.T + bg
            top_vals, top_idx = jax.lax.top_k(logits, TOPK)
            rw = jax.nn.softmax(top_vals.astype(jnp.float32), axis=-1).astype(xt.dtype)
            onehot = jax.nn.one_hot(top_idx, NEXP, dtype=xt.dtype)
            cw = jnp.einsum('tk,tke->te', rw, onehot)
            gu = jnp.einsum('th,ehf->tef', xt, Wgu) + bgu[None]
            gate = gu[..., ::2]
            up = gu[..., 1::2]
            gate = jnp.minimum(gate, LIMIT)
            up = jnp.clip(up, -LIMIT, LIMIT)
            glu = gate * jax.nn.sigmoid(gate * ALPHA)
            gated = (up + 1.0) * glu
            out_e = jnp.einsum('tef,efh->teh', gated, Wd) + bd[None]
            out = jnp.einsum('teh,te->th', out_e, cw)
            return out.reshape(b, s, h)
        return _moe_forward(hidden_states, Wg, bg, Wgu, bgu, Wd, bd)
    x = x + _L0_xattn_ref(_layernorm(x, axis=-1), ctx_1024, L0_xattn_W_qkv, L0_xattn_W_out, L0_xattn_b_out)
    x = x + _L0_ffn_ref(_layernorm(x, axis=-1), L0_ffn_Wg, L0_ffn_bg, L0_ffn_Wgu, L0_ffn_bgu, L0_ffn_Wd, L0_ffn_bd)
    return x

_drawn_inputs = setup_inputs


def setup_inputs(seed=0):
    import zlib

    import numpy as np

    out = dict(_drawn_inputs(seed))
    spreads = {'L0_xattn_b_out': (0.0, 0.1)}
    factors = {'L0_ffn_bgu': 8.0, 'L0_ffn_bd': 8.0}
    for name, (base, spread) in spreads.items():
        noise = np.random.default_rng([zlib.crc32(name.encode()), seed]).standard_normal(out[name].shape)
        drawn = base * np.exp(spread * noise) if base else spread * noise
        out[name] = jnp.asarray(drawn.astype(out[name].dtype))
    for name, factor in factors.items():
        out[name] = (out[name] * factor).astype(out[name].dtype)
    return out
```

```python
from contextlib import ExitStack

import concourse.bass as bass
from concourse import mybir

F32 = mybir.dt.float32
F16 = mybir.dt.float16
I32 = mybir.dt.int32
U32 = mybir.dt.uint32
ALU = mybir.AluOpType
ACT = mybir.ActivationFunctionType
AX = mybir.AxisListType

P = 128
HI, LO = 0, 1
TOP = 16.0
TINY = 1e-30
EPS = 1e-5
ALPHA = 1.702
LIMIT = 7.0
NOWHERE = 1 << 20


def xattn_moe_kernel(nc, x, ctx, W_qkv, W_out, b_out, Wg, bg, Wgu, bgu, Wd, bd, out):
    NB, S, D = x.shape
    INNER = W_out.shape[0]
    NE = Wg.shape[0]
    DH = 64
    NH = INNER // DH
    PAIRS = NB // 2
    QUADS = NH // 4
    STEPS = 2 * QUADS
    ALLQ = PAIRS * STEPS
    TOK = NB * S
    ROOM = TOK + P
    ROW = P + 2
    BLOCKS = 2 * TOK // P + NE
    BPAIRS = BLOCKS // 2
    NBUF = 8
    VW = DH + 2
    assert S == P and D == P and NE == 16 and STEPS == 8 and BLOCKS == 80

    places = nc.dram_tensor("places", [NE * ROOM + P, ROW], F32, kind="Internal").ap()
    results = nc.dram_tensor("results", [2 * TOK, D], F32, kind="Internal").ap()

    bias_gu_rows = nc.dram_tensor("bias_gu_rows", [2, 2, NE * P], F16, kind="Internal").ap()
    bias_d_rows = nc.dram_tensor("bias_d_rows", [2, NE * P], F16, kind="Internal").ap()

    es = ExitStack()
    with es:
        def sb(name, shape, dt=F32):
            return es.enter_context(nc.sbuf_tensor(name, shape, dt))

        def sem(name):
            return es.enter_context(nc.semaphore(name))

        banks = [es.enter_context(nc.psum_tensor(f"bank{i}", [P, 512], F32)) for i in range(8)]
        score_bank = banks[0:2]
        pt_bank, o_bank, qk_bank, misc_bank, ot_bank, out_bank = banks[2:8]

        x_sb = sb("x_sb", [P, NB, D])
        ctx_sb = sb("ctx_sb", [P, NB, D])
        stage = sb("stage", [P, 4096])
        w_qkv = sb("w_qkv", [P, 2, 3 * INNER], F16)
        w_out = sb("w_out", [P, 2, 8, D], F16)
        w_gu = sb("w_gu", [P, 2, NE, 256], F16)
        w_d = sb("w_d", [P, 2, NE, D], F16)
        bias_gu = sb("bias_gu", [2, NE, 256], F16)
        bias_d = sb("bias_d", [2, NE, D], F16)
        bgu_sb = sb("bgu_sb", [P, 32])
        bd_sb = sb("bd_sb", [P, 16])
        bgu_half = sb("bgu_half", [P, 2, 2, 16], F16)
        bd_half = sb("bd_half", [P, 2, 16], F16)
        bout_bc = sb("bout_bc", [P, D])
        bg_bc = sb("bg_bc", [P, NE])
        wg_nat = sb("wg_nat", [NE, D])
        wg_T = sb("wg_T", [P, NE])
        largest = sb("largest", [P, 8])
        top = sb("top", [P, 8])
        scale_to = sb("scale_to", [P, 8])
        scale_from = sb("scale_from", [P, 8])
        fac = sb("fac", [P, 8])
        ident = sb("ident", [P, P])
        ident16 = sb("ident16", [P, P], F16)
        ones16 = sb("ones16", [P, P], F16)
        before16 = sb("before16", [P, P], F16)
        expert_no = sb("expert_no", [P, NE])
        next_place = sb("next_place", [P, 2, NE])
        row_no = sb("row_no", [P, NB, 2], I32)
        minus_half = sb("minus_half", [P, 2])
        part_no = sb("part_no", [P, 1])
        blank = sb("blank", [P, ROW])
        xhat = sb("xhat", [P, 2, 2, D])
        xT = sb("xT", [P, 2, 2, 512], F16)
        stats = sb("stats", [P, 2, 6])
        mv = sb("mv", [P, 2, 2])
        var_eps = sb("var_eps", [P, 2])
        rstd = sb("rstd", [P, 2])
        zeros = sb("zeros", [P, 512])
        qkf = sb("qkf", [P, 2, 512])
        qk = sb("qk", [P, 2, 2, 2, 8, 256], F16)
        v = sb("v", [P, 2, 2, 2, NH, VW], F16)
        qmax = sb("qmax", [P, 2, 4])
        nbias = sb("nbias", [P, 2, 4])
        probs = sb("probs", [P, 2, 4, P])
        pT = sb("pT", [P, 2, 2, 512], F16)
        rsum = sb("rsum", [P, 4])
        o_nat = sb("o_nat", [P, 2, 256])
        oT = sb("oT", [P, 2, 2, 256], F16)
        stats2 = sb("stats2", [P, 2, 6])
        mv2 = sb("mv2", [P, 2, 2])
        var_eps2 = sb("var_eps2", [P, 2])
        rstd2 = sb("rstd2", [P, 2])
        y = sb("y", [P, 2, D])
        yT = sb("yT", [P, 256])
        logits = sb("logits", [P, 2, NE])
        best = sb("best", [P, 2, 8])
        best_at = sb("best_at", [P, 2, 8], U32)
        choice = sb("choice", [P, 4])
        gap = sb("gap", [P, 2])
        egap = sb("egap", [P, 2])
        onehot = sb("onehot", [P, 4, NE])
        chosen16 = sb("chosen16", [P, 2, NE], F16)
        place_all = sb("place_all", [P, 2, NE])
        picked = sb("picked", [P, 4, NE])
        slots = sb("slots", [P, 2, 4], U32)
        denom = sb("denom", [P, 2])
        payload = sb("payload", [P, 2, 2, 2, ROW])
        rows_in = sb("rows_in", [P, NBUF, 2, ROW])
        bT = sb("bT", [P, 2, 2, 2, P], F16)
        gate = sb("gate", [P, 2, P])
        up = sb("up", [P, 2, P])
        sig = sb("sig", [P, 2, P])
        glu = sb("glu", [P, 2, P])
        hidden = sb("hidden", [P, 2, 2, P])
        hT = sb("hT", [P, 2, 2, 256], F16)
        z = sb("z", [P, 4, 2, P])
        blocks_f = sb("blocks_f", [P, 6, NE])
        blocks_i = sb("blocks_i", [P, NE], I32)
        table_f = sb("table_f", [P, 4])
        table = sb("table", [1, 2, P], I32)
        ends = sb("ends", [1, NE], I32)

        names = """carrier in_w in_x in_ctx in_small in_wo in_wd in_wgu
        zeroed consts ones_v blank_ok blank_in absmax allmax scales scales2
        w_hi w_lo wo_hi wo_lo d_hi d_lo gu_hi gu_lo bias_half bias_out bias_in wgT_mm wgT_ok setup
        stat stat_agg pool_add rstd_ok xhat_ok x_bias prep_mm prep_hi
        qk_mm qk_copied qk_high qk_split v_mm v_hi misc_free
        score_mm qmax_ok nbias_ok exp_ok pt_mm pt_hi pt_lo pv_mm rsum_ok o_ok ot_mm ot_hi ot_lo out_mm
        x1_ok stat2 stat2_agg rstd2_ok y_ok yhalf yT_mm lg_mm rank_mm
        best_ok best_at_ok gap_ok choice_ok onehot_ok chosen_ok egap_ok
        place_ok picked_ok slots_ok denom_ok wgt_ok
        table_cols table_mm table_ok ends_ok cleared
        t_mm t_ok gu_mm gate_ok up_ok sig_ok glu_ok h_ok ht_mm ht_hi ht_lo d_mm z_ok
        sum_ok fin_ok fin_sent""".split()
        s = {n: sem("s_" + n) for n in names}
        block_in = [sem(f"s_block_in{i}") for i in range(NBUF)]
        scattered = [sem(f"s_scattered{i}") for i in range(2)]
        z_sent = [sem(f"s_z_sent{i}") for i in range(4)]
        results_in = [sem(f"s_results_in{i}") for i in range(4)]

        def wait(eng, name, value):
            if not isinstance(value, int) or value > 0:
                eng.wait_ge(s[name], value)

        def wait_alone(eng, name, value):
            wait(eng, name, value)
            if not isinstance(value, int):
                eng.sem_inc(s["carrier"], 1)

        def live(p, r, lag):
            return not isinstance(p, int) or 0 <= p * STEPS + r - lag < ALLQ

        def pair_live(q):
            return not isinstance(q, int) or 0 <= q < PAIRS

        USES = {"LG": -2, "V0": 1, "V1": 1, "RANK": -2, "PREP": 2, "V2": 1, "V3": 1, "YT": -1}
        ORDER = list(USES)

        def misc_before(p, item):
            if not isinstance(p, int):
                return p * len(ORDER) + (misc_before(2, item) - 2 * len(ORDER))
            before = [(pp, it) for pp in range(p) for it in ORDER]
            before += [(p, it) for it in ORDER[:ORDER.index(item)]]
            return 6 + sum(0 <= pp + USES[it] < PAIRS for pp, it in before)

        FIRST, LAST = 2, PAIRS - 2

        def over_pairs(eng, body):
            for p in range(FIRST):
                body(p, p % 2)
            with eng.Fori(0, (LAST - FIRST) // 2) as i:
                body(i * 2 + FIRST, 0)
                body(i * 2 + FIRST + 1, 1)
            for p in range(LAST, PAIRS + 2):
                body(p, p % 2)

        STAGES = 3

        def block_live(q, lag):
            return not isinstance(q, int) or 0 <= q - lag < BPAIRS

        def sent_count(q, u, by):
            if isinstance(q, int):
                return 32 * ((q + by) // 4)
            return q * 8 + (32 * ((u + by) // 4) - 8 * u)

        def over_blocks(eng, body):
            for q in range(NBUF):
                body(q, q)
            with eng.Fori(1, BPAIRS // NBUF) as i:
                for u in range(NBUF):
                    body(i * NBUF + u, u)
            for q in range(BPAIRS, BPAIRS + STAGES):
                body(q, q % NBUF)

        halves = payload[:, :, :, :, 0:P].bitcast(F16)
        rows16 = rows_in[:, :, :, 0:P].bitcast(F16)
        t_bank = banks[0][:, :].bitcast(F16)
        gu_bank = banks[1:3]
        ht_bank, d_bank, table_bank = banks[3], banks[4], banks[5]
        r_in = ctx_sb[:, 0:NB, :].rearrange("p (u c b) d -> p u c b d", u=4, c=2)

        block = es.enter_context(nc.Block())

        @block.sync
        def _(sp):
            sp.dma_start(stage[:, 0:3 * INNER], W_qkv).then_inc(s["in_w"], 16)
            sp.dma_start(x_sb[:, 0:4, :], x[0:4].rearrange("b t d -> t b d")).then_inc(s["in_x"], 16)
            sp.dma_start(x_sb[:, 4:NB, :], x[4:NB].rearrange("b t d -> t b d")).then_inc(s["in_x"], 16)
            by_head = W_out.rearrange("(h j i c d) n -> h c j i d n", h=2, j=2, i=2, c=2)
            for h in range(2):
                for c in range(2):
                    for i in range(2):
                        at = 3 * INNER + (2 * h + c) * 256
                        sp.dma_start(stage[64 * i:64 * i + 64, at:at + 256].rearrange("d (j n) -> d j n", j=2),
                                     by_head[h, c, :, i].rearrange("j d n -> d j n")).then_inc(s["in_wo"], 16)
            sp.wait_ge(s["w_lo"], 1)
            sp.dma_start(stage[:, 0:NE * D].rearrange("f (e n) -> f e n", e=NE),
                         Wd.rearrange("e f n -> f e n")).then_inc(s["in_wd"], 16)
            sp.wait_ge(s["wo_lo"], 1)
            sp.wait_ge(s["d_lo"], 1)
            sp.dma_start(stage[:, :].rearrange("h (e n) -> h e n", e=NE),
                         Wgu.rearrange("e h n -> h e n")).then_inc(s["in_wgu"], 16)
            sp.wait_ge(s["bias_half"], 3)
            for half in range(2):
                for c in range(2):
                    sp.dma_start(bias_gu_rows[half, c].rearrange("(k f) -> k f", f=16),
                                 bgu_half[:, half, c, :]).then_inc(s["bias_out"], 16)
                sp.dma_start(bias_d_rows[half].rearrange("(k f) -> k f", f=16), bd_half[:, half, :]).then_inc(s["bias_out"], 16)
            sp.wait_ge(s["bias_out"], 16 * 6)
            for half in range(2):
                sp.dma_start(bias_gu[half:half + 1].rearrange("o e (c f) -> o e c f", c=2),
                             bias_gu_rows[half:half + 1].rearrange("o c (e f) -> o e c f", e=NE)).then_inc(s["bias_in"], 16)
                sp.dma_start(bias_d[half:half + 1].rearrange("o e f -> o (e f)"), bias_d_rows[half:half + 1]).then_inc(s["bias_in"], 16)
            sp.wait_ge(s["blank_ok"], 2)
            sp.dma_start(places[NE * ROOM:NE * ROOM + P, :], blank[:, :]).then_inc(s["blank_in"], 16)

            sp.wait_ge(s["ends_ok"], 1)
            for e in range(NE):
                end = sp.value_load(ends[0:1, e:e + 1], min_val=e * ROOM, max_val=e * ROOM + TOK)
                sp.dma_start(places[bass.ds(end, P), :], blank[:, :]).then_inc(s["cleared"], 16)
            for par in range(2):
                sp.wait_ge(scattered[par], 64 * (PAIRS // 2))
            sp.wait_ge(s["cleared"], 16 * NE)
            sp.wait_ge(s["blank_in"], 16)
            sp.wait_ge(s["table_ok"], 1)

            def load(q, u):
                if block_live(q, 0):
                    if not isinstance(q, int) or q >= NBUF:
                        sp.wait_ge(z_sent[u % 4], sent_count(q, u, -4))
                    for t in range(2):
                        place = sp.value_load(table[0:1, 1, bass.ds(q * 2 + t, 1)], min_val=0, max_val=NE * ROOM)
                        sp.dma_start(rows_in[:, u, t, :], places[bass.ds(place, P), :]).then_inc(block_in[u], 16)

            over_blocks(sp, load)

            for k in range(4):
                sp.wait_ge(z_sent[k], 32 * (BPAIRS // 4))
            res = results.rearrange("(c b p) d -> c p b d", c=2, p=P)
            for g in range(NB // 4):
                if g >= 4:
                    sp.wait_ge(s["fin_ok"], g - 3)
                for c in range(2):
                    sp.dma_start(r_in[:, g % 4, c], res[c, :, 4 * g:4 * g + 4]).then_inc(results_in[g % 4], 16)

        @block.scalar
        def _(act):
            act.dma_start(ctx_sb[:, :, :], ctx.rearrange("b t d -> t b d")).then_inc(s["in_ctx"], 16)
            act.dma_start(bout_bc[:, :], b_out.rearrange("(o d) -> o d", o=1).broadcast_to([P, D])).then_inc(s["in_small"], 16)
            act.dma_start(bg_bc[:, :], bg.rearrange("(o d) -> o d", o=1).broadcast_to([P, NE])).then_inc(s["in_small"], 16)
            act.dma_start(wg_nat[:, :], Wg).then_inc(s["in_small"], 16)
            act.dma_start(bgu_sb[:, :], bgu.rearrange("e (k f) -> (e k) f", k=8)).then_inc(s["in_small"], 16)
            act.dma_start(bd_sb[:, :], bd.rearrange("e (k f) -> (e k) f", k=8)).then_inc(s["in_small"], 16)
            act.wait_ge(s["scales"], 1)
            nc.scalar.activation(w_qkv[:, HI, :], stage[:, 0:3 * INNER], ACT.Copy, scale=scale_to[:, 0:1]).then_inc(s["w_hi"], 1)
            nc.scalar.activation(w_out[:, HI].rearrange("p b n -> p (b n)"), stage[:, 3 * INNER:4096], ACT.Copy, scale=scale_to[:, 2:3]).then_inc(s["wo_hi"], 1)
            for q in range(2):
                act.wait_ge(s["prep_mm"], q + 1)
                nc.scalar.activation(xT[:, q, HI, :], misc_bank[:, :], ACT.Copy).then_inc(s["prep_hi"], 1)

            def copy_qk(q, t):
                wait(act, "qk_mm", q * 8 + t + 1)
                wait(act, "qk_split", q * 8 + t - 1)
                nc.scalar.activation(qkf[:, t % 2, :], qk_bank[:, :], ACT.Copy).then_inc(s["qk_copied"], 1)

            def v_high(q, par, k):
                wait(act, "v_mm", q * 4 + k + 1)
                wait(act, "pv_mm", q * 8 - 12 + 4 * (k // 2))
                nc.scalar.activation(v[:, par, HI, k // 2, 8 * (k % 2):8 * (k % 2) + 8, 0:DH],
                                     misc_bank[:, :].rearrange("p (h d) -> p h d", h=8), ACT.Copy).then_inc(s["v_hi"], 1)

            for t in range(8):
                copy_qk(0, t)
                if t < 4:
                    v_high(0, 0, t)

            act.wait_ge(s["scales2"], 1)
            act.wait_ge(s["in_wd"], 16)
            nc.scalar.activation(w_d[:, HI, :, :].rearrange("p e n -> p (e n)"), stage[:, 0:NE * D], ACT.Copy,
                                 scale=scale_to[:, 3:4]).then_inc(s["d_hi"], 1)
            act.wait_ge(s["scales2"], 2)
            for c in range(2):
                nc.scalar.activation(w_gu[:, HI, :, c * P:(c + 1) * P],
                                     stage[:, :].rearrange("p (e f c) -> p c e f", e=NE, c=2)[:, c], ACT.Copy,
                                     scale=scale_to[:, 5:6]).then_inc(s["gu_hi"], 1)

            def steps(p, par):
                for r in range(STEPS):
                    n = p * STEPS + r
                    if live(p, r, 5):
                        wait(act, "ot_mm", n - 4)
                        wait(act, "out_mm", n - 6)
                        nc.scalar.activation(oT[:, (r + 1) % 2, HI, :], ot_bank[:, 0:256], ACT.Copy).then_inc(s["ot_hi"], 1)
                    if live(p, r, 1):
                        wait(act, "nbias_ok", n)
                        wait(act, "pt_mm", n - 2)
                        b = (r + 1) % 2
                        for k in range(4):
                            last = nc.scalar.activation(probs[:, b, k, :], score_bank[b][:, k * P:(k + 1) * P],
                                                        ACT.Exp, bias=nbias[:, b, k:k + 1], scale=fac[:, 0:1])
                        last.then_inc(s["exp_ok"], 1)
                    if r == 3 and pair_live(p - 2):
                        wait(act, "gap_ok", p - 1)
                        nc.scalar.activation(egap[:, :], gap[:, :], ACT.Exp).then_inc(s["egap_ok"], 1)
                    if pair_live(p + 1):
                        copy_qk(p + 1, r)
                    if live(p, r, 2):
                        wait(act, "pt_mm", n - 1)
                        wait(act, "pv_mm", n - 3)
                        nc.scalar.activation(pT[:, r % 2, HI, :], pt_bank[:, :], ACT.Copy).then_inc(s["pt_hi"], 1)
                    if ORDER[r][0] == "V" and pair_live(p + 1):
                        v_high(p + 1, 1 - par, int(ORDER[r][1]))
                    if ORDER[r] == "PREP" and pair_live(p + 2):
                        wait(act, "prep_mm", p + 3)
                        nc.scalar.activation(xT[:, par, HI, :], misc_bank[:, :], ACT.Copy).then_inc(s["prep_hi"], 1)
                    if ORDER[r] == "YT" and pair_live(p - 1):
                        wait(act, "yT_mm", p)
                        nc.scalar.activation(yT[:, :], misc_bank[:, 0:256], ACT.Copy).then_inc(s["misc_free"], 1)

            over_pairs(act, steps)

            def expert_steps(q, u):
                if block_live(q, 0):
                    wait(act, "t_mm", q + 1)
                    wait(act, "gu_mm", q - 1)
                    nc.scalar.activation(bT[:, u % 2].rearrange("p a b c -> p (a b c)"), t_bank[:, 0:512],
                                         ACT.Copy).then_inc(s["t_ok"], 1)
                if block_live(q, 1):
                    wait(act, "gate_ok", q)
                    nc.scalar.activation(sig[:, :, :], gate[:, :, :], ACT.Sigmoid, scale=ALPHA).then_inc(s["sig_ok"], 1)
                if block_live(q, 2):
                    wait(act, "ht_mm", q - 1)
                    wait(act, "d_mm", q - 3)
                    nc.scalar.activation(hT[:, u % 2, HI, :], ht_bank[:, 0:256], ACT.Copy).then_inc(s["ht_hi"], 1)
                if block_live(q, 3):
                    wait(act, "d_mm", q - 2)
                    if not isinstance(q, int) or q - 3 >= 4:
                        act.wait_ge(z_sent[(u + 1) % 4], sent_count(q, u, -3))
                    for t in range(2):
                        nc.scalar.activation(z[:, (u + 1) % 4, t, :], d_bank[:, t * P:(t + 1) * P], ACT.Copy,
                                             scale=rows_in[:, (u + NBUF - 3) % NBUF, t, P:P + 1]).then_inc(s["z_ok"], 1)

            over_blocks(act, expert_steps)
            for g in range(NB // 4):
                act.wait_ge(s["fin_ok"], g + 1)
                act.dma_start(out[4 * g:4 * g + 4].rearrange("b t d -> t b d"), x_sb[:, 4 * g:4 * g + 4, :]).then_inc(s["fin_sent"], 16)
            act.wait_ge(s["fin_sent"], 16 * (NB // 4))

        @block.gpsimd
        def _(pool):
            nc.gpsimd.memset(ident[:, :], 0.0).then_inc(s["zeroed"], 1)
            nc.gpsimd.memset(ident16[:, :], 0.0).then_inc(s["zeroed"], 1)
            nc.gpsimd.memset(ones16[:, :], 1.0).then_inc(s["zeroed"], 1)
            nc.gpsimd.memset(minus_half[:, :], -0.5).then_inc(s["zeroed"], 1)
            nc.gpsimd.memset(zeros[:, :], 0.0).then_inc(s["zeroed"], 1)
            pool.wait_ge(s["zeroed"], 5)
            for t in (ident, ident16):
                nc.gpsimd.affine_select(out=t[:, :], in_=t[:, :], compare_op=ALU.not_equal, fill=1.0, base=0,
                                        pattern=[[-1, P]], channel_multiplier=1).then_inc(s["consts"], 1)
            nc.gpsimd.affine_select(out=before16[:, :], in_=ones16[:, :], compare_op=ALU.is_gt, fill=0.0, base=0,
                                    pattern=[[1, P]], channel_multiplier=-1).then_inc(s["consts"], 1)
            nc.gpsimd.memset(v[:, :, HI, :, :, DH:VW], 1.0).then_inc(s["ones_v"], 1)
            nc.gpsimd.memset(v[:, :, LO, :, :, DH:VW], 0.0).then_inc(s["ones_v"], 1)

            def inverse_root(ready, count, mean_var, ve, rs, done, adds):
                wait_alone(pool, ready, count)
                nc.gpsimd.tensor_scalar(ve[:, :], mean_var[:, :, 1], EPS, None, ALU.add).then_inc(s["pool_add"], 1)
                wait(pool, "pool_add", adds)
                nc.gpsimd.tensor_tensor(rs[:, :], ve[:, :], minus_half[:, :], ALU.pow).then_inc(s[done], 1)

            def add_b_out(q):
                wait(pool, "xhat_ok", q * 3 + 3)
                for j in range(2):
                    nc.gpsimd.tensor_tensor(x_sb[:, q * 2 + j, :], x_sb[:, q * 2 + j, :], bout_bc[:, :],
                                            ALU.add).then_inc(s["x_bias"], 1)

            pool.wait_ge(s["absmax"], 3)
            nc.gpsimd.partition_all_reduce(top[:, 0:3], largest[:, 0:3], P, bass.bass_isa.ReduceOp.max).then_inc(s["allmax"], 1)
            inverse_root("stat_agg", 2, mv, var_eps, rstd, "rstd_ok", 1)
            inverse_root("stat_agg", 4, mv, var_eps, rstd, "rstd_ok", 2)
            nc.gpsimd.iota(expert_no[:, :], pattern=[[1, NE]], base=0, channel_multiplier=0,
                           allow_small_or_imprecise_dtypes=True).then_inc(s["consts"], 1)
            nc.gpsimd.iota(next_place[:, 0, :], pattern=[[ROOM, NE]], base=0, channel_multiplier=0,
                           allow_small_or_imprecise_dtypes=True).then_inc(s["consts"], 1)
            nc.gpsimd.iota(row_no[:, :, :], pattern=[[P, NB], [TOK, 2]], base=0, channel_multiplier=1).then_inc(s["consts"], 1)
            nc.gpsimd.iota(part_no[:, :], pattern=[[0, 1]], base=0, channel_multiplier=1,
                           allow_small_or_imprecise_dtypes=True).then_inc(s["consts"], 1)
            nc.gpsimd.memset(blank[:, 0:P + 1], 0.0).then_inc(s["blank_ok"], 1)
            nc.gpsimd.memset(blank[:, P + 1:ROW].bitcast(I32), NOWHERE).then_inc(s["blank_ok"], 1)

            def split_qk(q, par, t):
                which, blk = (t % 4) // 2, 4 * (t // 4) + 2 * (t % 2)
                src = qkf[:, t % 2, :].rearrange("p (i n) -> p i n", i=2)
                wait_alone(pool, "qk_copied", q * 8 + t + 1)
                if t == 0:
                    wait_alone(pool, "score_mm", q * 8 - 8)
                nc.gpsimd.tensor_tensor(qk[:, par, which, HI, blk:blk + 2, :], src, zeros[:, :].rearrange("p (i n) -> p i n", i=2),
                                        ALU.add).then_inc(s["qk_high"], 1)
                wait(pool, "qk_high", q * 8 + t + 1)
                nc.gpsimd.tensor_tensor(qk[:, par, which, LO, blk:blk + 2, :], src, qk[:, par, which, HI, blk:blk + 2, :],
                                        ALU.subtract).then_inc(s["qk_split"], 1)

            for t in range(8):
                split_qk(0, 0, t)
            pool.wait_ge(s["in_small"], 16 * 5)
            add_b_out(0)
            add_b_out(1)
            for k, (a, b) in enumerate(((3, 5), (5, 7))):
                pool.wait_ge(s["absmax"], b)
                nc.gpsimd.partition_all_reduce(top[:, a:b], largest[:, a:b], P, bass.bass_isa.ReduceOp.max).then_inc(s["allmax"], 1)

            def adds_before(p):
                if isinstance(p, int):
                    return 2 + sum((pp + 2 < PAIRS) + (0 <= pp - 1 < PAIRS) for pp in range(p))
                return p * 2 + (adds_before(2) - 4)

            def steps(p, par):
                adds = adds_before(p)
                for r in range(STEPS):
                    if pair_live(p + 1):
                        split_qk(p + 1, 1 - par, r)
                    if r == 0 and pair_live(p + 2):
                        adds = adds + 1
                        inverse_root("stat_agg", p * 2 + 6, mv, var_eps, rstd, "rstd_ok", adds)
                    if r == 2 and pair_live(p + 2):
                        add_b_out(p + 2)
                    if r == 5 and pair_live(p - 1):
                        adds = adds + 1
                        inverse_root("stat2_agg", p * 2, mv2, var_eps2, rstd2, "rstd2_ok", adds)
                    if r == 5 and pair_live(p - 2):
                        wait(pool, "slots_ok", p - 1)
                        wait(pool, "wgt_ok", p * 3 - 3)
                        wait_alone(pool, "yhalf", p * 4 - 4)
                        for j in range(2):
                            for c in range(2):
                                nc.gpsimd.indirect_dma_start(
                                    out=places, out_offset=bass.IndirectOffsetOnAxis(ap=slots[:, par, 2 * j + c:2 * j + c + 1], axis=0),
                                    in_=payload[:, par, j, c, :], in_offset=None).then_inc(scattered[par], 16)

            over_pairs(pool, steps)

            def send(q, u):
                if block_live(q, 3):
                    for t in range(2):
                        wait_alone(pool, "z_ok", q * 2 - 5 + t)
                        to = rows_in[:, (u + NBUF - 3) % NBUF, t, P + 1:ROW].bitcast(U32)
                        nc.gpsimd.indirect_dma_start(
                            out=results, out_offset=bass.IndirectOffsetOnAxis(ap=to, axis=0),
                            in_=z[:, (u + 1) % 4, t, :], in_offset=None,
                            bounds_check=2 * TOK - 1, oob_is_err=False).then_inc(z_sent[(u + 1) % 4], 16)

            over_blocks(pool, send)

        @block.vector
        def _(dve):
            count = [0]

            def link(ins):
                count[0] += 1
                ins.then_inc(s["setup"], 1)
                dve.wait_ge(s["setup"], count[0])

            def magnitude(col, ap):
                nc.vector.tensor_reduce(largest[:, col:col + 1], ap, AX.X, ALU.max,
                                        apply_absolute_value=True).then_inc(s["absmax"], 1)

            def make_scales(a, b, name):
                link(nc.vector.tensor_scalar(top[:, a:b], top[:, a:b], TINY, 1.0 / TOP, ALU.max, ALU.mult))
                link(nc.vector.tensor_copy(scale_from[:, a:b], top[:, a:b]))
                nc.vector.reciprocal(scale_to[:, a:b], scale_from[:, a:b]).then_inc(s[name], 1)

            def prep_stats(q):
                wait_alone(dve, "xhat_ok", q * 3)
                for j in range(2):
                    nc.vector.bn_stats(stats[:, j, :], x_sb[:, q * 2 + j, :]).then_inc(s["stat"], 1)
                for j in range(2):
                    wait_alone(dve, "stat", q * 2 + j + 1)
                    nc.vector.bn_aggr(mv[:, j, :], stats[:, j, :]).then_inc(s["stat_agg"], 1)

            def prep_rows(q):
                wait(dve, "rstd_ok", q + 1)
                wait(dve, "prep_mm", q)
                for j in range(2):
                    nc.vector.tensor_scalar(xhat[:, 0, j, :], x_sb[:, q * 2 + j, :], mv[:, j, 0:1], rstd[:, j:j + 1],
                                            ALU.subtract, ALU.mult).then_inc(s["xhat_ok"], 1)
                nc.vector.tensor_scalar(xhat[:, 1, :, :], ctx_sb[:, bass.ds(q * 2, 2), :], scale_to[:, 1:2], None,
                                        ALU.mult).then_inc(s["xhat_ok"], 1)

            def prep_low(q, par):
                wait(dve, "prep_hi", q + 1)
                nc.vector.tensor_tensor(xT[:, par, LO, :], misc_bank[:, :], xT[:, par, HI, :], ALU.subtract).then_inc(s["misc_free"], 1)

            def v_low(q, par, k):
                wait(dve, "v_hi", q * 4 + k + 1)
                heads = slice(8 * (k % 2), 8 * (k % 2) + 8)
                nc.vector.tensor_tensor(v[:, par, LO, k // 2, heads, 0:DH], misc_bank[:, :].rearrange("p (h d) -> p h d", h=8),
                                        v[:, par, HI, k // 2, heads, 0:DH], ALU.subtract).then_inc(s["misc_free"], 1)

            dve.wait_ge(s["in_w"], 16)
            magnitude(0, stage[:, 0:3 * INNER])
            dve.wait_ge(s["in_ctx"], 16)
            magnitude(1, ctx_sb[:, :, :].rearrange("p b d -> p (b d)"))
            dve.wait_ge(s["in_wo"], 16 * 8)
            magnitude(2, stage[:, 3 * INNER:4096])
            dve.wait_ge(s["in_x"], 32)
            prep_stats(0)
            dve.wait_ge(s["allmax"], 1)
            make_scales(0, 3, "scales")
            link(nc.vector.tensor_tensor(fac[:, 1:2], scale_from[:, 0:1], scale_from[:, 1:2], ALU.mult))
            link(nc.vector.tensor_tensor(fac[:, 4:5], fac[:, 1:2], scale_from[:, 0:1], ALU.mult))
            link(nc.vector.tensor_scalar(fac[:, 0:1], fac[:, 4:5], DH ** -0.5, None, ALU.mult))
            link(nc.vector.tensor_scalar(fac[:, 2:3], fac[:, 4:5], -DH ** -0.5, None, ALU.mult))
            link(nc.vector.tensor_tensor(fac[:, 3:4], fac[:, 1:2], scale_from[:, 2:3], ALU.mult))
            dve.wait_ge(s["scales"], 1)
            prep_rows(0)
            prep_stats(1)
            dve.wait_ge(s["w_hi"], 1)
            nc.vector.scalar_tensor_tensor(out=w_qkv[:, LO, :], in0=stage[:, 0:3 * INNER], scalar=scale_to[:, 0:1],
                                           in1=w_qkv[:, HI, :], op0=ALU.mult, op1=ALU.subtract).then_inc(s["w_lo"], 1)
            prep_low(0, 0)
            prep_rows(1)
            prep_low(1, 1)
            dve.wait_ge(s["wo_hi"], 1)
            nc.vector.scalar_tensor_tensor(out=w_out[:, LO].rearrange("p b n -> p (b n)"), in0=stage[:, 3 * INNER:4096],
                                           scalar=scale_to[:, 2:3], in1=w_out[:, HI].rearrange("p b n -> p (b n)"), op0=ALU.mult, op1=ALU.subtract).then_inc(s["wo_lo"], 1)
            for k in range(4):
                v_low(0, 0, k)


            def with_bias(a, b):
                dve.wait_ge(s["allmax"], 2 if a == 3 else 3)
                link(nc.vector.tensor_tensor(top[:, a:a + 1], top[:, a:a + 1], top[:, b:b + 1], ALU.max))
                make_scales(a, a + 1, "scales2")
                dve.wait_ge(s["scales2"], 1 if a == 3 else 2)

            def split(hi, lo, src, scale):
                link(nc.vector.tensor_scalar(hi, src, scale, None, ALU.mult))
                nc.vector.scalar_tensor_tensor(out=lo, in0=src, scalar=scale, in1=hi,
                                               op0=ALU.mult, op1=ALU.subtract).then_inc(s["bias_half"], 1)

            dve.wait_ge(s["in_small"], 16 * 5)
            b_up = bgu_sb[:, :].rearrange("p (f c) -> p f c", c=2)[:, :, 1]
            link(nc.vector.tensor_scalar(b_up, b_up, 1.0, None, ALU.add))
            dve.wait_ge(s["wgT_mm"], 1)
            nc.vector.tensor_copy(wg_T[:, :], out_bank[:, 0:NE]).then_inc(s["wgT_ok"], 1)
            dve.wait_ge(s["in_wd"], 16)
            magnitude(3, stage[:, 0:NE * D])
            magnitude(4, bd_sb[:, :])
            with_bias(3, 4)
            dve.wait_ge(s["d_hi"], 1)
            nc.vector.scalar_tensor_tensor(out=w_d[:, LO].rearrange("p e n -> p (e n)"), in0=stage[:, 0:NE * D],
                                           scalar=scale_to[:, 3:4], in1=w_d[:, HI].rearrange("p e n -> p (e n)"),
                                           op0=ALU.mult, op1=ALU.subtract).then_inc(s["d_lo"], 1)
            split(bd_half[:, HI, :], bd_half[:, LO, :], bd_sb[:, :], scale_to[:, 3:4])
            dve.wait_ge(s["in_wgu"], 16)
            magnitude(5, stage[:, :])
            magnitude(6, bgu_sb[:, :])
            with_bias(5, 6)
            for c in range(2):
                dve.wait_ge(s["gu_hi"], c + 1)
                for g in range(4):
                    e4 = slice(4 * g, 4 * g + 4)
                    nc.vector.scalar_tensor_tensor(
                        out=w_gu[:, LO, e4, c * P:(c + 1) * P],
                        in0=stage[:, :].rearrange("p (e f c) -> p c e f", e=NE, c=2)[:, c, e4], scalar=scale_to[:, 5:6],
                        in1=w_gu[:, HI, e4, c * P:(c + 1) * P], op0=ALU.mult, op1=ALU.subtract).then_inc(s["gu_lo"], 1)
            for c in range(2):
                split(bgu_half[:, HI, c, :], bgu_half[:, LO, c, :],
                      bgu_sb[:, :].rearrange("p (f c) -> p c f", c=2)[:, c], scale_to[:, 5:6])

            def steps(p, par):
                for r in range(STEPS):
                    n = p * STEPS + r
                    if live(p, r, 0):
                        wait(dve, "score_mm", n + 1)
                        nc.vector.tensor_reduce(qmax[:, r % 2, :], score_bank[r % 2][:, :].rearrange("p (h k) -> p h k", h=4),
                                                AX.X, ALU.max).then_inc(s["qmax_ok"], 1)
                    if live(p, r, 5):
                        wait(dve, "ot_hi", n - 4)
                        nc.vector.tensor_tensor(oT[:, (r + 1) % 2, LO, :], ot_bank[:, 0:256], oT[:, (r + 1) % 2, HI, :],
                                                ALU.subtract).then_inc(s["ot_lo"], 1)
                    if live(p, r, 0):
                        wait(dve, "qmax_ok", n + 1)
                        wait(dve, "exp_ok", n - 1)
                        nc.vector.tensor_scalar(nbias[:, r % 2, :], qmax[:, r % 2, :], fac[:, 2:3], None,
                                                ALU.mult).then_inc(s["nbias_ok"], 1)
                    if r in (1, 5) and pair_live(p - 1):
                        j = r // 4
                        wait(dve, "out_mm", p * 8 - 4 + 4 * j)
                        wait(dve, "x_bias", p * 2)
                        row = x_sb[:, p * 2 - 2 + j, :]
                        nc.vector.scalar_tensor_tensor(out=row, in0=out_bank[:, 0:P], scalar=fac[:, 3:4], in1=row,
                                                       op0=ALU.mult, op1=ALU.add).then_inc(s["x1_ok"], 1)
                    if r == 1 and pair_live(p - 2):
                        wait_alone(dve, "misc_free", misc_before(p, "V0"))
                        for j in range(2):
                            nc.vector.max(best[:, j, :], logits[:, j, :]).then_inc(s["best_ok"], 1)
                    if r == 2 and pair_live(p - 2):
                        wait(dve, "best_at_ok", p * 2 - 2)
                        nc.vector.tensor_copy(choice[:, :].rearrange("p (j k) -> p j k", j=2), best_at[:, :, 0:2]).then_inc(s["choice_ok"], 1)
                        nc.vector.tensor_tensor(gap[:, :], best[:, :, 1], best[:, :, 0], ALU.subtract).then_inc(s["gap_ok"], 1)
                    if r == 4 and pair_live(p - 2):
                        wait(dve, "rank_mm", p - 1)
                        now = next_place[:, par, :]
                        nc.vector.tensor_tensor(place_all[:, :, :], misc_bank[:, 0:2 * NE].rearrange("p (j e) -> p j e", j=2),
                                                now.unsqueeze(1).to_broadcast([P, 2, NE]), ALU.add).then_inc(s["place_ok"], 1)
                        nc.vector.tensor_tensor(next_place[:, 1 - par, :], misc_bank[:, 2 * NE:3 * NE], now, ALU.add).then_inc(s["misc_free"], 1)
                    if r == 5 and pair_live(p - 1):
                        for j in range(2):
                            wait_alone(dve, "x1_ok", p * 2 - 1 + j)
                            nc.vector.bn_stats(stats2[:, j, :], x_sb[:, p * 2 - 2 + j, :]).then_inc(s["stat2"], 1)
                    if live(p, r, 2):
                        wait(dve, "pt_hi", n - 1)
                        nc.vector.tensor_tensor(pT[:, r % 2, LO, :], pt_bank[:, :], pT[:, r % 2, HI, :],
                                                ALU.subtract).then_inc(s["pt_lo"], 1)
                    if live(p, r, 3):
                        wait(dve, "pv_mm", n - 2)
                        nc.vector.reciprocal(rsum[:, :], o_bank[:, 0:4 * (DH + 1)].rearrange("p (h w) -> p h w", h=4)[:, :, DH]).then_inc(s["rsum_ok"], 1)
                    if ORDER[r][0] == "V" and pair_live(p + 1):
                        v_low(p + 1, 1 - par, int(ORDER[r][1]))
                    if r == 0 and pair_live(p + 2):
                        prep_stats(p + 2)
                    if r == 1 and pair_live(p - 2):
                        for j in range(2):
                            wait_alone(dve, "best_ok", p * 2 - 3 + j)
                            nc.vector.max_index(best_at[:, j, :], best[:, j, :], logits[:, j, :]).then_inc(s["best_at_ok"], 1)
                    if r == 2 and pair_live(p - 2):
                        wait(dve, "choice_ok", p - 1)
                        nc.vector.tensor_tensor(onehot[:, :, :], expert_no[:, :].unsqueeze(1).to_broadcast([P, 4, NE]),
                                                choice[:, :].unsqueeze(2).to_broadcast([P, 4, NE]), ALU.is_equal).then_inc(s["onehot_ok"], 1)
                    if r == 4 and pair_live(p - 2):
                        wait(dve, "place_ok", p - 1)
                        for j in range(2):
                            nc.vector.tensor_tensor(picked[:, 2 * j:2 * j + 2, :], onehot[:, 2 * j:2 * j + 2, :],
                                                    place_all[:, j, :].unsqueeze(1).to_broadcast([P, 2, NE]), ALU.mult).then_inc(s["picked_ok"], 1)
                        wait(dve, "egap_ok", p - 1)
                        nc.vector.tensor_scalar(denom[:, :], egap[:, :], 1.0, None, ALU.add).then_inc(s["denom_ok"], 1)
                    if r == 5 and pair_live(p - 1):
                        for j in range(2):
                            wait_alone(dve, "stat2", p * 2 - 1 + j)
                            nc.vector.bn_aggr(mv2[:, j, :], stats2[:, j, :]).then_inc(s["stat2_agg"], 1)
                    if r == 6 and pair_live(p - 1):
                        wait(dve, "rstd2_ok", p)
                        wait(dve, "yT_mm", p - 1)
                        for j in range(2):
                            nc.vector.tensor_scalar(y[:, j, :], x_sb[:, p * 2 - 2 + j, :], mv2[:, j, 0:1], rstd2[:, j:j + 1],
                                                    ALU.subtract, ALU.mult).then_inc(s["y_ok"], 1)
                    if live(p, r, 3):
                        wait(dve, "rsum_ok", n - 2)
                        wait(dve, "ot_mm", n - 4)
                        nc.vector.tensor_tensor(o_nat[:, (r + 1) % 2, :].rearrange("p (h d) -> p h d", h=4),
                                                o_bank[:, 0:4 * (DH + 1)].rearrange("p (h w) -> p h w", h=4)[:, :, 0:DH],
                                                rsum[:, :].unsqueeze(2).to_broadcast([P, 4, DH]), ALU.mult).then_inc(s["o_ok"], 1)
                    if r == 2 and pair_live(p - 2):
                        wait(dve, "onehot_ok", p - 1)
                        both = onehot[:, :, :].rearrange("p (j k) e -> p j k e", j=2)
                        nc.vector.tensor_tensor(chosen16[:, :, :], both[:, :, 0, :], both[:, :, 1, :], ALU.add).then_inc(s["chosen_ok"], 1)
                    if r == 4 and pair_live(p - 2):
                        wait(dve, "picked_ok", p * 2 - 2)
                        with nc.allow_low_precision(reason="one whole number and zeros, exact"):
                            nc.vector.tensor_reduce(slots[:, par, :], picked[:, :, :], AX.X, ALU.add).then_inc(s["slots_ok"], 1)
                        wait(dve, "denom_ok", p - 1)
                        nc.vector.reciprocal(payload[:, par, :, 0, P], denom[:, :]).then_inc(s["wgt_ok"], 1)
                        nc.vector.tensor_copy(payload[:, par, :, :, P + 1].bitcast(I32), row_no[:, bass.ds(p * 2 - 4, 2), :]).then_inc(s["wgt_ok"], 1)
                        wait(dve, "wgt_ok", p * 3 - 4)
                        nc.vector.tensor_tensor(payload[:, par, :, 1, P], payload[:, par, :, 0, P], egap[:, :], ALU.mult).then_inc(s["wgt_ok"], 1)
                    if r == 6 and pair_live(p - 1):
                        if not isinstance(p, int) or p > 2:
                            dve.wait_ge(scattered[1 - par], (p - 2 + par) * 32)
                        for j in range(2):
                            wait(dve, "y_ok", p * 2 - 1 + j)
                            nc.vector.tensor_copy(halves[:, 1 - par, j, :, 0:P], y[:, j, :].unsqueeze(1).to_broadcast([P, 2, P])).then_inc(s["yhalf"], 1)
                    if r == 6 and pair_live(p - 1):
                        for j in range(2):
                            wait(dve, "yhalf", p * 4 - 3 + j)
                            nc.vector.tensor_tensor(halves[:, 1 - par, j, :, P:2 * P], y[:, j, :].unsqueeze(1).to_broadcast([P, 2, P]),
                                                    halves[:, 1 - par, j, :, 0:P], ALU.subtract).then_inc(s["yhalf"], 1)
                    if r == 2 and pair_live(p + 2):
                        prep_rows(p + 2)
                    if ORDER[r] == "PREP" and pair_live(p + 2):
                        prep_low(p + 2, par)
                    if ORDER[r] == "LG" and pair_live(p - 2):
                        wait(dve, "lg_mm", p - 1)
                        nc.vector.tensor_tensor(logits[:, :, :], misc_bank[:, 0:2 * NE].rearrange("p (j e) -> p j e", j=2),
                                                bg_bc[:, :].unsqueeze(1).to_broadcast([P, 2, NE]), ALU.add).then_inc(s["misc_free"], 1)

            over_pairs(dve, steps)

            final = next_place[:, PAIRS % 2, :]
            dve.wait_ge(s["misc_free"], misc_before(PAIRS + 2, "V0"))
            counts, blocks, upto, passed, mine, first = (blocks_f[:, k, :] for k in range(6))
            nc.vector.tensor_copy(ends[:, :], final[0:1, :]).then_inc(s["ends_ok"], 1)
            link(nc.vector.scalar_tensor_tensor(out=counts, in0=expert_no[:, :], scalar=-float(ROOM), in1=final, op0=ALU.mult, op1=ALU.add))
            link(nc.vector.tensor_scalar(blocks_i[:, :], counts, float(P - 1), None, ALU.add))
            link(nc.vector.tensor_scalar(blocks_i[:, :], blocks_i[:, :], 7, None, ALU.logical_shift_right))
            link(nc.vector.tensor_copy(blocks, blocks_i[:, :]))
            link(nc.vector.memset(first, 1.0))
            link(nc.vector.tensor_tensor_scan(upto, first, blocks, 0.0, ALU.mult, ALU.add))
            link(nc.vector.tensor_scalar(passed, upto, part_no[:, 0:1], None, ALU.is_le))
            link(nc.vector.tensor_tensor(mine, passed, blocks, ALU.mult))
            link(nc.vector.tensor_reduce(table_f[:, 0:1], passed, AX.X, ALU.add))
            link(nc.vector.tensor_reduce(table_f[:, 2:3], mine, AX.X, ALU.add))
            link(nc.vector.tensor_tensor(table_f[:, 3:4], part_no[:, :], table_f[:, 2:3], ALU.subtract))
            link(nc.vector.tensor_scalar(table_f[:, 3:4], table_f[:, 3:4], float(P), None, ALU.mult))
            link(nc.vector.scalar_tensor_tensor(out=table_f[:, 1:2], in0=table_f[:, 0:1], scalar=float(ROOM), in1=table_f[:, 3:4],
                                                op0=ALU.mult, op1=ALU.add))
            link(nc.vector.tensor_scalar(table_f[:, 1:2], table_f[:, 1:2], float(NE * ROOM), None, ALU.min))
            nc.vector.tensor_scalar(table_f[:, 0:1], table_f[:, 0:1], float(NE - 1), None, ALU.min).then_inc(s["table_cols"], 1)
            dve.wait_ge(s["table_mm"], 1)
            nc.vector.tensor_copy(table[:, :, :], table_bank[0:1, 0:2 * P].rearrange("p (c b) -> p c b", c=2)).then_inc(s["table_ok"], 1)

            def expert_steps(q, u):
                if block_live(q, 1):
                    wait(dve, "gu_mm", q)
                    bank = gu_bank[(u + 1) % 2][:, :].rearrange("p (t c f) -> p t c f", t=2, c=2)
                    nc.vector.tensor_scalar(gate[:, :, :], bank[:, :, 0, :], scale_from[:, 5:6], LIMIT, ALU.mult, ALU.min).then_inc(s["gate_ok"], 1)
                    wait(dve, "h_ok", q - 1)
                    nc.vector.tensor_scalar(up[:, :, :], bank[:, :, 1, :], scale_from[:, 5:6], 1.0 + LIMIT, ALU.mult, ALU.min).then_inc(s["up_ok"], 1)
                if block_live(q, 2):
                    wait(dve, "ht_hi", q - 1)
                    nc.vector.tensor_tensor(hT[:, u % 2, LO, :], ht_bank[:, 0:256], hT[:, u % 2, HI, :], ALU.subtract).then_inc(s["ht_lo"], 1)
                if block_live(q, 1):
                    wait(dve, "sig_ok", q)
                    nc.vector.tensor_tensor(glu[:, :, :], gate[:, :, :], sig[:, :, :], ALU.mult).then_inc(s["glu_ok"], 1)
                    wait(dve, "glu_ok", q)
                    wait(dve, "ht_mm", q - 2)
                    nc.vector.scalar_tensor_tensor(out=hidden[:, (u + 1) % 2], in0=up[:, :, :], scalar=1.0 - LIMIT,
                                                   in1=glu[:, :, :], op0=ALU.max, op1=ALU.mult).then_inc(s["h_ok"], 1)

            over_blocks(dve, expert_steps)

            for g in range(NB // 4):
                dve.wait_ge(results_in[g % 4], 32 * (g // 4 + 1))
                nc.vector.tensor_tensor(r_in[:, g % 4, 0], r_in[:, g % 4, 0], r_in[:, g % 4, 1], ALU.add).then_inc(s["sum_ok"], 1)
                dve.wait_ge(s["sum_ok"], g + 1)
                rows = x_sb[:, 4 * g:4 * g + 4, :]
                nc.vector.scalar_tensor_tensor(out=rows, in0=r_in[:, g % 4, 0], scalar=scale_from[:, 3:4], in1=rows,
                                               op0=ALU.mult, op1=ALU.add).then_inc(s["fin_ok"], 1)

        @block.tensor
        def _(pe):
            def three(dst, a_hi, a_lo, b_hi, b_lo, start=True, stop=True):
                nc.tensor.matmul(dst, a_hi, b_hi, start=start, stop=False)
                nc.tensor.matmul(dst, a_hi, b_lo, start=False, stop=False)
                return nc.tensor.matmul(dst, a_lo, b_hi, start=False, stop=stop)

            def prep(q):
                wait(pe, "xhat_ok", q * 3 + 3)
                for w in range(2):
                    for j in range(2):
                        last = nc.tensor.transpose(misc_bank[:, (2 * w + j) * P:(2 * w + j + 1) * P], xhat[:, w, j, :], ident[:, :])
                last.then_inc(s["prep_mm"], 1)

            def project_qk(q, par, t):
                which, blk = (t % 4) // 2, 4 * (t // 4) + 2 * (t % 2)
                src = slice(which * 256, which * 256 + 256)
                wait(pe, "qk_copied", q * 8 + t)
                for i in range(2):
                    col = which * INNER + (blk + i) * P
                    last = three(qk_bank[:, i * 256:i * 256 + 256], w_qkv[:, HI, col:col + P], w_qkv[:, LO, col:col + P],
                                 xT[:, par, HI, src], xT[:, par, LO, src])
                last.then_inc(s["qk_mm"], 1)

            def project_v(par, k):
                tok = slice(256 + (k // 2) * P, 256 + (k // 2) * P + P)
                cols = slice(2 * INNER + (k % 2) * 512, 2 * INNER + (k % 2) * 512 + 512)
                three(misc_bank[:, :], xT[:, par, HI, tok], xT[:, par, LO, tok], w_qkv[:, HI, cols], w_qkv[:, LO, cols]
                      ).then_inc(s["v_mm"], 1)

            pe.wait_ge(s["consts"], 7)
            pe.wait_ge(s["in_small"], 16 * 5)
            nc.tensor.transpose(out_bank[:, 0:NE], wg_nat[:, :], ident[0:NE, 0:NE]).then_inc(s["wgT_mm"], 1)
            prep(0)
            wait(pe, "misc_free", 1)
            prep(1)
            pe.wait_ge(s["w_lo"], 1)
            for t in range(8):
                project_qk(0, 0, t)
                if t < 4:
                    wait(pe, "misc_free", 2 + t)
                    project_v(0, t)
            pe.wait_ge(s["wgT_ok"], 1)
            pe.wait_ge(s["wo_lo"], 1)
            pe.wait_ge(s["ones_v"], 2)

            def scores(par, r, n):
                j, half, odd = r // 4, (r // 2) % 2, r % 2
                rows, tok = slice(64 * odd, 64 * odd + 64), slice(j * P, j * P + P)
                wait(pe, "exp_ok", n - 1)
                for k in range(4):
                    a = [qk[rows, par, 0, h, 4 * half + k, tok] for h in range(2)]
                    b = [qk[rows, par, 1, h, 4 * half + k, tok] for h in range(2)]
                    last = three(score_bank[r % 2][:, k * P:(k + 1) * P], a[HI], a[LO], b[HI], b[LO])
                last.then_inc(s["score_mm"], 1)

            def steps(p, par):
                for r in range(STEPS):
                    n = p * STEPS + r
                    if live(p, r, 0):
                        if r in (0, 2):
                            wait(pe, "qk_split", p * 8 + 4 + 2 * r)
                        scores(par, r, n)
                    if pair_live(p + 1):
                        project_qk(p + 1, 1 - par, r)
                    if live(p, r, 2):
                        wait(pe, "exp_ok", n - 1)
                        wait(pe, "pt_lo", n - 2)
                        for k in range(4):
                            last = nc.tensor.transpose(pt_bank[:, k * P:(k + 1) * P], probs[:, r % 2, k, :], ident[:, :])
                        last.then_inc(s["pt_mm"], 1)
                    item = ORDER[r]
                    if pair_live(p + USES[item]):
                        wait(pe, "misc_free", misc_before(p, item))
                        if item[0] == "V":
                            project_v(1 - par, int(item[1]))
                        elif item == "PREP":
                            prep(p + 2)
                        elif item == "RANK":
                            wait(pe, "chosen_ok", p - 1)
                            c0, c1 = chosen16[:, 0, :], chosen16[:, 1, :]
                            nc.tensor.matmul(misc_bank[:, 0:NE], before16[:, :], c0, start=True, stop=True)
                            for at, first in ((NE, before16), (2 * NE, ones16)):
                                nc.tensor.matmul(misc_bank[:, at:at + NE], first[:, :], c1, start=True, stop=False)
                                last = nc.tensor.matmul(misc_bank[:, at:at + NE], ones16[:, :], c0, start=False, stop=True)
                            last.then_inc(s["rank_mm"], 1)
                        elif item == "YT":
                            wait(pe, "y_ok", p * 2)
                            for j in range(2):
                                last = nc.tensor.transpose(misc_bank[:, j * P:(j + 1) * P], y[:, j, :], ident[:, :])
                            last.then_inc(s["yT_mm"], 1)
                        else:
                            for j in range(2):
                                last = nc.tensor.matmul(misc_bank[:, j * NE:(j + 1) * NE], yT[:, j * P:(j + 1) * P], wg_T[:, :],
                                                        start=True, stop=True)
                            last.then_inc(s["lg_mm"], 1)
                    if live(p, r, 3):
                        vp = par if r >= 3 else 1 - par
                        rr = (r - 3) % STEPS
                        j, half, odd = rr // 4, (rr // 2) % 2, rr % 2
                        wait(pe, "pt_lo", n - 2)
                        wait(pe, "o_ok", n - 3)
                        if r == 3 and isinstance(p, int) and p < 2:
                            wait(pe, "misc_free", 6 if p == 0 else misc_before(0, "V3") + 1)
                        for k in range(4):
                            head, tok = 8 * half + 2 * k + odd, slice(k * P, k * P + P)
                            last = three(o_bank[:, k * (DH + 1):(k + 1) * (DH + 1)], pT[:, (r + 1) % 2, HI, tok], pT[:, (r + 1) % 2, LO, tok],
                                         v[:, vp, HI, j, head, 0:DH + 1], v[:, vp, LO, j, head, 0:DH + 1])
                        last.then_inc(s["pv_mm"], 1)
                    if live(p, r, 4):
                        wait(pe, "o_ok", n - 3)
                        wait(pe, "ot_lo", n - 4)
                        for k in range(2):
                            last = nc.tensor.transpose(ot_bank[:, k * P:(k + 1) * P], o_nat[:, r % 2, k * P:(k + 1) * P], ident[:, :])
                        last.then_inc(s["ot_mm"], 1)
                    if live(p, r, 5):
                        wait(pe, "ot_lo", n - 4)
                        if r % 4 == 1:
                            wait(pe, "x1_ok", p * 2 - 1 + r // 4)
                        for k in range(2):
                            blk = 2 * ((r - 5) % 4) + k
                            last = three(out_bank[:, 0:P], oT[:, (r + 1) % 2, HI, k * P:(k + 1) * P], oT[:, (r + 1) % 2, LO, k * P:(k + 1) * P],
                                         w_out[:, HI, blk, :], w_out[:, LO, blk, :], start=(blk == 0), stop=(blk == 7))
                        last.then_inc(s["out_mm"], 1)

            over_pairs(pe, steps)

            pe.wait_ge(s["table_cols"], 1)
            for c in range(2):
                last = nc.tensor.matmul(table_bank[0:1, c * P:(c + 1) * P], table_f[:, c:c + 1], ident[:, :], start=True, stop=True)
            last.then_inc(s["table_mm"], 1)
            pe.wait_ge(s["table_ok"], 1)
            pe.wait_ge(s["gu_lo"], 8)
            pe.wait_ge(s["bias_in"], 16 * 4)

            def plus_bias(dst, a_hi, a_lo, b_hi, b_lo, bias):
                nc.tensor.matmul(dst, ones16[0:2, :], bias, start=True, stop=False)
                return three(dst, a_hi, a_lo, b_hi, b_lo, start=False)

            def expert_of(q, t):
                return pe.value_load(table[0:1, 0, bass.ds(q * 2 + t, 1)], min_val=0, max_val=NE - 1)

            def expert_steps(q, u):
                if block_live(q, 0):
                    pe.wait_ge(block_in[u], (q // NBUF + 1) * 32 if isinstance(q, int) else (q - u) * (32 // NBUF) + 32)
                    wait_alone(pe, "t_ok", q)
                    for t in range(2):
                        for h in range(2):
                            at = (2 * t + h) * P
                            last = nc.tensor.transpose(t_bank[:, at:at + P], rows16[:, u, t, h * P:(h + 1) * P], ident16[:, :])
                    last.then_inc(s["t_mm"], 1)
                if block_live(q, 1):
                    wait_alone(pe, "t_ok", q)
                    wait_alone(pe, "up_ok", q - 2)
                    b = (u + 1) % 2
                    for t in range(2):
                        e = expert_of(q - 1, t)
                        last = plus_bias(gu_bank[b][:, t * 256:(t + 1) * 256], bT[:, b, t, HI, :], bT[:, b, t, LO, :],
                                         w_gu[:, HI, e, :], w_gu[:, LO, e, :], bias_gu[:, e, :])
                    last.then_inc(s["gu_mm"], 1)
                if block_live(q, 2):
                    wait(pe, "h_ok", q - 1)
                    wait(pe, "ht_lo", q - 2)
                    for t in range(2):
                        last = nc.tensor.transpose(ht_bank[:, t * P:(t + 1) * P], hidden[:, u % 2, t, :], ident[:, :])
                    last.then_inc(s["ht_mm"], 1)
                if block_live(q, 3):
                    wait(pe, "ht_lo", q - 2)
                    wait_alone(pe, "z_ok", q * 2 - 6)
                    b = (u + 1) % 2
                    for t in range(2):
                        e = expert_of(q - 3, t)
                        last = plus_bias(d_bank[:, t * P:(t + 1) * P], hT[:, b, HI, t * P:(t + 1) * P], hT[:, b, LO, t * P:(t + 1) * P],
                                         w_d[:, HI, e, :], w_d[:, LO, e, :], bias_d[:, e, :])
                    last.then_inc(s["d_mm"], 1)

            over_blocks(pe, expert_steps)


_INS = ["x", "ctx_1024", "L0_xattn_W_qkv", "L0_xattn_W_out", "L0_xattn_b_out", "L0_ffn_Wg", "L0_ffn_bg",
        "L0_ffn_Wgu", "L0_ffn_bgu", "L0_ffn_Wd", "L0_ffn_bd"]


def kernel(**inputs):
    import numpy as _np
    import concourse.bacc as _bacc
    from concourse import mybir as _mybir
    from concourse.bass_utils import run_bass_kernel_spmd as _run

    nc = _bacc.Bacc("TRN2", target_bir_lowering=False, num_devices=1)
    arrays, args = {}, []
    for name in _INS:
        a = _np.ascontiguousarray(inputs[name])
        arrays[f"in_{name}_dram"] = a
        args.append(nc.dram_tensor(f"in_{name}_dram", a.shape, _mybir.dt.from_np(a.dtype), kind="ExternalInput").ap())
    shape = inputs["x"].shape
    args.append(nc.dram_tensor("out_0_dram", shape, _mybir.dt.float32, kind="ExternalOutput").ap())
    xattn_moe_kernel(nc, *args)
    r = _run(nc, [arrays], core_ids=[0])
    return r.results[0]["out_0_dram"]
```

```python
from contextlib import ExitStack

import concourse.bass as bass
from concourse import mybir

F32 = mybir.dt.float32
F16 = mybir.dt.float16
I32 = mybir.dt.int32
U32 = mybir.dt.uint32
ALU = mybir.AluOpType
ACT = mybir.ActivationFunctionType
AX = mybir.AxisListType

P = 128
HI, LO = 0, 1
TOP = 16.0
TINY = 1e-30
EPS = 1e-5
ALPHA = 1.702
LIMIT = 7.0
NOWHERE = 1 << 20


def xattn_moe_kernel(nc, x, ctx, W_qkv, W_out, b_out, Wg, bg, Wgu, bgu, Wd, bd, out):
    NB, S, D = x.shape
    INNER = W_out.shape[0]
    NE = Wg.shape[0]
    DH = 64
    NH = INNER // DH
    PAIRS = NB // 2
    QUADS = NH // 4
    STEPS = 2 * QUADS
    ALLQ = PAIRS * STEPS
    TOK = NB * S
    ROOM = TOK + P
    ROW = P + 2
    BLOCKS = 2 * TOK // P + NE
    BPAIRS = BLOCKS // 2
    NBUF = 12
    NZ = 6
    VW = DH + 2
    assert S == P and D == P and NE == 16 and STEPS == 8 and BLOCKS == 80

    places = nc.dram_tensor("places", [NE * ROOM + P, ROW], F32, kind="Internal").ap()
    results = nc.dram_tensor("results", [2 * TOK, D], F32, kind="Internal").ap()

    bias_gu_rows = nc.dram_tensor("bias_gu_rows", [2, 2, NE * P], F16, kind="Internal").ap()
    bias_d_rows = nc.dram_tensor("bias_d_rows", [2, NE * P], F16, kind="Internal").ap()

    es = ExitStack()
    with es:
        def sb(name, shape, dt=F32):
            return es.enter_context(nc.sbuf_tensor(name, shape, dt))

        def sem(name):
            return es.enter_context(nc.semaphore(name))

        banks = [es.enter_context(nc.psum_tensor(f"bank{i}", [P, 512], F32)) for i in range(8)]
        score_bank = banks[0:2]
        pt_bank, o_bank, qk_bank, misc_bank, ot_bank, out_bank = banks[2:8]

        x_sb = sb("x_sb", [P, NB, D])
        ctx_sb = sb("ctx_sb", [P, NB, D])
        stage = sb("stage", [P, 4096])
        w_qkv = sb("w_qkv", [P, 2, 3 * INNER], F16)
        w_out = sb("w_out", [P, 2, 8, D], F16)
        w_gu = sb("w_gu", [P, 2, NE, 256], F16)
        w_d = sb("w_d", [P, 2, NE, D], F16)
        bias_gu = sb("bias_gu", [2, NE, 256], F16)
        bias_d = sb("bias_d", [2, NE, D], F16)
        bgu_sb = sb("bgu_sb", [P, 32])
        bd_sb = sb("bd_sb", [P, 16])
        bgu_half = sb("bgu_half", [P, 2, 2, 16], F16)
        bd_half = sb("bd_half", [P, 2, 16], F16)
        bout_bc = sb("bout_bc", [P, D])
        bg_bc = sb("bg_bc", [P, NE])
        wg_nat = sb("wg_nat", [NE, D])
        wg_T = sb("wg_T", [P, NE])
        part_largest = sb("part_largest", [P, 11])
        largest = sb("largest", [P, 8])
        top = sb("top", [P, 8])
        scale_to = sb("scale_to", [P, 8])
        scale_from = sb("scale_from", [P, 8])
        fac = sb("fac", [P, 8])
        ident = sb("ident", [P, P])
        ident16 = sb("ident16", [P, P], F16)
        ones16 = sb("ones16", [P, P], F16)
        before16 = sb("before16", [P, P], F16)
        expert_no = sb("expert_no", [P, NE])
        next_place = sb("next_place", [P, 2, NE])
        row_no = sb("row_no", [P, NB, 2], I32)
        minus_half = sb("minus_half", [P, 2])
        part_no = sb("part_no", [P, 1])
        blank = sb("blank", [P, ROW])
        xhat = sb("xhat", [P, 2, 2, D])
        xT = sb("xT", [P, 2, 2, 512], F16)
        stats = sb("stats", [P, 2, 6])
        mv = sb("mv", [P, 2, 2])
        var_eps = sb("var_eps", [P, 2])
        rstd = sb("rstd", [P, 2])
        zeros = sb("zeros", [P, 512])
        qkf = sb("qkf", [P, 2, 512])
        qk = sb("qk", [P, 2, 2, 2, 8, 256], F16)
        v = sb("v", [P, 2, 2, 2, NH, VW], F16)
        qmax = sb("qmax", [P, 2, 4])
        nbias = sb("nbias", [P, 2, 4])
        probs = sb("probs", [P, 2, 4, P])
        pT = sb("pT", [P, 2, 2, 512], F16)
        rsum = sb("rsum", [P, 4])
        o_nat = sb("o_nat", [P, 2, 256])
        oT = sb("oT", [P, 2, 2, 256], F16)
        stats2 = sb("stats2", [P, 2, 6])
        mv2 = sb("mv2", [P, 2, 2])
        var_eps2 = sb("var_eps2", [P, 2])
        rstd2 = sb("rstd2", [P, 2])
        y = sb("y", [P, 2, D])
        yT = sb("yT", [P, 256])
        logits = sb("logits", [P, 2, NE])
        best = sb("best", [P, 2, 8])
        best_at = sb("best_at", [P, 2, 8], U32)
        choice = sb("choice", [P, 4])
        gap = sb("gap", [P, 2])
        egap = sb("egap", [P, 2])
        onehot = sb("onehot", [P, 4, NE])
        chosen16 = sb("chosen16", [P, 2, NE], F16)
        place_all = sb("place_all", [P, 2, NE])
        picked = sb("picked", [P, 4, NE])
        slots = sb("slots", [P, 2, 4], U32)
        denom = sb("denom", [P, 2])
        payload = sb("payload", [P, 2, 2, 2, ROW])
        bT = sb("bT", [P, 2, 2, 2, P], F16)
        gate = sb("gate", [P, 2, 2, P])
        up = sb("up", [P, 2, 2, P])
        sig = sb("sig", [P, 2, 2, P])
        glu = sb("glu", [P, 2, P])
        hidden = sb("hidden", [P, 2, 2, P])
        hT = sb("hT", [P, 2, 2, 256], F16)
        z = sb("z", [P, NZ, 2, P])
        blocks_f = sb("blocks_f", [P, 6, NE])
        blocks_i = sb("blocks_i", [P, NE], I32)
        table_f = sb("table_f", [P, 4])
        expert_pairs = sb("expert_pairs", [1, P // 2])
        block_experts = sb("block_experts", [1, P // 4], I32)
        block_starts = sb("block_starts", [1, P // 2], I32)
        firsts = sb("firsts", [1, 2, P // 2])
        ends = sb("ends", [1, NE], I32)

        names = """carrier in_small in_wo in_wd in_wgu
        zeroed consts ones_v blank_ok blank_in part_max absmax allmax scales scales2
        w_hi w_lo wo_hi wo_lo d_hi d_lo gu_hi gu_lo bias_half bias_out bias_in wgT_mm wgT_ok setup
        stat stat_agg pool_add rstd_ok xhat_ok x_bias prep_mm prep_hi
        qk_mm qk_copied qk_high qk_split v_mm v_hi misc_free
        score_mm qmax_ok nbias_ok exp_ok pt_mm pt_hi pt_lo pv_mm rsum_ok o_ok ot_mm ot_hi ot_lo out_mm
        x1_ok stat2 stat2_agg rstd2_ok y_ok yhalf yT_mm lg_mm rank_mm
        best_ok best_at_ok gap_ok choice_ok onehot_ok chosen_ok egap_ok
        place_ok picked_ok slots_ok denom_ok wgt_ok
        table_cols table_mm first_ok table_ok ends_ok cleared
        t_mm t_ok gu_mm gate_ok up_ok sig_ok glu_ok h_ok ht_mm ht_hi ht_lo d_mm z_ok
        sum_ok fin_ok fin_sent""".split()
        s = {n: sem("s_" + n) for n in names}
        block_in = [sem(f"s_block_in{i}") for i in range(NBUF)]
        scattered = [sem(f"s_scattered{i}") for i in range(2)]
        z_sent = [sem(f"s_z_sent{i}") for i in range(NZ)]
        in_w = [sem(f"s_in_w{i}") for i in range(3)]
        in_ctx = [sem(f"s_in_ctx{i}") for i in range(4)]
        in_x = [sem(f"s_in_x{i}") for i in range(2)]
        results_in = [sem(f"s_results_in{i}") for i in range(4)]

        def wait(eng, name, value):
            if not isinstance(value, int) or value > 0:
                eng.wait_ge(s[name], value)

        def wait_alone(eng, name, value):
            wait(eng, name, value)
            if not isinstance(value, int):
                eng.sem_inc(s["carrier"], 1)

        def live(p, r, lag):
            return not isinstance(p, int) or 0 <= p * STEPS + r - lag < ALLQ

        def pair_live(q):
            return not isinstance(q, int) or 0 <= q < PAIRS

        USES = {"LG": -2, "V0": 1, "V1": 1, "RANK": -2, "PREP": 2, "V2": 1, "V3": 1, "YT": -1}
        ORDER = list(USES)

        def misc_before(p, item):
            if not isinstance(p, int):
                return p * len(ORDER) + (misc_before(2, item) - 2 * len(ORDER))
            before = [(pp, it) for pp in range(p) for it in ORDER]
            before += [(p, it) for it in ORDER[:ORDER.index(item)]]
            return 6 + sum(0 <= pp + USES[it] < PAIRS for pp, it in before)

        FIRST, LAST = 2, PAIRS - 2

        def over_pairs(eng, body):
            for p in range(FIRST):
                body(p, p % 2)
            with eng.Fori(0, (LAST - FIRST) // 2) as i:
                body(i * 2 + FIRST, 0)
                body(i * 2 + FIRST + 1, 1)
            for p in range(LAST, PAIRS + 2):
                body(p, p % 2)

        STAGES = 5

        def block_live(q, lag):
            return not isinstance(q, int) or 0 <= q - lag < BPAIRS

        def over_blocks(eng, body):
            for q in range(NBUF):
                body(q, q, 0)
            with eng.Fori(1, BPAIRS // NBUF) as i:
                for u in range(NBUF):
                    body(i * NBUF + u, u, i)
            for q in range(BPAIRS // NBUF * NBUF, BPAIRS + STAGES):
                body(q, q % NBUF, q // NBUF)

        def wait_sent(eng, q, u, i, lag):
            if not isinstance(q, int) or q >= lag:
                eng.wait_ge(z_sent[(u - lag) % NZ], i * (NBUF // NZ * 32) + 32 * ((u - lag) // NZ + 1))

        halves = payload[:, :, :, :, 0:P].bitcast(F16)
        rows_in = stage[:, 0:NBUF * 2 * ROW].rearrange("p (b t w) -> p b t w", b=NBUF, t=2)
        rows16 = rows_in[:, :, :, 0:P].bitcast(F16)
        t_bank = [banks[0][:, :].bitcast(F16), banks[1][:, :].bitcast(F16)]
        gu_bank, ht_bank, d_bank, table_bank = banks[2:4], banks[4:6], banks[6:8], banks[7]
        r_in = ctx_sb[:, 0:NB, :].rearrange("p (u c b) d -> p u c b d", u=4, c=2)

        gu_stage = stage[:, :].rearrange("p (e f c) -> p c e f", e=NE, c=2)

        def gu_chunk(p, r):
            at = p * STEPS + r - PAIRS * STEPS - 1 if isinstance(p, int) else -1
            return at if 0 <= at < 8 else None

        block = es.enter_context(nc.Block())

        def clear_ends(eng, experts):
            firsts_unused = [eng.value_load(ends[0:1, e:e + 1], min_val=e * ROOM, max_val=e * ROOM + TOK) for e in experts]
            for first in firsts_unused:
                eng.dma_start(places[bass.ds(first, P), :], blank[:, :]).then_inc(s["cleared"], 16)

        @block.sync
        def _(sp):
            for c in range(3):
                third = slice(c * INNER, (c + 1) * INNER)
                sp.dma_start(stage[:, third], W_qkv[:, third]).then_inc(in_w[c], 16)
            sp.dma_start(x_sb[:, 0:4, :], x[0:4].rearrange("b t d -> t b d")).then_inc(in_x[0], 16)
            by_head = W_out.rearrange("(h j i c d) n -> h c j i d n", h=2, j=2, i=2, c=2)
            for h in range(2):
                for c in range(2):
                    for i in range(2):
                        at = 3 * INNER + (2 * h + c) * 256
                        sp.dma_start(stage[64 * i:64 * i + 64, at:at + 256].rearrange("d (j n) -> d j n", j=2),
                                     by_head[h, c, :, i].rearrange("j d n -> d j n")).then_inc(s["in_wo"], 16)
            sp.dma_start(x_sb[:, 4:NB, :], x[4:NB].rearrange("b t d -> t b d")).then_inc(in_x[1], 16)
            sp.wait_ge(s["w_lo"], 3)
            sp.dma_start(stage[:, 0:NE * D].rearrange("f (e n) -> f e n", e=NE),
                         Wd.rearrange("e f n -> f e n")).then_inc(s["in_wd"], 16)
            sp.wait_ge(s["wo_lo"], 1)
            sp.wait_ge(s["d_lo"], 1)
            sp.dma_start(stage[:, :].rearrange("h (e n) -> h e n", e=NE),
                         Wgu.rearrange("e h n -> h e n")).then_inc(s["in_wgu"], 16)
            sp.wait_ge(s["bias_half"], 3)
            for half in range(2):
                for c in range(2):
                    sp.dma_start(bias_gu_rows[half, c].rearrange("(k f) -> k f", f=16),
                                 bgu_half[:, half, c, :]).then_inc(s["bias_out"], 16)
                sp.dma_start(bias_d_rows[half].rearrange("(k f) -> k f", f=16), bd_half[:, half, :]).then_inc(s["bias_out"], 16)
            sp.wait_ge(s["bias_out"], 16 * 6)
            for half in range(2):
                sp.dma_start(bias_gu[half:half + 1].rearrange("o e (c f) -> o e c f", c=2),
                             bias_gu_rows[half:half + 1].rearrange("o c (e f) -> o e c f", e=NE)).then_inc(s["bias_in"], 16)
                sp.dma_start(bias_d[half:half + 1].rearrange("o e f -> o (e f)"), bias_d_rows[half:half + 1]).then_inc(s["bias_in"], 16)
            sp.wait_ge(s["blank_ok"], 2)
            sp.dma_start(places[NE * ROOM:NE * ROOM + P, :], blank[:, :]).then_inc(s["blank_in"], 16)

            sp.wait_ge(s["ends_ok"], 1)
            clear_ends(sp, range(NE // 2))
            for par in range(2):
                sp.wait_ge(scattered[par], 64 * (PAIRS // 2))
            sp.wait_ge(s["cleared"], 16 * NE)
            sp.wait_ge(s["blank_in"], 16)
            sp.wait_ge(s["gu_lo"], 8)
            sp.wait_ge(s["table_ok"], 2)

            def load(q, u, i):
                if block_live(q, 0):
                    both = sp.value_load(block_starts[0:1, bass.ds(q, 1)], min_val=0, max_val=1024 * 1024 - 1)
                    wait_sent(sp, q, u, i, NBUF)
                    for t, at in enumerate((both % 1024, both // 1024)):
                        place = nc.s_assert_within(at, 0, NE * ROOM // P, skip_runtime_bounds_check_because="the table holds no other") * P
                        sp.dma_start(rows_in[:, u, t, :], places[bass.ds(place, P), :]).then_inc(block_in[u], 16)

            over_blocks(sp, load)

            for k in range(NZ):
                sp.wait_ge(z_sent[k], 32 * len(range(k, BPAIRS, NZ)))
            res = results.rearrange("(c b p) d -> c p b d", c=2, p=P)
            for g in range(NB // 4):
                if g >= 4:
                    sp.wait_ge(s["fin_ok"], g - 3)
                for c in range(2):
                    sp.dma_start(r_in[:, g % 4, c], res[c, :, 4 * g:4 * g + 4]).then_inc(results_in[g % 4], 16)

        @block.scalar
        def _(act):
            for c in range(4):
                act.dma_start(ctx_sb[:, 8 * c:8 * c + 8, :], ctx[8 * c:8 * c + 8].rearrange("b t d -> t b d")).then_inc(in_ctx[c], 16)
            act.dma_start(bout_bc[:, :], b_out.rearrange("(o d) -> o d", o=1).broadcast_to([P, D])).then_inc(s["in_small"], 16)
            act.dma_start(bg_bc[:, :], bg.rearrange("(o d) -> o d", o=1).broadcast_to([P, NE])).then_inc(s["in_small"], 16)
            act.dma_start(wg_nat[:, :], Wg).then_inc(s["in_small"], 16)
            act.dma_start(bgu_sb[:, :], bgu.rearrange("e (k f) -> (e k) f", k=8)).then_inc(s["in_small"], 16)
            act.dma_start(bd_sb[:, :], bd.rearrange("e (k f) -> (e k) f", k=8)).then_inc(s["in_small"], 16)
            act.wait_ge(s["scales"], 1)
            for c in range(3):
                third = slice(c * INNER, (c + 1) * INNER)
                nc.scalar.activation(w_qkv[:, HI, third], stage[:, third], ACT.Copy, scale=scale_to[:, 0:1]).then_inc(s["w_hi"], 1)
                if c == 0:
                    act.wait_ge(s["prep_mm"], 1)
                    nc.scalar.activation(xT[:, 0, HI, :], misc_bank[:, :], ACT.Copy).then_inc(s["prep_hi"], 1)

            def copy_qk(q, t):
                wait(act, "qk_mm", q * 8 + t + 1)
                wait(act, "qk_split", q * 8 + t - 1)
                nc.scalar.activation(qkf[:, t % 2, :], qk_bank[:, :], ACT.Copy).then_inc(s["qk_copied"], 1)

            def v_high(q, par, k):
                wait(act, "v_mm", q * 4 + k + 1)
                wait(act, "pv_mm", q * 8 - 12 + 4 * (k // 2))
                nc.scalar.activation(v[:, par, HI, k // 2, 8 * (k % 2):8 * (k % 2) + 8, 0:DH],
                                     misc_bank[:, :].rearrange("p (h d) -> p h d", h=8), ACT.Copy).then_inc(s["v_hi"], 1)

            for t in range(8):
                act.wait_ge(s["qk_mm"], t + 1)
                which, blk = (t % 4) // 2, 4 * (t // 4) + 2 * (t % 2)
                nc.scalar.activation(qk[:, 0, which, HI, blk:blk + 2, :].rearrange("p i n -> p (i n)"), qk_bank[:, :],
                                     ACT.Copy).then_inc(s["qk_high"], 1)
                if t >= 4:
                    v_high(0, 0, t - 4)
            act.wait_ge(s["prep_mm"], 2)
            nc.scalar.activation(xT[:, 1, HI, :], misc_bank[:, :], ACT.Copy).then_inc(s["prep_hi"], 1)
            act.wait_ge(s["scales"], 2)
            nc.scalar.activation(w_out[:, HI].rearrange("p b n -> p (b n)"), stage[:, 3 * INNER:4096], ACT.Copy,
                                 scale=scale_to[:, 2:3]).then_inc(s["wo_hi"], 1)

            def weights_high(p, r):
                if (p, r) == (0, 5):
                    act.wait_ge(s["scales2"], 1)
                    act.wait_ge(s["in_wd"], 16)
                    nc.scalar.activation(w_d[:, HI, :, :].rearrange("p e n -> p (e n)"), stage[:, 0:NE * D], ACT.Copy,
                                         scale=scale_to[:, 3:4]).then_inc(s["d_hi"], 1)
                k = gu_chunk(p, r)
                if k is not None:
                    act.wait_ge(s["scales2"], 2)
                    e4, half = slice(4 * (k % 4), 4 * (k % 4) + 4), k // 4
                    nc.scalar.activation(w_gu[:, HI, e4, half * P:(half + 1) * P], gu_stage[:, half, e4], ACT.Copy,
                                         scale=scale_to[:, 5:6]).then_inc(s["gu_hi"], 1)

            def steps(p, par):
                for r in range(STEPS):
                    n = p * STEPS + r
                    if live(p, r, 5):
                        wait(act, "ot_mm", n - 4)
                        wait(act, "out_mm", n - 6)
                        nc.scalar.activation(oT[:, (r + 1) % 2, HI, :], ot_bank[:, 0:256], ACT.Copy).then_inc(s["ot_hi"], 1)
                    if live(p, r, 1):
                        wait(act, "nbias_ok", n)
                        wait(act, "pt_mm", n - 2)
                        b = (r + 1) % 2
                        for k in range(4):
                            last = nc.scalar.activation(probs[:, b, k, :], score_bank[b][:, k * P:(k + 1) * P],
                                                        ACT.Exp, bias=nbias[:, b, k:k + 1], scale=fac[:, 0:1])
                        last.then_inc(s["exp_ok"], 1)
                    if r == 3 and pair_live(p - 2):
                        wait(act, "gap_ok", p - 1)
                        nc.scalar.activation(egap[:, :], gap[:, :], ACT.Exp).then_inc(s["egap_ok"], 1)
                    if pair_live(p + 1):
                        copy_qk(p + 1, r)
                    if live(p, r, 2):
                        wait(act, "pt_mm", n - 1)
                        wait(act, "pv_mm", n - 3)
                        nc.scalar.activation(pT[:, r % 2, HI, :], pt_bank[:, :], ACT.Copy).then_inc(s["pt_hi"], 1)
                    if ORDER[r][0] == "V" and pair_live(p + 1):
                        v_high(p + 1, 1 - par, int(ORDER[r][1]))
                    if ORDER[r] == "PREP" and pair_live(p + 2):
                        wait(act, "prep_mm", p + 3)
                        nc.scalar.activation(xT[:, par, HI, :], misc_bank[:, :], ACT.Copy).then_inc(s["prep_hi"], 1)
                    if ORDER[r] == "YT" and pair_live(p - 1):
                        wait(act, "yT_mm", p)
                        nc.scalar.activation(yT[:, :], misc_bank[:, 0:256], ACT.Copy).then_inc(s["misc_free"], 1)
                    if isinstance(p, int):
                        weights_high(p, r)

            over_pairs(act, steps)
            act.wait_ge(s["ends_ok"], 1)
            act.wait_ge(s["blank_ok"], 2)
            clear_ends(act, range(NE // 2, NE))

            def expert_steps(q, u, i):
                if block_live(q, 5):
                    wait(act, "d_mm", q - 4)
                    wait_sent(act, q, u, i, 5 + NZ)
                    for t in range(2):
                        nc.scalar.activation(z[:, (u - 5) % NZ, t, :], d_bank[(u + 1) % 2][:, t * P:(t + 1) * P], ACT.Copy,
                                             scale=rows_in[:, (u + NBUF - 5) % NBUF, t, P:P + 1]).then_inc(s["z_ok"], 1)
                if block_live(q, 0):
                    wait(act, "t_mm", q + 1)
                    wait(act, "gu_mm", q - 1)
                    nc.scalar.activation(bT[:, u % 2].rearrange("p a b c -> p (a b c)"), t_bank[u % 2][:, 0:512],
                                         ACT.Copy).then_inc(s["t_ok"], 1)
                if block_live(q, 3):
                    wait(act, "ht_mm", q - 2)
                    wait(act, "d_mm", q - 4)
                    nc.scalar.activation(hT[:, (u + 1) % 2, HI, :], ht_bank[(u + 1) % 2][:, 0:256], ACT.Copy).then_inc(s["ht_hi"], 1)
                if block_live(q, 1):
                    wait(act, "gate_ok", q)
                    wait(act, "glu_ok", q - 2)
                    nc.scalar.activation(sig[:, (u + 1) % 2], gate[:, (u + 1) % 2], ACT.Sigmoid, scale=ALPHA).then_inc(s["sig_ok"], 1)

            over_blocks(act, expert_steps)
            for g in range(NB // 4):
                act.wait_ge(s["fin_ok"], g + 1)
                act.dma_start(out[4 * g:4 * g + 4].rearrange("b t d -> t b d"), x_sb[:, 4 * g:4 * g + 4, :]).then_inc(s["fin_sent"], 16)
            act.wait_ge(s["fin_sent"], 16 * (NB // 4))

        @block.gpsimd
        def _(pool):
            nc.gpsimd.memset(ident[:, :], 0.0).then_inc(s["zeroed"], 1)
            nc.gpsimd.memset(ident16[:, :], 0.0).then_inc(s["zeroed"], 1)
            nc.gpsimd.memset(ones16[:, :], 1.0).then_inc(s["zeroed"], 1)
            nc.gpsimd.memset(minus_half[:, :], -0.5).then_inc(s["zeroed"], 1)
            nc.gpsimd.memset(zeros[:, :], 0.0).then_inc(s["zeroed"], 1)
            pool.wait_ge(s["zeroed"], 5)
            for t in (ident, ident16):
                nc.gpsimd.affine_select(out=t[:, :], in_=t[:, :], compare_op=ALU.not_equal, fill=1.0, base=0,
                                        pattern=[[-1, P]], channel_multiplier=1).then_inc(s["consts"], 1)
            nc.gpsimd.affine_select(out=before16[:, :], in_=ones16[:, :], compare_op=ALU.is_gt, fill=0.0, base=0,
                                    pattern=[[1, P]], channel_multiplier=-1).then_inc(s["consts"], 1)
            nc.gpsimd.memset(v[:, :, HI, :, :, DH:VW], 1.0).then_inc(s["ones_v"], 1)
            nc.gpsimd.memset(v[:, :, LO, :, :, DH:VW], 0.0).then_inc(s["ones_v"], 1)

            def inverse_root(ready, count, mean_var, ve, rs, done, adds):
                wait_alone(pool, ready, count)
                nc.gpsimd.tensor_scalar(ve[:, :], mean_var[:, :, 1], EPS, None, ALU.add).then_inc(s["pool_add"], 1)
                wait(pool, "pool_add", adds)
                nc.gpsimd.tensor_tensor(rs[:, :], ve[:, :], minus_half[:, :], ALU.pow).then_inc(s[done], 1)

            def add_b_out(q):
                wait(pool, "xhat_ok", q * 3 + 3)
                for j in range(2):
                    nc.gpsimd.tensor_tensor(x_sb[:, q * 2 + j, :], x_sb[:, q * 2 + j, :], bout_bc[:, :],
                                            ALU.add).then_inc(s["x_bias"], 1)

            def all_largest(a, b, count):
                pool.wait_ge(s["absmax"], count)
                nc.gpsimd.partition_all_reduce(top[:, a:b], largest[:, a:b], P, bass.bass_isa.ReduceOp.max).then_inc(s["allmax"], 1)

            inverse_root("stat_agg", 2, mv, var_eps, rstd, "rstd_ok", 1)
            all_largest(0, 2, 2)
            nc.gpsimd.iota(expert_no[:, :], pattern=[[1, NE]], base=0, channel_multiplier=0,
                           allow_small_or_imprecise_dtypes=True).then_inc(s["consts"], 1)
            nc.gpsimd.iota(next_place[:, 0, :], pattern=[[ROOM, NE]], base=0, channel_multiplier=0,
                           allow_small_or_imprecise_dtypes=True).then_inc(s["consts"], 1)
            nc.gpsimd.iota(row_no[:, :, :], pattern=[[P, NB], [TOK, 2]], base=0, channel_multiplier=1).then_inc(s["consts"], 1)
            nc.gpsimd.iota(part_no[:, :], pattern=[[0, 1]], base=0, channel_multiplier=1,
                           allow_small_or_imprecise_dtypes=True).then_inc(s["consts"], 1)
            nc.gpsimd.memset(blank[:, 0:P + 1], 0.0).then_inc(s["blank_ok"], 1)
            nc.gpsimd.memset(blank[:, P + 1:ROW].bitcast(I32), NOWHERE).then_inc(s["blank_ok"], 1)

            def split_qk(q, par, t):
                which, blk = (t % 4) // 2, 4 * (t // 4) + 2 * (t % 2)
                src = qkf[:, t % 2, :].rearrange("p (i n) -> p i n", i=2)
                wait(pool, "qk_copied", q * 8 + t - 7)
                if t == 0:
                    wait_alone(pool, "score_mm", q * 8 - 8)
                nc.gpsimd.tensor_tensor(qk[:, par, which, HI, blk:blk + 2, :], src, zeros[:, :].rearrange("p (i n) -> p i n", i=2),
                                        ALU.add).then_inc(s["qk_high"], 1)
                wait(pool, "qk_high", q * 8 + t + 1)
                nc.gpsimd.tensor_tensor(qk[:, par, which, LO, blk:blk + 2, :], src, qk[:, par, which, HI, blk:blk + 2, :],
                                        ALU.subtract).then_inc(s["qk_split"], 1)

            inverse_root("stat_agg", 4, mv, var_eps, rstd, "rstd_ok", 2)
            all_largest(2, 3, 3)
            pool.wait_ge(s["in_small"], 16 * 5)
            add_b_out(0)
            add_b_out(1)

            def adds_before(p):
                if isinstance(p, int):
                    return 2 + sum((pp + 2 < PAIRS) + (0 <= pp - 1 < PAIRS) for pp in range(p))
                return p * 2 + (adds_before(2) - 4)

            def steps(p, par):
                adds = adds_before(p)
                for r in range(STEPS):
                    if isinstance(p, int) and (p, r) == (0, 3):
                        all_largest(3, 5, 5)
                    if isinstance(p, int) and (p, r) == (1, 7):
                        all_largest(5, 7, 7)
                    if pair_live(p + 1):
                        split_qk(p + 1, 1 - par, r)
                    if r == 0 and pair_live(p + 2):
                        adds = adds + 1
                        inverse_root("stat_agg", p * 2 + 6, mv, var_eps, rstd, "rstd_ok", adds)
                    if r == 2 and pair_live(p + 2):
                        add_b_out(p + 2)
                    if r == 5 and pair_live(p - 1):
                        adds = adds + 1
                        inverse_root("stat2_agg", p * 2, mv2, var_eps2, rstd2, "rstd2_ok", adds)
                    if r == 5 and pair_live(p - 2):
                        wait(pool, "slots_ok", p - 1)
                        wait(pool, "wgt_ok", p * 3 - 3)
                        wait_alone(pool, "yhalf", p * 4 - 4)
                        for j in range(2):
                            for c in range(2):
                                nc.gpsimd.indirect_dma_start(
                                    out=places, out_offset=bass.IndirectOffsetOnAxis(ap=slots[:, par, 2 * j + c:2 * j + c + 1], axis=0),
                                    in_=payload[:, par, j, c, :], in_offset=None).then_inc(scattered[par], 16)

            over_pairs(pool, steps)

            def send(q, u, i):
                if block_live(q, 5):
                    for t in range(2):
                        wait_alone(pool, "z_ok", q * 2 - 9 + t)
                        to = rows_in[:, (u + NBUF - 5) % NBUF, t, P + 1:ROW].bitcast(U32)
                        nc.gpsimd.indirect_dma_start(
                            out=results, out_offset=bass.IndirectOffsetOnAxis(ap=to, axis=0),
                            in_=z[:, (u - 5) % NZ, t, :], in_offset=None,
                            bounds_check=2 * TOK - 1, oob_is_err=False).then_inc(z_sent[(u - 5) % NZ], 16)

            over_blocks(pool, send)

        @block.vector
        def _(dve):
            count = [0]

            def link(ins):
                count[0] += 1
                ins.then_inc(s["setup"], 1)
                dve.wait_ge(s["setup"], count[0])

            def magnitude(col, ap):
                nc.vector.tensor_reduce(largest[:, col:col + 1], ap, AX.X, ALU.max,
                                        apply_absolute_value=True).then_inc(s["absmax"], 1)

            parts = [0]

            def part_magnitude(ap):
                nc.vector.tensor_reduce(part_largest[:, parts[0]:parts[0] + 1], ap, AX.X, ALU.max,
                                        apply_absolute_value=True).then_inc(s["part_max"], 1)
                parts[0] += 1

            def make_scales(a, b, name):
                link(nc.vector.tensor_scalar(top[:, a:b], top[:, a:b], TINY, 1.0 / TOP, ALU.max, ALU.mult))
                link(nc.vector.tensor_copy(scale_from[:, a:b], top[:, a:b]))
                nc.vector.reciprocal(scale_to[:, a:b], scale_from[:, a:b]).then_inc(s[name], 1)

            def prep_stats(q):
                wait_alone(dve, "xhat_ok", q * 3)
                for j in range(2):
                    nc.vector.bn_stats(stats[:, j, :], x_sb[:, q * 2 + j, :]).then_inc(s["stat"], 1)
                for j in range(2):
                    wait_alone(dve, "stat", q * 2 + j + 1)
                    nc.vector.bn_aggr(mv[:, j, :], stats[:, j, :]).then_inc(s["stat_agg"], 1)

            def prep_rows(q):
                wait(dve, "rstd_ok", q + 1)
                wait(dve, "prep_mm", q)
                for j in range(2):
                    nc.vector.tensor_scalar(xhat[:, 0, j, :], x_sb[:, q * 2 + j, :], mv[:, j, 0:1], rstd[:, j:j + 1],
                                            ALU.subtract, ALU.mult).then_inc(s["xhat_ok"], 1)
                nc.vector.tensor_scalar(xhat[:, 1, :, :], ctx_sb[:, bass.ds(q * 2, 2), :], scale_to[:, 1:2], None,
                                        ALU.mult).then_inc(s["xhat_ok"], 1)

            def prep_low(q, par):
                wait(dve, "prep_hi", q + 1)
                nc.vector.tensor_tensor(xT[:, par, LO, :], misc_bank[:, :], xT[:, par, HI, :], ALU.subtract).then_inc(s["misc_free"], 1)

            def v_low(q, par, k):
                wait(dve, "v_hi", q * 4 + k + 1)
                heads = slice(8 * (k % 2), 8 * (k % 2) + 8)
                nc.vector.tensor_tensor(v[:, par, LO, k // 2, heads, 0:DH], misc_bank[:, :].rearrange("p (h d) -> p h d", h=8),
                                        v[:, par, HI, k // 2, heads, 0:DH], ALU.subtract).then_inc(s["misc_free"], 1)

            for c in range(3):
                dve.wait_ge(in_w[c], 16)
                part_magnitude(stage[:, c * INNER:(c + 1) * INNER])
            dve.wait_ge(in_x[0], 16)
            prep_stats(0)
            for c in range(4):
                dve.wait_ge(in_ctx[c], 16)
                part_magnitude(ctx_sb[:, 8 * c:8 * c + 8, :].rearrange("p b d -> p (b d)"))
            dve.wait_ge(s["part_max"], 7)
            magnitude(0, part_largest[:, 0:3])
            magnitude(1, part_largest[:, 3:7])
            dve.wait_ge(s["allmax"], 1)
            make_scales(0, 2, "scales")
            dve.wait_ge(s["scales"], 1)
            prep_rows(0)

            def qkv_low(c):
                third = slice(c * INNER, (c + 1) * INNER)
                dve.wait_ge(s["w_hi"], c + 1)
                nc.vector.scalar_tensor_tensor(out=w_qkv[:, LO, third], in0=stage[:, third], scalar=scale_to[:, 0:1],
                                               in1=w_qkv[:, HI, third], op0=ALU.mult, op1=ALU.subtract).then_inc(s["w_lo"], 1)

            def first_low(t):
                which, blk = (t % 4) // 2, 4 * (t // 4) + 2 * (t % 2)
                dve.wait_ge(s["qk_high"], t + 1)
                nc.vector.tensor_tensor(qk[:, 0, which, LO, blk:blk + 2, :], qk_bank[:, :].rearrange("p (i n) -> p i n", i=2),
                                        qk[:, 0, which, HI, blk:blk + 2, :], ALU.subtract).then_inc(s["qk_split"], 1)

            qkv_low(0)
            prep_low(0, 0)
            qkv_low(1)
            first_low(0)
            qkv_low(2)
            first_low(1)
            prep_stats(1)
            first_low(2)
            dve.wait_ge(s["in_wo"], 16 * 8)
            magnitude(2, stage[:, 3 * INNER:4096])
            first_low(3)
            prep_rows(1)
            link(nc.vector.tensor_tensor(fac[:, 1:2], scale_from[:, 0:1], scale_from[:, 1:2], ALU.mult))
            for t in range(4, 8):
                first_low(t)
                if t == 4:
                    link(nc.vector.tensor_tensor(fac[:, 4:5], fac[:, 1:2], scale_from[:, 0:1], ALU.mult))
                    link(nc.vector.tensor_scalar(fac[:, 0:1], fac[:, 4:5], DH ** -0.5, None, ALU.mult))
                    link(nc.vector.tensor_scalar(fac[:, 2:3], fac[:, 4:5], -DH ** -0.5, None, ALU.mult))
                v_low(0, 0, t - 4)
            prep_low(1, 1)
            dve.wait_ge(s["allmax"], 2)
            make_scales(2, 3, "scales")
            dve.wait_ge(s["scales"], 2)
            link(nc.vector.tensor_tensor(fac[:, 3:4], fac[:, 1:2], scale_from[:, 2:3], ALU.mult))
            dve.wait_ge(s["wo_hi"], 1)
            nc.vector.scalar_tensor_tensor(out=w_out[:, LO].rearrange("p b n -> p (b n)"), in0=stage[:, 3 * INNER:4096],
                                           scalar=scale_to[:, 2:3], in1=w_out[:, HI].rearrange("p b n -> p (b n)"),
                                           op0=ALU.mult, op1=ALU.subtract).then_inc(s["wo_lo"], 1)

            def with_bias(a, b):
                dve.wait_ge(s["allmax"], 3 if a == 3 else 4)
                link(nc.vector.tensor_tensor(top[:, a:a + 1], top[:, a:a + 1], top[:, b:b + 1], ALU.max))
                make_scales(a, a + 1, "scales2")
                dve.wait_ge(s["scales2"], 1 if a == 3 else 2)

            def split(hi, lo, src, scale):
                link(nc.vector.tensor_scalar(hi, src, scale, None, ALU.mult))
                nc.vector.scalar_tensor_tensor(out=lo, in0=src, scalar=scale, in1=hi,
                                               op0=ALU.mult, op1=ALU.subtract).then_inc(s["bias_half"], 1)

            dve.wait_ge(s["in_small"], 16 * 5)
            b_up = bgu_sb[:, :].rearrange("p (f c) -> p f c", c=2)[:, :, 1]
            link(nc.vector.tensor_scalar(b_up, b_up, 1.0, None, ALU.add))
            dve.wait_ge(s["wgT_mm"], 1)
            nc.vector.tensor_copy(wg_T[:, :], out_bank[:, 0:NE]).then_inc(s["wgT_ok"], 1)

            def weights_low(p, r):
                if (p, r) == (0, 2):
                    dve.wait_ge(s["in_wd"], 16)
                    magnitude(3, stage[:, 0:NE * D])
                    magnitude(4, bd_sb[:, :])
                if (p, r) == (0, 4):
                    with_bias(3, 4)
                    split(bd_half[:, HI, :], bd_half[:, LO, :], bd_sb[:, :], scale_to[:, 3:4])
                if (p, r) == (0, 6):
                    dve.wait_ge(s["d_hi"], 1)
                    nc.vector.scalar_tensor_tensor(out=w_d[:, LO].rearrange("p e n -> p (e n)"), in0=stage[:, 0:NE * D],
                                                   scalar=scale_to[:, 3:4], in1=w_d[:, HI].rearrange("p e n -> p (e n)"),
                                                   op0=ALU.mult, op1=ALU.subtract).then_inc(s["d_lo"], 1)
                if p == 1 and 2 <= r < 6:
                    dve.wait_ge(s["in_wgu"], 16)
                    part_magnitude(stage[:, (r - 2) * 1024:(r - 1) * 1024])
                if (p, r) == (1, 6):
                    dve.wait_ge(s["part_max"], 11)
                    magnitude(5, part_largest[:, 7:11])
                    magnitude(6, bgu_sb[:, :])
                if (p, r) == (LAST, 0):
                    with_bias(5, 6)
                    for c in range(2):
                        split(bgu_half[:, HI, c, :], bgu_half[:, LO, c, :],
                              bgu_sb[:, :].rearrange("p (f c) -> p c f", c=2)[:, c], scale_to[:, 5:6])
                k = gu_chunk(p, r)
                if k is not None:
                    e4, half = slice(4 * (k % 4), 4 * (k % 4) + 4), k // 4
                    dve.wait_ge(s["gu_hi"], k + 1)
                    nc.vector.scalar_tensor_tensor(out=w_gu[:, LO, e4, half * P:(half + 1) * P], in0=gu_stage[:, half, e4],
                                                   scalar=scale_to[:, 5:6], in1=w_gu[:, HI, e4, half * P:(half + 1) * P],
                                                   op0=ALU.mult, op1=ALU.subtract).then_inc(s["gu_lo"], 1)

            def steps(p, par):
                for r in range(STEPS):
                    n = p * STEPS + r
                    if live(p, r, 0):
                        wait(dve, "score_mm", n + 1)
                        nc.vector.tensor_reduce(qmax[:, r % 2, :], score_bank[r % 2][:, :].rearrange("p (h k) -> p h k", h=4),
                                                AX.X, ALU.max).then_inc(s["qmax_ok"], 1)
                    if live(p, r, 5):
                        wait(dve, "ot_hi", n - 4)
                        nc.vector.tensor_tensor(oT[:, (r + 1) % 2, LO, :], ot_bank[:, 0:256], oT[:, (r + 1) % 2, HI, :],
                                                ALU.subtract).then_inc(s["ot_lo"], 1)
                    if live(p, r, 0):
                        wait(dve, "qmax_ok", n + 1)
                        wait(dve, "exp_ok", n - 1)
                        nc.vector.tensor_scalar(nbias[:, r % 2, :], qmax[:, r % 2, :], fac[:, 2:3], None,
                                                ALU.mult).then_inc(s["nbias_ok"], 1)
                    if r in (1, 5) and pair_live(p - 1):
                        j = r // 4
                        wait(dve, "out_mm", p * 8 - 4 + 4 * j)
                        wait(dve, "x_bias", p * 2)
                        row = x_sb[:, p * 2 - 2 + j, :]
                        nc.vector.scalar_tensor_tensor(out=row, in0=out_bank[:, 0:P], scalar=fac[:, 3:4], in1=row,
                                                       op0=ALU.mult, op1=ALU.add).then_inc(s["x1_ok"], 1)
                    if r == 1 and pair_live(p - 2):
                        wait_alone(dve, "misc_free", misc_before(p, "V0"))
                        for j in range(2):
                            nc.vector.max(best[:, j, :], logits[:, j, :]).then_inc(s["best_ok"], 1)
                    if r == 2 and pair_live(p - 2):
                        wait(dve, "best_at_ok", p * 2 - 2)
                        nc.vector.tensor_copy(choice[:, :].rearrange("p (j k) -> p j k", j=2), best_at[:, :, 0:2]).then_inc(s["choice_ok"], 1)
                        nc.vector.tensor_tensor(gap[:, :], best[:, :, 1], best[:, :, 0], ALU.subtract).then_inc(s["gap_ok"], 1)
                    if r == 4 and pair_live(p - 2):
                        wait(dve, "rank_mm", p - 1)
                        now = next_place[:, par, :]
                        nc.vector.tensor_tensor(place_all[:, :, :], misc_bank[:, 0:2 * NE].rearrange("p (j e) -> p j e", j=2),
                                                now.unsqueeze(1).to_broadcast([P, 2, NE]), ALU.add).then_inc(s["place_ok"], 1)
                        nc.vector.tensor_tensor(next_place[:, 1 - par, :], misc_bank[:, 2 * NE:3 * NE], now, ALU.add).then_inc(s["misc_free"], 1)
                    if r == 5 and pair_live(p - 1):
                        for j in range(2):
                            wait_alone(dve, "x1_ok", p * 2 - 1 + j)
                            nc.vector.bn_stats(stats2[:, j, :], x_sb[:, p * 2 - 2 + j, :]).then_inc(s["stat2"], 1)
                    if live(p, r, 2):
                        wait(dve, "pt_hi", n - 1)
                        nc.vector.tensor_tensor(pT[:, r % 2, LO, :], pt_bank[:, :], pT[:, r % 2, HI, :],
                                                ALU.subtract).then_inc(s["pt_lo"], 1)
                    if live(p, r, 3):
                        wait(dve, "pv_mm", n - 2)
                        nc.vector.reciprocal(rsum[:, :], o_bank[:, 0:4 * (DH + 1)].rearrange("p (h w) -> p h w", h=4)[:, :, DH]).then_inc(s["rsum_ok"], 1)
                    if ORDER[r][0] == "V" and pair_live(p + 1):
                        v_low(p + 1, 1 - par, int(ORDER[r][1]))
                    if r == 0 and pair_live(p + 2):
                        if isinstance(p, int) and p == 0:
                            dve.wait_ge(in_x[1], 16)
                        prep_stats(p + 2)
                    if r == 1 and pair_live(p - 2):
                        for j in range(2):
                            wait_alone(dve, "best_ok", p * 2 - 3 + j)
                            nc.vector.max_index(best_at[:, j, :], best[:, j, :], logits[:, j, :]).then_inc(s["best_at_ok"], 1)
                    if r == 2 and pair_live(p - 2):
                        wait(dve, "choice_ok", p - 1)
                        nc.vector.tensor_tensor(onehot[:, :, :], expert_no[:, :].unsqueeze(1).to_broadcast([P, 4, NE]),
                                                choice[:, :].unsqueeze(2).to_broadcast([P, 4, NE]), ALU.is_equal).then_inc(s["onehot_ok"], 1)
                    if r == 4 and pair_live(p - 2):
                        wait(dve, "place_ok", p - 1)
                        for j in range(2):
                            nc.vector.tensor_tensor(picked[:, 2 * j:2 * j + 2, :], onehot[:, 2 * j:2 * j + 2, :],
                                                    place_all[:, j, :].unsqueeze(1).to_broadcast([P, 2, NE]), ALU.mult).then_inc(s["picked_ok"], 1)
                        wait(dve, "egap_ok", p - 1)
                        nc.vector.tensor_scalar(denom[:, :], egap[:, :], 1.0, None, ALU.add).then_inc(s["denom_ok"], 1)
                    if r == 5 and pair_live(p - 1):
                        for j in range(2):
                            wait_alone(dve, "stat2", p * 2 - 1 + j)
                            nc.vector.bn_aggr(mv2[:, j, :], stats2[:, j, :]).then_inc(s["stat2_agg"], 1)
                    if r == 6 and pair_live(p - 1):
                        wait(dve, "rstd2_ok", p)
                        wait(dve, "yT_mm", p - 1)
                        for j in range(2):
                            nc.vector.tensor_scalar(y[:, j, :], x_sb[:, p * 2 - 2 + j, :], mv2[:, j, 0:1], rstd2[:, j:j + 1],
                                                    ALU.subtract, ALU.mult).then_inc(s["y_ok"], 1)
                    if live(p, r, 3):
                        wait(dve, "rsum_ok", n - 2)
                        wait(dve, "ot_mm", n - 4)
                        nc.vector.tensor_tensor(o_nat[:, (r + 1) % 2, :].rearrange("p (h d) -> p h d", h=4),
                                                o_bank[:, 0:4 * (DH + 1)].rearrange("p (h w) -> p h w", h=4)[:, :, 0:DH],
                                                rsum[:, :].unsqueeze(2).to_broadcast([P, 4, DH]), ALU.mult).then_inc(s["o_ok"], 1)
                    if r == 2 and pair_live(p - 2):
                        wait(dve, "onehot_ok", p - 1)
                        both = onehot[:, :, :].rearrange("p (j k) e -> p j k e", j=2)
                        nc.vector.tensor_tensor(chosen16[:, :, :], both[:, :, 0, :], both[:, :, 1, :], ALU.add).then_inc(s["chosen_ok"], 1)
                    if r == 4 and pair_live(p - 2):
                        wait(dve, "picked_ok", p * 2 - 2)
                        with nc.allow_low_precision(reason="one whole number and zeros, exact"):
                            nc.vector.tensor_reduce(slots[:, par, :], picked[:, :, :], AX.X, ALU.add).then_inc(s["slots_ok"], 1)
                        wait(dve, "denom_ok", p - 1)
                        nc.vector.reciprocal(payload[:, par, :, 0, P], denom[:, :]).then_inc(s["wgt_ok"], 1)
                        nc.vector.tensor_copy(payload[:, par, :, :, P + 1].bitcast(I32), row_no[:, bass.ds(p * 2 - 4, 2), :]).then_inc(s["wgt_ok"], 1)
                        wait(dve, "wgt_ok", p * 3 - 4)
                        nc.vector.tensor_tensor(payload[:, par, :, 1, P], payload[:, par, :, 0, P], egap[:, :], ALU.mult).then_inc(s["wgt_ok"], 1)
                    if r == 6 and pair_live(p - 1):
                        if not isinstance(p, int) or p > 2:
                            dve.wait_ge(scattered[1 - par], (p - 2 + par) * 32)
                        for j in range(2):
                            wait(dve, "y_ok", p * 2 - 1 + j)
                            nc.vector.tensor_copy(halves[:, 1 - par, j, :, 0:P], y[:, j, :].unsqueeze(1).to_broadcast([P, 2, P])).then_inc(s["yhalf"], 1)
                    if r == 6 and pair_live(p - 1):
                        for j in range(2):
                            wait(dve, "yhalf", p * 4 - 3 + j)
                            nc.vector.tensor_tensor(halves[:, 1 - par, j, :, P:2 * P], y[:, j, :].unsqueeze(1).to_broadcast([P, 2, P]),
                                                    halves[:, 1 - par, j, :, 0:P], ALU.subtract).then_inc(s["yhalf"], 1)
                    if r == 2 and pair_live(p + 2):
                        prep_rows(p + 2)
                    if ORDER[r] == "PREP" and pair_live(p + 2):
                        prep_low(p + 2, par)
                    if ORDER[r] == "LG" and pair_live(p - 2):
                        wait(dve, "lg_mm", p - 1)
                        nc.vector.tensor_tensor(logits[:, :, :], misc_bank[:, 0:2 * NE].rearrange("p (j e) -> p j e", j=2),
                                                bg_bc[:, :].unsqueeze(1).to_broadcast([P, 2, NE]), ALU.add).then_inc(s["misc_free"], 1)

                    if isinstance(p, int):
                        weights_low(p, r)

            over_pairs(dve, steps)

            final = next_place[:, PAIRS % 2, :]
            dve.wait_ge(s["misc_free"], misc_before(PAIRS + 2, "V0"))
            counts, blocks, upto, passed, mine, first = (blocks_f[:, k, :] for k in range(6))
            nc.vector.tensor_copy(ends[:, :], final[0:1, :]).then_inc(s["ends_ok"], 1)
            link(nc.vector.scalar_tensor_tensor(out=counts, in0=expert_no[:, :], scalar=-float(ROOM), in1=final, op0=ALU.mult, op1=ALU.add))
            link(nc.vector.tensor_scalar(blocks_i[:, :], counts, float(P - 1), None, ALU.add))
            link(nc.vector.tensor_scalar(blocks_i[:, :], blocks_i[:, :], 7, None, ALU.logical_shift_right))
            link(nc.vector.tensor_copy(blocks, blocks_i[:, :]))
            link(nc.vector.memset(first, 1.0))
            link(nc.vector.tensor_tensor_scan(upto, first, blocks, 0.0, ALU.mult, ALU.add))
            link(nc.vector.tensor_scalar(passed, upto, part_no[:, 0:1], None, ALU.is_le))
            link(nc.vector.tensor_tensor(mine, passed, blocks, ALU.mult))
            link(nc.vector.tensor_reduce(table_f[:, 0:1], passed, AX.X, ALU.add))
            link(nc.vector.tensor_reduce(table_f[:, 2:3], mine, AX.X, ALU.add))
            link(nc.vector.tensor_tensor(table_f[:, 3:4], part_no[:, :], table_f[:, 2:3], ALU.subtract))
            link(nc.vector.scalar_tensor_tensor(out=table_f[:, 1:2], in0=table_f[:, 0:1], scalar=float(ROOM // P), in1=table_f[:, 3:4],
                                                op0=ALU.mult, op1=ALU.add))
            link(nc.vector.tensor_scalar(table_f[:, 1:2], table_f[:, 1:2], float(NE * ROOM // P), None, ALU.min))
            nc.vector.tensor_scalar(table_f[:, 0:1], table_f[:, 0:1], float(NE - 1), None, ALU.min).then_inc(s["table_cols"], 1)
            dve.wait_ge(s["table_mm"], 1)
            two = table_bank[0:1, 0:2 * P].rearrange("p (c b t) -> p c b t", c=2, t=2)
            nc.vector.tensor_copy(firsts[:, :, :], two[:, :, :, 0]).then_inc(s["first_ok"], 1)
            dve.wait_ge(s["first_ok"], 1)
            for c, (packed, base) in enumerate(((expert_pairs, NE), (block_starts, 1024))):
                nc.vector.scalar_tensor_tensor(out=packed[:, :], in0=two[:, c, :, 1], scalar=float(base), in1=firsts[:, c, :],
                                               op0=ALU.mult, op1=ALU.add).then_inc(s["table_ok"], 1)

            dve.wait_ge(s["table_ok"], 2)
            four = expert_pairs[:, :].rearrange("o (g t) -> o g t", t=2)
            nc.vector.scalar_tensor_tensor(out=block_experts[:, :], in0=four[:, :, 1], scalar=float(NE * NE), in1=four[:, :, 0],
                                           op0=ALU.mult, op1=ALU.add).then_inc(s["table_ok"], 1)

            def expert_steps(q, u, i):
                if block_live(q, 2):
                    wait(dve, "sig_ok", q - 1)
                    wait(dve, "h_ok", q - 2)
                    nc.vector.tensor_tensor(glu[:, :, :], gate[:, u % 2], sig[:, u % 2], ALU.mult).then_inc(s["glu_ok"], 1)
                    wait(dve, "glu_ok", q - 1)
                    wait(dve, "ht_mm", q - 3)
                    nc.vector.scalar_tensor_tensor(out=hidden[:, u % 2], in0=up[:, u % 2], scalar=1.0 - LIMIT,
                                                   in1=glu[:, :, :], op0=ALU.max, op1=ALU.mult).then_inc(s["h_ok"], 1)
                if block_live(q, 1):
                    wait(dve, "gu_mm", q)
                    wait(dve, "h_ok", q - 2)
                    b = (u + 1) % 2
                    bank = gu_bank[b][:, :].rearrange("p (t c f) -> p t c f", t=2, c=2)
                    nc.vector.tensor_scalar(gate[:, b], bank[:, :, 0, :], scale_from[:, 5:6], LIMIT, ALU.mult, ALU.min).then_inc(s["gate_ok"], 1)
                    nc.vector.tensor_scalar(up[:, b], bank[:, :, 1, :], scale_from[:, 5:6], 1.0 + LIMIT, ALU.mult, ALU.min).then_inc(s["up_ok"], 1)
                if block_live(q, 3):
                    wait(dve, "ht_hi", q - 2)
                    nc.vector.tensor_tensor(hT[:, (u + 1) % 2, LO, :], ht_bank[(u + 1) % 2][:, 0:256], hT[:, (u + 1) % 2, HI, :],
                                            ALU.subtract).then_inc(s["ht_lo"], 1)

            over_blocks(dve, expert_steps)

            for g in range(NB // 4):
                dve.wait_ge(results_in[g % 4], 32 * (g // 4 + 1))
                nc.vector.tensor_tensor(r_in[:, g % 4, 0], r_in[:, g % 4, 0], r_in[:, g % 4, 1], ALU.add).then_inc(s["sum_ok"], 1)
                dve.wait_ge(s["sum_ok"], g + 1)
                rows = x_sb[:, 4 * g:4 * g + 4, :]
                nc.vector.scalar_tensor_tensor(out=rows, in0=r_in[:, g % 4, 0], scalar=scale_from[:, 3:4], in1=rows,
                                               op0=ALU.mult, op1=ALU.add).then_inc(s["fin_ok"], 1)

        @block.tensor
        def _(pe):
            def three(dst, a_hi, a_lo, b_hi, b_lo, start=True, stop=True):
                nc.tensor.matmul(dst, a_hi, b_hi, start=start, stop=False)
                nc.tensor.matmul(dst, a_hi, b_lo, start=False, stop=False)
                return nc.tensor.matmul(dst, a_lo, b_hi, start=False, stop=stop)

            def prep(q):
                wait(pe, "xhat_ok", q * 3 + 3)
                for w in range(2):
                    for j in range(2):
                        last = nc.tensor.transpose(misc_bank[:, (2 * w + j) * P:(2 * w + j + 1) * P], xhat[:, w, j, :], ident[:, :])
                last.then_inc(s["prep_mm"], 1)

            def project_qk(q, par, t):
                which, blk = (t % 4) // 2, 4 * (t // 4) + 2 * (t % 2)
                src = slice(which * 256, which * 256 + 256)
                if isinstance(q, int) and q * 8 + t <= 8:
                    wait(pe, "qk_split", q * 8 + t)
                else:
                    wait(pe, "qk_copied", q * 8 + t - 8)
                for i in range(2):
                    col = which * INNER + (blk + i) * P
                    last = three(qk_bank[:, i * 256:i * 256 + 256], w_qkv[:, HI, col:col + P], w_qkv[:, LO, col:col + P],
                                 xT[:, par, HI, src], xT[:, par, LO, src])
                last.then_inc(s["qk_mm"], 1)

            def project_v(par, k):
                tok = slice(256 + (k // 2) * P, 256 + (k // 2) * P + P)
                cols = slice(2 * INNER + (k % 2) * 512, 2 * INNER + (k % 2) * 512 + 512)
                three(misc_bank[:, :], xT[:, par, HI, tok], xT[:, par, LO, tok], w_qkv[:, HI, cols], w_qkv[:, LO, cols]
                      ).then_inc(s["v_mm"], 1)

            pe.wait_ge(s["consts"], 7)
            pe.wait_ge(s["in_small"], 16 * 5)
            nc.tensor.transpose(out_bank[:, 0:NE], wg_nat[:, :], ident[0:NE, 0:NE]).then_inc(s["wgT_mm"], 1)
            prep(0)
            wait(pe, "misc_free", 1)
            for t in range(8):
                pe.wait_ge(s["w_lo"], min(t // 2 + 1, 3))
                project_qk(0, 0, t)
                if t >= 4:
                    wait(pe, "misc_free", t - 3)
                    project_v(0, t - 4)
            wait(pe, "misc_free", 5)
            prep(1)
            pe.wait_ge(s["wgT_ok"], 1)
            pe.wait_ge(s["ones_v"], 2)

            def scores(par, r, n):
                j, half, odd = r // 4, (r // 2) % 2, r % 2
                rows, tok = slice(64 * odd, 64 * odd + 64), slice(j * P, j * P + P)
                wait(pe, "exp_ok", n - 1)
                for k in range(4):
                    a = [qk[rows, par, 0, h, 4 * half + k, tok] for h in range(2)]
                    b = [qk[rows, par, 1, h, 4 * half + k, tok] for h in range(2)]
                    last = three(score_bank[r % 2][:, k * P:(k + 1) * P], a[HI], a[LO], b[HI], b[LO])
                last.then_inc(s["score_mm"], 1)

            def steps(p, par):
                for r in range(STEPS):
                    n = p * STEPS + r
                    if live(p, r, 0):
                        if r in (0, 2):
                            wait(pe, "qk_split", p * 8 + 4 + 2 * r)
                        scores(par, r, n)
                    if pair_live(p + 1):
                        project_qk(p + 1, 1 - par, r)
                    if live(p, r, 2):
                        wait(pe, "exp_ok", n - 1)
                        wait(pe, "pt_lo", n - 2)
                        for k in range(4):
                            last = nc.tensor.transpose(pt_bank[:, k * P:(k + 1) * P], probs[:, r % 2, k, :], ident[:, :])
                        last.then_inc(s["pt_mm"], 1)
                    item = ORDER[r]
                    if pair_live(p + USES[item]):
                        wait(pe, "misc_free", misc_before(p, item))
                        if item[0] == "V":
                            project_v(1 - par, int(item[1]))
                        elif item == "PREP":
                            prep(p + 2)
                        elif item == "RANK":
                            wait(pe, "chosen_ok", p - 1)
                            c0, c1 = chosen16[:, 0, :], chosen16[:, 1, :]
                            nc.tensor.matmul(misc_bank[:, 0:NE], before16[:, :], c0, start=True, stop=True)
                            for at, first in ((NE, before16), (2 * NE, ones16)):
                                nc.tensor.matmul(misc_bank[:, at:at + NE], first[:, :], c1, start=True, stop=False)
                                last = nc.tensor.matmul(misc_bank[:, at:at + NE], ones16[:, :], c0, start=False, stop=True)
                            last.then_inc(s["rank_mm"], 1)
                        elif item == "YT":
                            wait(pe, "y_ok", p * 2)
                            for j in range(2):
                                last = nc.tensor.transpose(misc_bank[:, j * P:(j + 1) * P], y[:, j, :], ident[:, :])
                            last.then_inc(s["yT_mm"], 1)
                        else:
                            for j in range(2):
                                last = nc.tensor.matmul(misc_bank[:, j * NE:(j + 1) * NE], yT[:, j * P:(j + 1) * P], wg_T[:, :],
                                                        start=True, stop=True)
                            last.then_inc(s["lg_mm"], 1)
                    if live(p, r, 3):
                        vp = par if r >= 3 else 1 - par
                        rr = (r - 3) % STEPS
                        j, half, odd = rr // 4, (rr // 2) % 2, rr % 2
                        wait(pe, "pt_lo", n - 2)
                        wait(pe, "o_ok", n - 3)
                        if r == 3 and isinstance(p, int) and p < 2:
                            wait(pe, "misc_free", 6 if p == 0 else misc_before(0, "V3") + 1)
                        for k in range(4):
                            head, tok = 8 * half + 2 * k + odd, slice(k * P, k * P + P)
                            last = three(o_bank[:, k * (DH + 1):(k + 1) * (DH + 1)], pT[:, (r + 1) % 2, HI, tok], pT[:, (r + 1) % 2, LO, tok],
                                         v[:, vp, HI, j, head, 0:DH + 1], v[:, vp, LO, j, head, 0:DH + 1])
                        last.then_inc(s["pv_mm"], 1)
                    if live(p, r, 4):
                        wait(pe, "o_ok", n - 3)
                        wait(pe, "ot_lo", n - 4)
                        for k in range(2):
                            last = nc.tensor.transpose(ot_bank[:, k * P:(k + 1) * P], o_nat[:, r % 2, k * P:(k + 1) * P], ident[:, :])
                        last.then_inc(s["ot_mm"], 1)
                    if live(p, r, 5):
                        wait(pe, "ot_lo", n - 4)
                        if isinstance(p, int) and (p, r) == (0, 5):
                            pe.wait_ge(s["wo_lo"], 1)
                        if r % 4 == 1:
                            wait(pe, "x1_ok", p * 2 - 1 + r // 4)
                        for k in range(2):
                            blk = 2 * ((r - 5) % 4) + k
                            last = three(out_bank[:, 0:P], oT[:, (r + 1) % 2, HI, k * P:(k + 1) * P], oT[:, (r + 1) % 2, LO, k * P:(k + 1) * P],
                                         w_out[:, HI, blk, :], w_out[:, LO, blk, :], start=(blk == 0), stop=(blk == 7))
                        last.then_inc(s["out_mm"], 1)

            over_pairs(pe, steps)

            pe.wait_ge(s["table_cols"], 1)
            for c in range(2):
                last = nc.tensor.matmul(table_bank[0:1, c * P:(c + 1) * P], table_f[:, c:c + 1], ident[:, :], start=True, stop=True)
            last.then_inc(s["table_mm"], 1)
            pe.wait_ge(s["table_ok"], 3)
            pe.wait_ge(s["gu_lo"], 8)
            pe.wait_ge(s["bias_in"], 16 * 4)

            def plus_bias(dst, a_hi, a_lo, b_hi, b_lo, bias):
                nc.tensor.matmul(dst, ones16[0:2, :], bias, start=True, stop=False)
                return three(dst, a_hi, a_lo, b_hi, b_lo, start=False)

            known = {}

            def load_experts(g, i):
                if g not in known:
                    four = pe.value_load(block_experts[0:1, bass.ds(i * (NBUF // 2) + g, 1)], min_val=0, max_val=NE ** 4 - 1)
                    known[g] = [four % NE, four // NE % NE, four // NE ** 2 % NE, four // NE ** 3]

            def experts_of(v):
                return known[v // 2][v % 2 * 2:v % 2 * 2 + 2]

            def expert_steps(q, u, i):
                if u == 0:
                    known.clear()
                if block_live(q, 1):
                    load_experts((u - 1) // 2, i)
                if block_live(q, 0):
                    pe.wait_ge(block_in[u], i * 32 + 32)
                    wait(pe, "t_ok", q - 1)
                    for t in range(2):
                        for h in range(2):
                            at = (2 * t + h) * P
                            last = nc.tensor.transpose(t_bank[u % 2][:, at:at + P], rows16[:, u, t, h * P:(h + 1) * P], ident16[:, :])
                    last.then_inc(s["t_mm"], 1)
                if block_live(q, 1):
                    wait(pe, "t_ok", q)
                    wait(pe, "up_ok", q - 2)
                    b = (u + 1) % 2
                    for t, e in enumerate(experts_of(u - 1)):
                        last = plus_bias(gu_bank[b][:, t * 256:(t + 1) * 256], bT[:, b, t, HI, :], bT[:, b, t, LO, :],
                                         w_gu[:, HI, e, :], w_gu[:, LO, e, :], bias_gu[:, e, :])
                    last.then_inc(s["gu_mm"], 1)
                if block_live(q, 0) and u + 1 < NBUF:
                    load_experts(u // 2, i)
                if block_live(q, 4):
                    load_experts((u - 4) // 2, i)
                if block_live(q, 3):
                    wait(pe, "h_ok", q - 2)
                    wait(pe, "ht_lo", q - 4)
                    for t in range(2):
                        last = nc.tensor.transpose(ht_bank[(u + 1) % 2][:, t * P:(t + 1) * P], hidden[:, (u + 1) % 2, t, :], ident[:, :])
                    last.then_inc(s["ht_mm"], 1)
                if block_live(q, 4):
                    wait(pe, "ht_lo", q - 3)
                    wait(pe, "z_ok", q * 2 - 10)
                    b = u % 2
                    for t, e in enumerate(experts_of(u - 4)):
                        last = plus_bias(d_bank[b][:, t * P:(t + 1) * P], hT[:, b, HI, t * P:(t + 1) * P], hT[:, b, LO, t * P:(t + 1) * P],
                                         w_d[:, HI, e, :], w_d[:, LO, e, :], bias_d[:, e, :])
                    last.then_inc(s["d_mm"], 1)

            over_blocks(pe, expert_steps)


_INS = ["x", "ctx_1024", "L0_xattn_W_qkv", "L0_xattn_W_out", "L0_xattn_b_out", "L0_ffn_Wg", "L0_ffn_bg",
        "L0_ffn_Wgu", "L0_ffn_bgu", "L0_ffn_Wd", "L0_ffn_bd"]


def kernel(**inputs):
    import numpy as _np
    import concourse.bacc as _bacc
    from concourse import mybir as _mybir
    from concourse.bass_utils import run_bass_kernel_spmd as _run

    nc = _bacc.Bacc("TRN2", target_bir_lowering=False, num_devices=1)
    arrays, args = {}, []
    for name in _INS:
        a = _np.ascontiguousarray(inputs[name])
        arrays[f"in_{name}_dram"] = a
        args.append(nc.dram_tensor(f"in_{name}_dram", a.shape, _mybir.dt.from_np(a.dtype), kind="ExternalInput").ap())
    shape = inputs["x"].shape
    args.append(nc.dram_tensor("out_0_dram", shape, _mybir.dt.float32, kind="ExternalOutput").ap())
    xattn_moe_kernel(nc, *args)
    r = _run(nc, [arrays], core_ids=[0])
    return r.results[0]["out_0_dram"]
```

```python
from contextlib import ExitStack

import concourse.bass as bass
from concourse import mybir

F32 = mybir.dt.float32
F16 = mybir.dt.float16
I32 = mybir.dt.int32
U32 = mybir.dt.uint32
ALU = mybir.AluOpType
ACT = mybir.ActivationFunctionType
AX = mybir.AxisListType

P = 128
HI, LO = 0, 1
TOP = 16.0
TINY = 1e-30
EPS = 1e-5
ALPHA = 1.702
LIMIT = 7.0
NOWHERE = 1 << 20


def xattn_moe_kernel(nc, x, ctx, W_qkv, W_out, b_out, Wg, bg, Wgu, bgu, Wd, bd, out):
    NB, S, D = x.shape
    INNER = W_out.shape[0]
    NE = Wg.shape[0]
    DH = 64
    NH = INNER // DH
    PAIRS = NB // 2
    QUADS = NH // 4
    STEPS = 2 * QUADS
    ALLQ = PAIRS * STEPS
    TOK = NB * S
    ROOM = TOK + P
    ROW = P + 2
    BLOCKS = 2 * TOK // P + NE
    BPAIRS = BLOCKS // 2
    NBUF = 12
    NZ = 6
    VW = DH + 2
    assert S == P and D == P and NE == 16 and STEPS == 8 and BLOCKS == 80

    places = nc.dram_tensor("places", [NE * ROOM + P, ROW], F32, kind="Internal").ap()
    results = nc.dram_tensor("results", [2 * TOK, D], F32, kind="Internal").ap()

    bias_gu_rows = nc.dram_tensor("bias_gu_rows", [2, 2, NE * P], F16, kind="Internal").ap()
    bias_d_rows = nc.dram_tensor("bias_d_rows", [2, NE * P], F16, kind="Internal").ap()

    es = ExitStack()
    with es:
        def sb(name, shape, dt=F32):
            return es.enter_context(nc.sbuf_tensor(name, shape, dt))

        def sem(name):
            return es.enter_context(nc.semaphore(name))

        banks = [es.enter_context(nc.psum_tensor(f"bank{i}", [P, 512], F32)) for i in range(8)]
        score_bank = banks[0:2]
        pt_bank, o_bank, qk_bank, misc_bank, ot_bank, out_bank = banks[2:8]

        first_bank = (qk_bank, pt_bank)
        first_v_bank = (misc_bank, o_bank)

        x_sb = sb("x_sb", [P, NB, D])
        ctx_sb = sb("ctx_sb", [P, NB, D])
        stage = sb("stage", [P, 4096])
        w_qkv = sb("w_qkv", [P, 2, 3 * INNER], F16)
        w_out = sb("w_out", [P, 2, 8, D], F16)
        w_gu = sb("w_gu", [P, 2, NE, 256], F16)
        w_d = sb("w_d", [P, 2, NE, D], F16)
        bias_gu = sb("bias_gu", [2, NE, 256], F16)
        bias_d = sb("bias_d", [2, NE, D], F16)
        bgu_sb = sb("bgu_sb", [P, 32])
        bd_sb = sb("bd_sb", [P, 16])
        bgu_half = sb("bgu_half", [P, 2, 2, 16], F16)
        bd_half = sb("bd_half", [P, 2, 16], F16)
        bout_bc = sb("bout_bc", [P, D])
        bg_bc = sb("bg_bc", [P, NE])
        wg_nat = sb("wg_nat", [NE, D])
        wg_T = sb("wg_T", [P, NE])
        part_largest = sb("part_largest", [P, 11])
        largest = sb("largest", [P, 8])
        top = sb("top", [P, 8])
        scale_to = sb("scale_to", [P, 8])
        scale_from = sb("scale_from", [P, 8])
        fac = sb("fac", [P, 8])
        ident = sb("ident", [P, P])
        ident16 = sb("ident16", [P, P], F16)
        ones16 = sb("ones16", [P, P], F16)
        before16 = sb("before16", [P, P], F16)
        expert_no = sb("expert_no", [P, NE])
        next_place = sb("next_place", [P, 2, NE])
        row_no = sb("row_no", [P, NB, 2], I32)
        minus_half = sb("minus_half", [P, 2])
        part_no = sb("part_no", [P, 1])
        blank = sb("blank", [P, ROW])
        xhat = sb("xhat", [P, 2, 2, D])
        xT = sb("xT", [P, 2, 2, 512], F16)
        stats = sb("stats", [P, 2, 6])
        mv = sb("mv", [P, 2, 2])
        var_eps = sb("var_eps", [P, 2])
        rstd = sb("rstd", [P, 2])
        zeros = sb("zeros", [P, 512])
        qkf = sb("qkf", [P, 2, 512])
        qk = sb("qk", [P, 2, 2, 2, 8, 256], F16)
        v = sb("v", [P, 2, 2, 2, NH, VW], F16)
        qmax = sb("qmax", [P, 2, 4])
        nbias = sb("nbias", [P, 2, 4])
        probs = sb("probs", [P, 2, 4, P])
        pT = sb("pT", [P, 2, 2, 512], F16)
        rsum = sb("rsum", [P, 4])
        o_nat = sb("o_nat", [P, 4, 256])
        oT = sb("oT", [P, 2, 2, 256], F16)
        stats2 = sb("stats2", [P, 2, 6])
        mv2 = sb("mv2", [P, 2, 2])
        var_eps2 = sb("var_eps2", [P, 2])
        rstd2 = sb("rstd2", [P, 2])
        y = sb("y", [P, 2, D])
        yT = sb("yT", [P, 256])
        logits = sb("logits", [P, 2, NE])
        best = sb("best", [P, 2, 8])
        best_at = sb("best_at", [P, 2, 8], U32)
        choice = sb("choice", [P, 4])
        gap = sb("gap", [P, 2])
        egap = sb("egap", [P, 2])
        onehot = sb("onehot", [P, 4, NE])
        chosen16 = sb("chosen16", [P, 2, NE], F16)
        place_all = sb("place_all", [P, 2, NE])
        picked = sb("picked", [P, 4, NE])
        slots = sb("slots", [P, 2, 4], U32)
        denom = sb("denom", [P, 2])
        payload = sb("payload", [P, 2, 2, 2, ROW])
        bT = sb("bT", [P, 2, 2, 2, P], F16)
        gate = sb("gate", [P, 2, 2, P])
        up = sb("up", [P, 2, 2, P])
        sig = sb("sig", [P, 2, 2, P])
        glu = sb("glu", [P, 2, P])
        hidden = sb("hidden", [P, 2, 2, P])
        hT = sb("hT", [P, 2, 2, 256], F16)
        z = sb("z", [P, NZ, 2, P])
        blocks_f = sb("blocks_f", [P, 6, NE])
        blocks_i = sb("blocks_i", [P, NE], I32)
        table_f = sb("table_f", [P, 4])
        GROUPS = (BLOCKS + 2 + 5) // 6
        experts_row = sb("experts_row", [1, 6 * GROUPS])
        packing = sb("packing", [1, GROUPS])
        expert_groups = sb("expert_groups", [1, GROUPS], I32)
        block_starts = sb("block_starts", [1, P // 2], I32)
        first_starts = sb("first_starts", [1, P // 2])
        ends = sb("ends", [1, NE], I32)

        names = """carrier in_small in_wo in_wd in_wgu
        zeroed consts ones_v blank_ok blank_in part_max absmax allmax scales scales2
        w_hi w_lo wo_hi wo_lo d_hi d_lo gu_hi gu_lo bias_half bias_out bias_in wgT_mm wgT_ok setup
        factors stat stat_agg pool_add rstd_ok xhat_ok ctx_ok x_bias prep_mm prep_hi
        qk_mm qk_copied first_high qk_high act_high qk_split v_mm v_hi misc_free
        score_mm qmax_ok nbias_ok exp_ok pt_mm pt_hi pt_lo pv_mm rsum_ok o_ok ot_mm ot_hi ot_lo out_mm
        x1_ok stat2 stat2_agg rstd2_ok y_ok yhalf ylow yT_mm lg_mm rank_mm
        best_ok best_at_ok gap_ok choice_ok onehot_ok chosen_ok egap_ok
        place_ok picked_ok slots_ok denom_ok wgt_ok
        table_cols table_mm table_ok ends_ok cleared pool_cleared
        t_mm t_ok gu_mm gate_ok up_ok sig_ok glu_ok h_ok ht_mm ht_hi ht_lo d_mm z_ok
        sum_ok fin_ok fin_sent""".split()
        s = {n: sem("s_" + n) for n in names}
        block_in = [sem(f"s_block_in{i}") for i in range(NBUF)]
        scattered = [sem(f"s_scattered{i}") for i in range(2)]
        z_sent = [sem(f"s_z_sent{i}") for i in range(NZ)]
        in_w = [sem(f"s_in_w{i}") for i in range(3)]
        in_ctx = [sem(f"s_in_ctx{i}") for i in range(4)]
        in_x = [sem(f"s_in_x{i}") for i in range(2)]
        results_in = [sem(f"s_results_in{i}") for i in range(4)]

        def wait(eng, name, value):
            if not isinstance(value, int) or value > 0:
                eng.wait_ge(s[name], value)

        def wait_alone(eng, name, value):
            wait(eng, name, value)
            if not isinstance(value, int):
                eng.sem_inc(s["carrier"], 1)

        def live(p, r, lag):
            return not isinstance(p, int) or 0 <= p * STEPS + r - lag < ALLQ

        def pair_live(q):
            return not isinstance(q, int) or 0 <= q < PAIRS

        USES = {"YT": -2, "LG": -2, "V0": 1, "V1": 1, "RANK": -2, "PREP": 2, "V2": 1, "V3": 1}
        ORDER = list(USES)

        def misc_before(p, item):
            if not isinstance(p, int):
                return p * len(ORDER) + (misc_before(2, item) - 2 * len(ORDER))
            before = [(pp, it) for pp in range(p) for it in ORDER]
            before += [(p, it) for it in ORDER[:ORDER.index(item)]]
            return 6 + sum(0 <= pp + USES[it] < PAIRS for pp, it in before)

        FIRST, LAST = 2, PAIRS - 2

        ACT_HIGH = (0, 4)

        def qk_item(par, t, half):
            which, blk = (t % 4) // 2, 4 * (t // 4) + 2 * (t % 2)
            return qk[:, par, which, half, blk:blk + 2, :]

        def over_pairs(eng, body):
            for p in range(FIRST):
                body(p, p % 2)
            with eng.Fori(0, (LAST - FIRST) // 2) as i:
                body(i * 2 + FIRST, 0)
                body(i * 2 + FIRST + 1, 1)
            for p in range(LAST, PAIRS + 2):
                body(p, p % 2)

        STAGES = 5

        def block_live(q, lag):
            return not isinstance(q, int) or 0 <= q - lag < BPAIRS

        def over_blocks(eng, body):
            for q in range(NBUF):
                body(q, q, 0)
            with eng.Fori(1, BPAIRS // NBUF) as i:
                for u in range(NBUF):
                    body(i * NBUF + u, u, i)
            for q in range(BPAIRS // NBUF * NBUF, BPAIRS + STAGES):
                body(q, q % NBUF, q // NBUF)

        def wait_sent(eng, q, u, i, lag):
            if not isinstance(q, int) or q >= lag:
                eng.wait_ge(z_sent[(u - lag) % NZ], i * (NBUF // NZ * 32) + 32 * ((u - lag) // NZ + 1))

        halves = payload[:, :, :, :, 0:P].bitcast(F16)
        rows_in = stage[:, 0:NBUF * 2 * ROW].rearrange("p (b t w) -> p b t w", b=NBUF, t=2)
        rows16 = rows_in[:, :, :, 0:P].bitcast(F16)
        t_bank = [banks[0][:, :].bitcast(F16), banks[1][:, :].bitcast(F16)]
        gu_bank, ht_bank, d_bank, table_bank = banks[2:4], banks[4:6], banks[6:8], banks[7]
        r_in = ctx_sb[:, 0:NB, :].rearrange("p (u c b) d -> p u c b d", u=4, c=2)

        gu_stage = stage[:, :].rearrange("p (e f c) -> p c e f", e=NE, c=2)

        def gu_chunk(p, r):
            at = p * STEPS + r - PAIRS * STEPS - 1 if isinstance(p, int) else -1
            return at if 0 <= at < 8 else None

        block = es.enter_context(nc.Block())

        def clear_ends(eng, experts, done="cleared"):
            for e in experts:
                first = eng.value_load(ends[0:1, e:e + 1], min_val=e * ROOM, max_val=e * ROOM + TOK)
                eng.dma_start(places[bass.ds(first, P), :], blank[:, :]).then_inc(s[done], 16)

        @block.sync
        def _(sp):
            for c in range(3):
                third = slice(c * INNER, (c + 1) * INNER)
                sp.dma_start(stage[:, third], W_qkv[:, third]).then_inc(in_w[c], 16)
            sp.dma_start(x_sb[:, 0:4, :], x[0:4].rearrange("b t d -> t b d")).then_inc(in_x[0], 16)
            by_head = W_out.rearrange("(h j i c d) n -> h c j i d n", h=2, j=2, i=2, c=2)
            for h in range(2):
                for c in range(2):
                    for i in range(2):
                        at = 3 * INNER + (2 * h + c) * 256
                        sp.dma_start(stage[64 * i:64 * i + 64, at:at + 256].rearrange("d (j n) -> d j n", j=2),
                                     by_head[h, c, :, i].rearrange("j d n -> d j n")).then_inc(s["in_wo"], 16)
            sp.dma_start(x_sb[:, 4:NB, :], x[4:NB].rearrange("b t d -> t b d")).then_inc(in_x[1], 16)
            sp.wait_ge(s["w_lo"], 3)
            sp.dma_start(stage[:, 0:NE * D].rearrange("f (e n) -> f e n", e=NE),
                         Wd.rearrange("e f n -> f e n")).then_inc(s["in_wd"], 16)
            sp.wait_ge(s["wo_lo"], 1)
            sp.wait_ge(s["d_lo"], 1)
            sp.dma_start(stage[:, :].rearrange("h (e n) -> h e n", e=NE),
                         Wgu.rearrange("e h n -> h e n")).then_inc(s["in_wgu"], 16)
            sp.wait_ge(s["bias_half"], 3)
            for half in range(2):
                for c in range(2):
                    sp.dma_start(bias_gu_rows[half, c].rearrange("(k f) -> k f", f=16),
                                 bgu_half[:, half, c, :]).then_inc(s["bias_out"], 16)
                sp.dma_start(bias_d_rows[half].rearrange("(k f) -> k f", f=16), bd_half[:, half, :]).then_inc(s["bias_out"], 16)
            sp.wait_ge(s["bias_out"], 16 * 6)
            for half in range(2):
                sp.dma_start(bias_gu[half:half + 1].rearrange("o e (c f) -> o e c f", c=2),
                             bias_gu_rows[half:half + 1].rearrange("o c (e f) -> o e c f", e=NE)).then_inc(s["bias_in"], 16)
                sp.dma_start(bias_d[half:half + 1].rearrange("o e f -> o (e f)"), bias_d_rows[half:half + 1]).then_inc(s["bias_in"], 16)
            sp.wait_ge(s["blank_ok"], 2)
            sp.dma_start(places[NE * ROOM:NE * ROOM + P, :], blank[:, :]).then_inc(s["blank_in"], 16)

            sp.wait_ge(s["ends_ok"], 1)
            clear_ends(sp, range(0, 7))
            for par in range(2):
                sp.wait_ge(scattered[par], 64 * (PAIRS // 2))
            sp.wait_ge(s["cleared"], 16 * 13)
            sp.wait_ge(s["pool_cleared"], 16 * 3)
            sp.wait_ge(s["blank_in"], 16)
            sp.wait_ge(s["gu_lo"], 8)
            sp.wait_ge(s["table_ok"], 1)

            def load(q, u, i):
                if block_live(q, 0):
                    both = sp.value_load(block_starts[0:1, bass.ds(q, 1)], min_val=0, max_val=1024 * 1024 - 1)
                    wait_sent(sp, q, u, i, NBUF)
                    for t, at in enumerate((both % 1024, both // 1024)):
                        place = nc.s_assert_within(at, 0, NE * ROOM // P, skip_runtime_bounds_check_because="the table holds no other") * P
                        sp.dma_start(rows_in[:, u, t, :], places[bass.ds(place, P), :]).then_inc(block_in[u], 16)

            over_blocks(sp, load)

            for k in range(NZ):
                sp.wait_ge(z_sent[k], 32 * len(range(k, BPAIRS, NZ)))
            res = results.rearrange("(c b p) d -> c p b d", c=2, p=P)
            for g in range(NB // 4):
                if g >= 4:
                    sp.wait_ge(s["fin_ok"], g - 3)
                for c in range(2):
                    sp.dma_start(r_in[:, g % 4, c], res[c, :, 4 * g:4 * g + 4]).then_inc(results_in[g % 4], 16)

        @block.scalar
        def _(act):
            for c in range(4):
                act.dma_start(ctx_sb[:, 8 * c:8 * c + 8, :], ctx[8 * c:8 * c + 8].rearrange("b t d -> t b d")).then_inc(in_ctx[c], 16)
            act.dma_start(bout_bc[:, :], b_out.rearrange("(o d) -> o d", o=1).broadcast_to([P, D])).then_inc(s["in_small"], 16)
            act.dma_start(bg_bc[:, :], bg.rearrange("(o d) -> o d", o=1).broadcast_to([P, NE])).then_inc(s["in_small"], 16)
            act.dma_start(wg_nat[:, :], Wg).then_inc(s["in_small"], 16)
            act.dma_start(bgu_sb[:, :], bgu.rearrange("e (k f) -> (e k) f", k=8)).then_inc(s["in_small"], 16)
            act.dma_start(bd_sb[:, :], bd.rearrange("e (k f) -> (e k) f", k=8)).then_inc(s["in_small"], 16)
            def scale_ctx(q):
                wait(act, "prep_mm", q)
                nc.scalar.activation(xhat[:, 1, :, :], ctx_sb[:, bass.ds(q * 2, 2), :], ACT.Copy,
                                     scale=scale_to[:, 1:2]).then_inc(s["ctx_ok"], 1)

            act.wait_ge(s["scales"], 1)
            scale_ctx(0)
            for c in range(3):
                third = slice(c * INNER, (c + 1) * INNER)
                nc.scalar.activation(w_qkv[:, HI, third], stage[:, third], ACT.Copy, scale=scale_to[:, 0:1]).then_inc(s["w_hi"], 1)
                if c == 0:
                    act.wait_ge(s["prep_mm"], 1)
                    nc.scalar.activation(xT[:, 0, HI, :], misc_bank[:, :], ACT.Copy).then_inc(s["prep_hi"], 1)
                    scale_ctx(1)

            def copy_qk(q, par, t):
                wait(act, "qk_mm", q * 8 + t + 1)
                wait(act, "qk_split", q * 8 + t - 1)
                if t in ACT_HIGH:
                    nc.scalar.activation(qk_item(par, t, HI).rearrange("p i n -> p (i n)"), qk_bank[:, :],
                                         ACT.Copy).then_inc(s["act_high"], 1)
                nc.scalar.activation(qkf[:, t % 2, :], qk_bank[:, :], ACT.Copy).then_inc(s["qk_copied"], 1)

            def v_high(q, par, k, bank=misc_bank):
                wait(act, "v_mm", q * 4 + k + 1)
                wait(act, "pv_mm", q * 8 - 12 + 4 * (k // 2))
                nc.scalar.activation(v[:, par, HI, k // 2, 8 * (k % 2):8 * (k % 2) + 8, 0:DH],
                                     bank[:, :].rearrange("p (h d) -> p h d", h=8), ACT.Copy).then_inc(s["v_hi"], 1)

            for t in range(8):
                act.wait_ge(s["qk_mm"], t + 1)
                nc.scalar.activation(qk_item(0, t, HI).rearrange("p i n -> p (i n)"), first_bank[t % 2][:, :],
                                     ACT.Copy).then_inc(s["first_high"], 1)
                if t >= 4:
                    v_high(0, 0, t - 4, first_v_bank[t % 2])
                if t == 5:
                    act.wait_ge(s["prep_mm"], 2)
                    nc.scalar.activation(xT[:, 1, HI, :], ot_bank[:, :], ACT.Copy).then_inc(s["prep_hi"], 1)

            exp_scale, bias_scale = act.alloc_register("exp_scale"), act.alloc_register("bias_scale")
            act.wait_ge(s["factors"], 1)
            act.reg_load(exp_scale, fac[0:1, 0:1].bitcast(I32))
            act.reg_load(bias_scale, fac[0:1, 2:3].bitcast(I32))

            def weights_high(p, r):
                if (p, r) == (0, 2):
                    act.wait_ge(s["scales"], 2)
                    nc.scalar.activation(w_out[:, HI].rearrange("p b n -> p (b n)"), stage[:, 3 * INNER:4096], ACT.Copy,
                                         scale=scale_to[:, 2:3]).then_inc(s["wo_hi"], 1)
                if (p, r) == (0, 6):
                    act.wait_ge(s["scales2"], 1)
                    act.wait_ge(s["in_wd"], 16)
                    nc.scalar.activation(w_d[:, HI, :, :].rearrange("p e n -> p (e n)"), stage[:, 0:NE * D], ACT.Copy,
                                         scale=scale_to[:, 3:4]).then_inc(s["d_hi"], 1)
                k = gu_chunk(p, r)
                if k is not None:
                    act.wait_ge(s["scales2"], 2)
                    e4, half = slice(4 * (k % 4), 4 * (k % 4) + 4), k // 4
                    nc.scalar.activation(w_gu[:, HI, e4, half * P:(half + 1) * P], gu_stage[:, half, e4], ACT.Copy,
                                         scale=scale_to[:, 5:6]).then_inc(s["gu_hi"], 1)

            def steps(p, par):
                for r in range(STEPS):
                    n = p * STEPS + r
                    if live(p, r, 6):
                        wait(act, "ot_mm", n - 5)
                        wait(act, "out_mm", n - 7)
                        nc.scalar.activation(oT[:, r % 2, HI, :], ot_bank[:, 0:256], ACT.Copy).then_inc(s["ot_hi"], 1)
                    if live(p, r, 1):
                        b = (r + 1) % 2
                        wait(act, "qmax_ok", n)
                        nc.scalar.activation(nbias[:, b, :], qmax[:, b, :], ACT.Copy, scale=bias_scale).then_inc(s["nbias_ok"], 1)
                        wait(act, "nbias_ok", n)
                        wait(act, "pt_mm", n - 2)
                        for k in range(4):
                            last = nc.scalar.activation(probs[:, b, k, :], score_bank[b][:, k * P:(k + 1) * P],
                                                        ACT.Exp, bias=nbias[:, b, k:k + 1], scale=exp_scale)
                        last.then_inc(s["exp_ok"], 1)
                    if r == 4 and pair_live(p - 2):
                        wait(act, "gap_ok", p - 1)
                        nc.scalar.activation(egap[:, :], gap[:, :], ACT.Exp).then_inc(s["egap_ok"], 1)
                    if live(p, r, 2):
                        wait(act, "pt_mm", n - 1)
                        wait(act, "pv_mm", n - 3)
                        nc.scalar.activation(pT[:, r % 2, HI, :], pt_bank[:, :], ACT.Copy).then_inc(s["pt_hi"], 1)
                    if pair_live(p + 1):
                        copy_qk(p + 1, 1 - par, r)
                    if ORDER[r][0] == "V" and pair_live(p + 1):
                        v_high(p + 1, 1 - par, int(ORDER[r][1]))
                    if r == 2 and pair_live(p + 2):
                        scale_ctx(p + 2)
                    if ORDER[r] == "PREP" and pair_live(p + 2):
                        wait(act, "prep_mm", p + 3)
                        nc.scalar.activation(xT[:, par, HI, :], misc_bank[:, :], ACT.Copy).then_inc(s["prep_hi"], 1)
                    if ORDER[r] == "YT" and pair_live(p - 2):
                        wait(act, "yT_mm", p - 1)
                        nc.scalar.activation(yT[:, :], misc_bank[:, 0:256], ACT.Copy).then_inc(s["misc_free"], 1)
                    if isinstance(p, int):
                        weights_high(p, r)

            over_pairs(act, steps)
            act.wait_ge(s["ends_ok"], 1)
            act.wait_ge(s["blank_ok"], 2)
            clear_ends(act, range(7, 13))

            def expert_steps(q, u, i):
                if block_live(q, 5):
                    wait(act, "d_mm", q - 4)
                    wait_sent(act, q, u, i, 5 + NZ)
                    for t in range(2):
                        nc.scalar.activation(z[:, (u - 5) % NZ, t, :], d_bank[(u + 1) % 2][:, t * P:(t + 1) * P], ACT.Copy,
                                             scale=rows_in[:, (u + NBUF - 5) % NBUF, t, P:P + 1]).then_inc(s["z_ok"], 1)
                if block_live(q, 0):
                    wait(act, "t_mm", q + 1)
                    wait(act, "gu_mm", q - 1)
                    nc.scalar.activation(bT[:, u % 2].rearrange("p a b c -> p (a b c)"), t_bank[u % 2][:, 0:512],
                                         ACT.Copy).then_inc(s["t_ok"], 1)
                if block_live(q, 3):
                    wait(act, "ht_mm", q - 2)
                    wait(act, "d_mm", q - 4)
                    nc.scalar.activation(hT[:, (u + 1) % 2, HI, :], ht_bank[(u + 1) % 2][:, 0:256], ACT.Copy).then_inc(s["ht_hi"], 1)
                if block_live(q, 1):
                    wait(act, "gate_ok", q)
                    wait(act, "glu_ok", q - 2)
                    nc.scalar.activation(sig[:, (u + 1) % 2], gate[:, (u + 1) % 2], ACT.Sigmoid, scale=ALPHA).then_inc(s["sig_ok"], 1)

            over_blocks(act, expert_steps)
            for g in range(NB // 4):
                act.wait_ge(s["fin_ok"], g + 1)
                act.dma_start(out[4 * g:4 * g + 4].rearrange("b t d -> t b d"), x_sb[:, 4 * g:4 * g + 4, :]).then_inc(s["fin_sent"], 16)
            act.wait_ge(s["fin_sent"], 16 * (NB // 4))

        @block.gpsimd
        def _(pool):
            nc.gpsimd.memset(ident[:, :], 0.0).then_inc(s["zeroed"], 1)
            nc.gpsimd.memset(ident16[:, :], 0.0).then_inc(s["zeroed"], 1)
            nc.gpsimd.memset(ones16[:, :], 1.0).then_inc(s["zeroed"], 1)
            nc.gpsimd.memset(minus_half[:, :], -0.5).then_inc(s["zeroed"], 1)
            nc.gpsimd.memset(zeros[:, :], 0.0).then_inc(s["zeroed"], 1)
            pool.wait_ge(s["zeroed"], 5)
            for t in (ident, ident16):
                nc.gpsimd.affine_select(out=t[:, :], in_=t[:, :], compare_op=ALU.not_equal, fill=1.0, base=0,
                                        pattern=[[-1, P]], channel_multiplier=1).then_inc(s["consts"], 1)
            nc.gpsimd.affine_select(out=before16[:, :], in_=ones16[:, :], compare_op=ALU.is_gt, fill=0.0, base=0,
                                    pattern=[[1, P]], channel_multiplier=-1).then_inc(s["consts"], 1)
            nc.gpsimd.memset(v[:, :, HI, :, :, DH:VW], 1.0).then_inc(s["ones_v"], 1)
            nc.gpsimd.memset(v[:, :, LO, :, :, DH:VW], 0.0).then_inc(s["ones_v"], 1)

            def inverse_root(ready, count, mean_var, ve, rs, done, adds):
                wait_alone(pool, ready, count)
                nc.gpsimd.tensor_scalar(ve[:, :], mean_var[:, :, 1], EPS, None, ALU.add).then_inc(s["pool_add"], 1)
                wait(pool, "pool_add", adds)
                nc.gpsimd.tensor_tensor(rs[:, :], ve[:, :], minus_half[:, :], ALU.pow).then_inc(s[done], 1)

            def add_b_out(q):
                wait(pool, "xhat_ok", q * 2 + 2)
                for j in range(2):
                    nc.gpsimd.tensor_tensor(x_sb[:, q * 2 + j, :], x_sb[:, q * 2 + j, :], bout_bc[:, :],
                                            ALU.add).then_inc(s["x_bias"], 1)

            def all_largest(a, b, count):
                pool.wait_ge(s["absmax"], count)
                nc.gpsimd.partition_all_reduce(top[:, a:b], largest[:, a:b], P, bass.bass_isa.ReduceOp.max).then_inc(s["allmax"], 1)

            inverse_root("stat_agg", 2, mv, var_eps, rstd, "rstd_ok", 1)
            all_largest(0, 2, 2)
            nc.gpsimd.iota(expert_no[:, :], pattern=[[1, NE]], base=0, channel_multiplier=0,
                           allow_small_or_imprecise_dtypes=True).then_inc(s["consts"], 1)
            nc.gpsimd.iota(next_place[:, 0, :], pattern=[[ROOM, NE]], base=0, channel_multiplier=0,
                           allow_small_or_imprecise_dtypes=True).then_inc(s["consts"], 1)
            nc.gpsimd.iota(row_no[:, :, :], pattern=[[P, NB], [TOK, 2]], base=0, channel_multiplier=1).then_inc(s["consts"], 1)
            nc.gpsimd.iota(part_no[:, :], pattern=[[0, 1]], base=0, channel_multiplier=1,
                           allow_small_or_imprecise_dtypes=True).then_inc(s["consts"], 1)
            nc.gpsimd.memset(blank[:, 0:P + 1], 0.0).then_inc(s["blank_ok"], 1)
            nc.gpsimd.memset(blank[:, P + 1:ROW].bitcast(I32), NOWHERE).then_inc(s["blank_ok"], 1)

            def split_qk(q, par, t):
                src = qkf[:, t % 2, :].rearrange("p (i n) -> p i n", i=2)
                wait(pool, "qk_copied", q * 8 + t - 7)
                if t in ACT_HIGH:
                    wait(pool, "act_high", q * len(ACT_HIGH) + (ACT_HIGH.index(t) + 1 - len(ACT_HIGH)))
                else:
                    of_pool = [k for k in range(8) if k not in ACT_HIGH]
                    if t == 0:
                        wait(pool, "score_mm", q * 8 - 8)
                    nc.gpsimd.tensor_tensor(qk_item(par, t, HI), src, zeros[:, :].rearrange("p (i n) -> p i n", i=2),
                                            ALU.add).then_inc(s["qk_high"], 1)
                    wait(pool, "qk_high", q * len(of_pool) + (of_pool.index(t) + 1 - len(of_pool)))
                nc.gpsimd.tensor_tensor(qk_item(par, t, LO), src, qk_item(par, t, HI), ALU.subtract).then_inc(s["qk_split"], 1)

            inverse_root("stat_agg", 4, mv, var_eps, rstd, "rstd_ok", 2)
            pool.wait_ge(s["in_small"], 16 * 5)
            add_b_out(0)
            add_b_out(1)

            def adds_before(p):
                if isinstance(p, int):
                    return 2 + sum((pp + 2 < PAIRS) + (0 <= pp - 1 < PAIRS) for pp in range(p))
                return p * 2 + (adds_before(2) - 4)

            def steps(p, par):
                adds = adds_before(p)
                for r in range(STEPS):
                    if isinstance(p, int) and (p, r) == (0, 1):
                        all_largest(2, 3, 3)
                    if isinstance(p, int) and (p, r) == (0, 4):
                        all_largest(3, 5, 5)
                    if isinstance(p, int) and (p, r) == (1, 7):
                        all_largest(5, 7, 7)
                    if pair_live(p + 1):
                        split_qk(p + 1, 1 - par, r)
                    if r == 0 and pair_live(p + 2):
                        adds = adds + 1
                        inverse_root("stat_agg", p * 2 + 6, mv, var_eps, rstd, "rstd_ok", adds)
                    if r == 2 and pair_live(p + 2):
                        add_b_out(p + 2)
                    if r == 6 and pair_live(p - 1):
                        adds = adds + 1
                        inverse_root("stat2_agg", p * 2, mv2, var_eps2, rstd2, "rstd2_ok", adds)
                    if r == 7 and pair_live(p - 1):
                        for j in range(2):
                            wait(pool, "yhalf", p * 2 - 1 + j)
                            nc.gpsimd.tensor_tensor(halves[:, 1 - par, j, :, P:2 * P], y[:, j, :].unsqueeze(1).to_broadcast([P, 2, P]),
                                                    halves[:, 1 - par, j, :, 0:P], ALU.subtract).then_inc(s["ylow"], 1)
                    if r == 6 and pair_live(p - 2):
                        wait(pool, "slots_ok", p - 1)
                        wait(pool, "wgt_ok", p * 3 - 3)
                        wait_alone(pool, "ylow", p * 2 - 2)
                        for j in range(2):
                            for c in range(2):
                                nc.gpsimd.indirect_dma_start(
                                    out=places, out_offset=bass.IndirectOffsetOnAxis(ap=slots[:, par, 2 * j + c:2 * j + c + 1], axis=0),
                                    in_=payload[:, par, j, c, :], in_offset=None).then_inc(scattered[par], 16)

            over_pairs(pool, steps)
            pool.wait_ge(s["ends_ok"], 1)
            clear_ends(pool, range(13, NE), "pool_cleared")

            def send(q, u, i):
                if block_live(q, 5):
                    for t in range(2):
                        wait_alone(pool, "z_ok", q * 2 - 9 + t)
                        to = rows_in[:, (u + NBUF - 5) % NBUF, t, P + 1:ROW].bitcast(U32)
                        nc.gpsimd.indirect_dma_start(
                            out=results, out_offset=bass.IndirectOffsetOnAxis(ap=to, axis=0),
                            in_=z[:, (u - 5) % NZ, t, :], in_offset=None,
                            bounds_check=2 * TOK - 1, oob_is_err=False).then_inc(z_sent[(u - 5) % NZ], 16)

            over_blocks(pool, send)

        @block.vector
        def _(dve):
            count = [0]

            def link(ins):
                count[0] += 1
                ins.then_inc(s["setup"], 1)
                dve.wait_ge(s["setup"], count[0])

            def magnitude(col, ap):
                nc.vector.tensor_reduce(largest[:, col:col + 1], ap, AX.X, ALU.max,
                                        apply_absolute_value=True).then_inc(s["absmax"], 1)

            parts = [0]

            def part_magnitude(ap):
                nc.vector.tensor_reduce(part_largest[:, parts[0]:parts[0] + 1], ap, AX.X, ALU.max,
                                        apply_absolute_value=True).then_inc(s["part_max"], 1)
                parts[0] += 1

            def make_scales(a, b, name):
                link(nc.vector.tensor_scalar(top[:, a:b], top[:, a:b], TINY, 1.0 / TOP, ALU.max, ALU.mult))
                link(nc.vector.tensor_copy(scale_from[:, a:b], top[:, a:b]))
                nc.vector.reciprocal(scale_to[:, a:b], scale_from[:, a:b]).then_inc(s[name], 1)

            def prep_stats(q):
                wait_alone(dve, "xhat_ok", q * 2)
                for j in range(2):
                    nc.vector.bn_stats(stats[:, j, :], x_sb[:, q * 2 + j, :]).then_inc(s["stat"], 1)
                for j in range(2):
                    wait_alone(dve, "stat", q * 2 + j + 1)
                    nc.vector.bn_aggr(mv[:, j, :], stats[:, j, :]).then_inc(s["stat_agg"], 1)

            def prep_rows(q):
                wait(dve, "rstd_ok", q + 1)
                wait(dve, "prep_mm", q)
                for j in range(2):
                    nc.vector.tensor_scalar(xhat[:, 0, j, :], x_sb[:, q * 2 + j, :], mv[:, j, 0:1], rstd[:, j:j + 1],
                                            ALU.subtract, ALU.mult).then_inc(s["xhat_ok"], 1)

            def prep_low(q, par, bank=misc_bank):
                wait(dve, "prep_hi", q + 1)
                nc.vector.tensor_tensor(xT[:, par, LO, :], bank[:, :], xT[:, par, HI, :], ALU.subtract).then_inc(s["misc_free"], 1)

            def v_low(q, par, k, bank=misc_bank):
                wait(dve, "v_hi", q * 4 + k + 1)
                heads = slice(8 * (k % 2), 8 * (k % 2) + 8)
                nc.vector.tensor_tensor(v[:, par, LO, k // 2, heads, 0:DH], bank[:, :].rearrange("p (h d) -> p h d", h=8),
                                        v[:, par, HI, k // 2, heads, 0:DH], ALU.subtract).then_inc(s["misc_free"], 1)

            for c in range(3):
                dve.wait_ge(in_w[c], 16)
                part_magnitude(stage[:, c * INNER:(c + 1) * INNER])
            dve.wait_ge(in_x[0], 16)
            prep_stats(0)
            for c in range(4):
                dve.wait_ge(in_ctx[c], 16)
                part_magnitude(ctx_sb[:, 8 * c:8 * c + 8, :].rearrange("p b d -> p (b d)"))
            dve.wait_ge(s["part_max"], 7)
            magnitude(0, part_largest[:, 0:3])
            magnitude(1, part_largest[:, 3:7])
            dve.wait_ge(s["allmax"], 1)
            make_scales(0, 2, "scales")
            dve.wait_ge(s["scales"], 1)
            prep_rows(0)

            def qkv_low(c):
                third = slice(c * INNER, (c + 1) * INNER)
                dve.wait_ge(s["w_hi"], c + 1)
                nc.vector.scalar_tensor_tensor(out=w_qkv[:, LO, third], in0=stage[:, third], scalar=scale_to[:, 0:1],
                                               in1=w_qkv[:, HI, third], op0=ALU.mult, op1=ALU.subtract).then_inc(s["w_lo"], 1)

            def first_low(t):
                dve.wait_ge(s["first_high"], t + 1)
                nc.vector.tensor_tensor(qk_item(0, t, LO), first_bank[t % 2][:, :].rearrange("p (i n) -> p i n", i=2),
                                        qk_item(0, t, HI), ALU.subtract).then_inc(s["qk_split"], 1)

            qkv_low(0)
            prep_low(0, 0)
            qkv_low(1)
            first_low(0)
            qkv_low(2)
            first_low(1)
            prep_stats(1)
            first_low(2)
            first_low(3)
            prep_rows(1)
            link(nc.vector.tensor_tensor(fac[:, 1:2], scale_from[:, 0:1], scale_from[:, 1:2], ALU.mult))
            for t in range(4, 8):
                first_low(t)
                if t == 4:
                    link(nc.vector.tensor_tensor(fac[:, 4:5], fac[:, 1:2], scale_from[:, 0:1], ALU.mult))
                    link(nc.vector.tensor_scalar(fac[:, 0:1], fac[:, 4:5], DH ** -0.5, None, ALU.mult))
                    nc.vector.tensor_scalar(fac[:, 2:3], fac[:, 4:5], -DH ** -0.5, None, ALU.mult).then_inc(s["factors"], 1)
                v_low(0, 0, t - 4, first_v_bank[t % 2])
                if t == 5:
                    prep_low(1, 1, ot_bank)
            def with_bias(a, b):
                dve.wait_ge(s["allmax"], 3 if a == 3 else 4)
                link(nc.vector.tensor_tensor(top[:, a:a + 1], top[:, a:a + 1], top[:, b:b + 1], ALU.max))
                make_scales(a, a + 1, "scales2")
                dve.wait_ge(s["scales2"], 1 if a == 3 else 2)

            def split(hi, lo, src, scale):
                link(nc.vector.tensor_scalar(hi, src, scale, None, ALU.mult))
                nc.vector.scalar_tensor_tensor(out=lo, in0=src, scalar=scale, in1=hi,
                                               op0=ALU.mult, op1=ALU.subtract).then_inc(s["bias_half"], 1)

            dve.wait_ge(s["in_small"], 16 * 5)
            b_up = bgu_sb[:, :].rearrange("p (f c) -> p f c", c=2)[:, :, 1]
            link(nc.vector.tensor_scalar(b_up, b_up, 1.0, None, ALU.add))
            dve.wait_ge(s["wgT_mm"], 1)
            nc.vector.tensor_copy(wg_T[:, :], out_bank[:, 0:NE]).then_inc(s["wgT_ok"], 1)

            def weights_low(p, r):
                if (p, r) == (0, 0):
                    dve.wait_ge(s["in_wo"], 16 * 8)
                    magnitude(2, stage[:, 3 * INNER:4096])
                if (p, r) == (0, 1):
                    dve.wait_ge(s["allmax"], 2)
                    make_scales(2, 3, "scales")
                    dve.wait_ge(s["scales"], 2)
                    link(nc.vector.tensor_tensor(fac[:, 3:4], fac[:, 1:2], scale_from[:, 2:3], ALU.mult))
                if (p, r) == (0, 2):
                    dve.wait_ge(s["wo_hi"], 1)
                    nc.vector.scalar_tensor_tensor(out=w_out[:, LO].rearrange("p b n -> p (b n)"), in0=stage[:, 3 * INNER:4096],
                                                   scalar=scale_to[:, 2:3], in1=w_out[:, HI].rearrange("p b n -> p (b n)"),
                                                   op0=ALU.mult, op1=ALU.subtract).then_inc(s["wo_lo"], 1)
                if (p, r) == (0, 3):
                    dve.wait_ge(s["in_wd"], 16)
                    magnitude(3, stage[:, 0:NE * D])
                    magnitude(4, bd_sb[:, :])
                if (p, r) == (0, 5):
                    with_bias(3, 4)
                    split(bd_half[:, HI, :], bd_half[:, LO, :], bd_sb[:, :], scale_to[:, 3:4])
                if (p, r) == (0, 7):
                    dve.wait_ge(s["d_hi"], 1)
                    nc.vector.scalar_tensor_tensor(out=w_d[:, LO].rearrange("p e n -> p (e n)"), in0=stage[:, 0:NE * D],
                                                   scalar=scale_to[:, 3:4], in1=w_d[:, HI].rearrange("p e n -> p (e n)"),
                                                   op0=ALU.mult, op1=ALU.subtract).then_inc(s["d_lo"], 1)
                if p == 1 and 2 <= r < 6:
                    dve.wait_ge(s["in_wgu"], 16)
                    part_magnitude(stage[:, (r - 2) * 1024:(r - 1) * 1024])
                if (p, r) == (1, 6):
                    dve.wait_ge(s["part_max"], 11)
                    magnitude(5, part_largest[:, 7:11])
                    magnitude(6, bgu_sb[:, :])
                if (p, r) == (LAST, 0):
                    with_bias(5, 6)
                    for c in range(2):
                        split(bgu_half[:, HI, c, :], bgu_half[:, LO, c, :],
                              bgu_sb[:, :].rearrange("p (f c) -> p c f", c=2)[:, c], scale_to[:, 5:6])
                k = gu_chunk(p, r)
                if k is not None:
                    e4, half = slice(4 * (k % 4), 4 * (k % 4) + 4), k // 4
                    dve.wait_ge(s["gu_hi"], k + 1)
                    nc.vector.scalar_tensor_tensor(out=w_gu[:, LO, e4, half * P:(half + 1) * P], in0=gu_stage[:, half, e4],
                                                   scalar=scale_to[:, 5:6], in1=w_gu[:, HI, e4, half * P:(half + 1) * P],
                                                   op0=ALU.mult, op1=ALU.subtract).then_inc(s["gu_lo"], 1)

            def steps(p, par):
                for r in range(STEPS):
                    n = p * STEPS + r
                    if live(p, r, 6):
                        wait(dve, "ot_hi", n - 5)
                        nc.vector.tensor_tensor(oT[:, r % 2, LO, :], ot_bank[:, 0:256], oT[:, r % 2, HI, :],
                                                ALU.subtract).then_inc(s["ot_lo"], 1)
                    if live(p, r, 0):
                        wait(dve, "score_mm", n + 1)
                        nc.vector.tensor_reduce(qmax[:, r % 2, :], score_bank[r % 2][:, :].rearrange("p (h k) -> p h k", h=4),
                                                AX.X, ALU.max).then_inc(s["qmax_ok"], 1)
                    if r in (2, 6) and pair_live(p - 1):
                        j = r // 4
                        wait(dve, "out_mm", p * 8 - 4 + 4 * j)
                        wait(dve, "x_bias", p * 2)
                        row = x_sb[:, p * 2 - 2 + j, :]
                        nc.vector.scalar_tensor_tensor(out=row, in0=out_bank[:, 0:P], scalar=fac[:, 3:4], in1=row,
                                                       op0=ALU.mult, op1=ALU.add).then_inc(s["x1_ok"], 1)
                    if r == 2 and pair_live(p - 2):
                        wait_alone(dve, "misc_free", misc_before(p, "V0"))
                        for j in range(2):
                            nc.vector.max(best[:, j, :], logits[:, j, :]).then_inc(s["best_ok"], 1)
                    if r == 3 and pair_live(p - 2):
                        wait(dve, "best_at_ok", p * 2 - 2)
                        nc.vector.tensor_copy(choice[:, :].rearrange("p (j k) -> p j k", j=2), best_at[:, :, 0:2]).then_inc(s["choice_ok"], 1)
                        nc.vector.tensor_tensor(gap[:, :], best[:, :, 1], best[:, :, 0], ALU.subtract).then_inc(s["gap_ok"], 1)
                    if r == 6 and pair_live(p - 1):
                        for j in range(2):
                            wait_alone(dve, "x1_ok", p * 2 - 1 + j)
                            nc.vector.bn_stats(stats2[:, j, :], x_sb[:, p * 2 - 2 + j, :]).then_inc(s["stat2"], 1)
                    if live(p, r, 2):
                        wait(dve, "pt_hi", n - 1)
                        nc.vector.tensor_tensor(pT[:, r % 2, LO, :], pt_bank[:, :], pT[:, r % 2, HI, :],
                                                ALU.subtract).then_inc(s["pt_lo"], 1)
                    if live(p, r, 3):
                        wait(dve, "pv_mm", n - 2)
                        nc.vector.reciprocal(rsum[:, :], o_bank[:, 0:4 * (DH + 1)].rearrange("p (h w) -> p h w", h=4)[:, :, DH]).then_inc(s["rsum_ok"], 1)
                    if ORDER[r][0] == "V" and pair_live(p + 1):
                        v_low(p + 1, 1 - par, int(ORDER[r][1]))
                    if r == 0 and pair_live(p + 2):
                        if isinstance(p, int) and p == 0:
                            dve.wait_ge(in_x[1], 16)
                        prep_stats(p + 2)
                    if r == 2 and pair_live(p - 2):
                        for j in range(2):
                            wait_alone(dve, "best_ok", p * 2 - 3 + j)
                            nc.vector.max_index(best_at[:, j, :], best[:, j, :], logits[:, j, :]).then_inc(s["best_at_ok"], 1)
                    if r == 3 and pair_live(p - 2):
                        wait(dve, "choice_ok", p - 1)
                        nc.vector.tensor_tensor(onehot[:, :, :], expert_no[:, :].unsqueeze(1).to_broadcast([P, 4, NE]),
                                                choice[:, :].unsqueeze(2).to_broadcast([P, 4, NE]), ALU.is_equal).then_inc(s["onehot_ok"], 1)
                    if r == 5 and pair_live(p - 2):
                        wait(dve, "place_ok", p - 1)
                        for j in range(2):
                            nc.vector.tensor_tensor(picked[:, 2 * j:2 * j + 2, :], onehot[:, 2 * j:2 * j + 2, :],
                                                    place_all[:, j, :].unsqueeze(1).to_broadcast([P, 2, NE]), ALU.mult).then_inc(s["picked_ok"], 1)
                        wait(dve, "egap_ok", p - 1)
                        nc.vector.tensor_scalar(denom[:, :], egap[:, :], 1.0, None, ALU.add).then_inc(s["denom_ok"], 1)
                    if r == 6 and pair_live(p - 1):
                        for j in range(2):
                            wait_alone(dve, "stat2", p * 2 - 1 + j)
                            nc.vector.bn_aggr(mv2[:, j, :], stats2[:, j, :]).then_inc(s["stat2_agg"], 1)
                    if r == 7 and pair_live(p - 1):
                        wait(dve, "rstd2_ok", p)
                        wait(dve, "yT_mm", p - 1)
                        wait(dve, "ylow", p * 2 - 2)
                        for j in range(2):
                            nc.vector.tensor_scalar(y[:, j, :], x_sb[:, p * 2 - 2 + j, :], mv2[:, j, 0:1], rstd2[:, j:j + 1],
                                                    ALU.subtract, ALU.mult).then_inc(s["y_ok"], 1)
                    if live(p, r, 3):
                        wait(dve, "rsum_ok", n - 2)
                        wait(dve, "ot_mm", n - 6)
                        nc.vector.tensor_tensor(o_nat[:, (r - 3) % 4, :].rearrange("p (h d) -> p h d", h=4),
                                                o_bank[:, 0:4 * (DH + 1)].rearrange("p (h w) -> p h w", h=4)[:, :, 0:DH],
                                                rsum[:, :].unsqueeze(2).to_broadcast([P, 4, DH]), ALU.mult).then_inc(s["o_ok"], 1)
                    if ORDER[r] == "RANK" and pair_live(p - 2):
                        wait(dve, "rank_mm", p - 1)
                        now = next_place[:, par, :]
                        nc.vector.tensor_tensor(place_all[:, :, :], misc_bank[:, 0:2 * NE].rearrange("p (j e) -> p j e", j=2),
                                                now.unsqueeze(1).to_broadcast([P, 2, NE]), ALU.add).then_inc(s["place_ok"], 1)
                        nc.vector.tensor_tensor(next_place[:, 1 - par, :], misc_bank[:, 2 * NE:3 * NE], now, ALU.add).then_inc(s["misc_free"], 1)
                    if r == 3 and pair_live(p - 2):
                        wait(dve, "onehot_ok", p - 1)
                        both = onehot[:, :, :].rearrange("p (j k) e -> p j k e", j=2)
                        nc.vector.tensor_tensor(chosen16[:, :, :], both[:, :, 0, :], both[:, :, 1, :], ALU.add).then_inc(s["chosen_ok"], 1)
                    if r == 5 and pair_live(p - 2):
                        wait(dve, "picked_ok", p * 2 - 2)
                        with nc.allow_low_precision(reason="one whole number and zeros, exact"):
                            nc.vector.tensor_reduce(slots[:, par, :], picked[:, :, :], AX.X, ALU.add).then_inc(s["slots_ok"], 1)
                        wait(dve, "denom_ok", p - 1)
                        nc.vector.reciprocal(payload[:, par, :, 0, P], denom[:, :]).then_inc(s["wgt_ok"], 1)
                        nc.vector.tensor_copy(payload[:, par, :, :, P + 1].bitcast(I32), row_no[:, bass.ds(p * 2 - 4, 2), :]).then_inc(s["wgt_ok"], 1)
                        wait(dve, "wgt_ok", p * 3 - 4)
                        nc.vector.tensor_tensor(payload[:, par, :, 1, P], payload[:, par, :, 0, P], egap[:, :], ALU.mult).then_inc(s["wgt_ok"], 1)
                    if r == 7 and pair_live(p - 1):
                        if not isinstance(p, int) or p > 2:
                            dve.wait_ge(scattered[1 - par], (p - 2 + par) * 32)
                        for j in range(2):
                            wait(dve, "y_ok", p * 2 - 1 + j)
                            nc.vector.tensor_copy(halves[:, 1 - par, j, :, 0:P], y[:, j, :].unsqueeze(1).to_broadcast([P, 2, P])).then_inc(s["yhalf"], 1)
                    if r == 2 and pair_live(p + 2):
                        prep_rows(p + 2)
                    if ORDER[r] == "PREP" and pair_live(p + 2):
                        prep_low(p + 2, par)
                    if ORDER[r] == "LG" and pair_live(p - 2):
                        wait(dve, "lg_mm", p - 1)
                        nc.vector.tensor_tensor(logits[:, :, :], misc_bank[:, 0:2 * NE].rearrange("p (j e) -> p j e", j=2),
                                                bg_bc[:, :].unsqueeze(1).to_broadcast([P, 2, NE]), ALU.add).then_inc(s["misc_free"], 1)

                    if isinstance(p, int):
                        weights_low(p, r)

            over_pairs(dve, steps)

            final = next_place[:, PAIRS % 2, :]
            dve.wait_ge(s["misc_free"], misc_before(PAIRS + 2, "V0"))
            counts, blocks, upto, passed, mine, first = (blocks_f[:, k, :] for k in range(6))
            nc.vector.tensor_copy(ends[:, :], final[0:1, :]).then_inc(s["ends_ok"], 1)
            link(nc.vector.scalar_tensor_tensor(out=counts, in0=expert_no[:, :], scalar=-float(ROOM), in1=final, op0=ALU.mult, op1=ALU.add))
            link(nc.vector.tensor_scalar(blocks_i[:, :], counts, float(P - 1), None, ALU.add))
            link(nc.vector.tensor_scalar(blocks_i[:, :], blocks_i[:, :], 7, None, ALU.logical_shift_right))
            link(nc.vector.tensor_copy(blocks, blocks_i[:, :]))
            link(nc.vector.memset(first, 1.0))
            link(nc.vector.tensor_tensor_scan(upto, first, blocks, 0.0, ALU.mult, ALU.add))
            link(nc.vector.tensor_scalar(passed, upto, part_no[:, 0:1], None, ALU.is_le))
            link(nc.vector.tensor_tensor(mine, passed, blocks, ALU.mult))
            link(nc.vector.tensor_reduce(table_f[:, 0:1], passed, AX.X, ALU.add))
            link(nc.vector.tensor_reduce(table_f[:, 2:3], mine, AX.X, ALU.add))
            link(nc.vector.tensor_tensor(table_f[:, 3:4], part_no[:, :], table_f[:, 2:3], ALU.subtract))
            link(nc.vector.scalar_tensor_tensor(out=table_f[:, 1:2], in0=table_f[:, 0:1], scalar=float(ROOM // P), in1=table_f[:, 3:4],
                                                op0=ALU.mult, op1=ALU.add))
            link(nc.vector.tensor_scalar(table_f[:, 1:2], table_f[:, 1:2], float(NE * ROOM // P), None, ALU.min))
            nc.vector.tensor_scalar(table_f[:, 0:1], table_f[:, 0:1], float(NE - 1), None, ALU.min).then_inc(s["table_cols"], 1)
            dve.wait_ge(s["table_mm"], 1)
            starts = table_bank[0:1, P:2 * P].rearrange("o (b t) -> o b t", t=2)
            link(nc.vector.tensor_copy(first_starts[:, :], starts[:, :, 0]))
            nc.vector.scalar_tensor_tensor(out=block_starts[:, :], in0=starts[:, :, 1], scalar=1024.0, in1=first_starts[:, :],
                                           op0=ALU.mult, op1=ALU.add).then_inc(s["table_ok"], 1)
            link(nc.vector.memset(experts_row[:, :], 0.0))
            link(nc.vector.tensor_copy(experts_row[:, 2:2 + BLOCKS], table_bank[0:1, 0:BLOCKS]))
            six = experts_row[:, :].rearrange("o (g k) -> o g k", k=6)
            link(nc.vector.tensor_copy(packing[:, :], six[:, :, 5]))
            for k in (4, 3, 2, 1):
                link(nc.vector.scalar_tensor_tensor(out=packing[:, :], in0=packing[:, :], scalar=float(NE), in1=six[:, :, k],
                                                    op0=ALU.mult, op1=ALU.add))
            nc.vector.scalar_tensor_tensor(out=expert_groups[:, :], in0=packing[:, :], scalar=float(NE), in1=six[:, :, 0],
                                           op0=ALU.mult, op1=ALU.add).then_inc(s["table_ok"], 1)

            def expert_steps(q, u, i):
                if block_live(q, 2):
                    wait(dve, "sig_ok", q - 1)
                    wait(dve, "h_ok", q - 2)
                    nc.vector.tensor_tensor(glu[:, :, :], gate[:, u % 2], sig[:, u % 2], ALU.mult).then_inc(s["glu_ok"], 1)
                    wait(dve, "glu_ok", q - 1)
                    wait(dve, "ht_mm", q - 3)
                    nc.vector.scalar_tensor_tensor(out=hidden[:, u % 2], in0=up[:, u % 2], scalar=1.0 - LIMIT,
                                                   in1=glu[:, :, :], op0=ALU.max, op1=ALU.mult).then_inc(s["h_ok"], 1)
                if block_live(q, 1):
                    wait(dve, "gu_mm", q)
                    wait(dve, "h_ok", q - 2)
                    b = (u + 1) % 2
                    bank = gu_bank[b][:, :].rearrange("p (t c f) -> p t c f", t=2, c=2)
                    nc.vector.tensor_scalar(gate[:, b], bank[:, :, 0, :], scale_from[:, 5:6], LIMIT, ALU.mult, ALU.min).then_inc(s["gate_ok"], 1)
                    nc.vector.tensor_scalar(up[:, b], bank[:, :, 1, :], scale_from[:, 5:6], 1.0 + LIMIT, ALU.mult, ALU.min).then_inc(s["up_ok"], 1)
                if block_live(q, 3):
                    wait(dve, "ht_hi", q - 2)
                    nc.vector.tensor_tensor(hT[:, (u + 1) % 2, LO, :], ht_bank[(u + 1) % 2][:, 0:256], hT[:, (u + 1) % 2, HI, :],
                                            ALU.subtract).then_inc(s["ht_lo"], 1)

            over_blocks(dve, expert_steps)

            for g in range(NB // 4):
                dve.wait_ge(results_in[g % 4], 32 * (g // 4 + 1))
                nc.vector.tensor_tensor(r_in[:, g % 4, 0], r_in[:, g % 4, 0], r_in[:, g % 4, 1], ALU.add).then_inc(s["sum_ok"], 1)
                dve.wait_ge(s["sum_ok"], g + 1)
                rows = x_sb[:, 4 * g:4 * g + 4, :]
                nc.vector.scalar_tensor_tensor(out=rows, in0=r_in[:, g % 4, 0], scalar=scale_from[:, 3:4], in1=rows,
                                               op0=ALU.mult, op1=ALU.add).then_inc(s["fin_ok"], 1)

        @block.tensor
        def _(pe):
            def three(dst, a_hi, a_lo, b_hi, b_lo, start=True, stop=True):
                nc.tensor.matmul(dst, a_hi, b_hi, start=start, stop=False)
                nc.tensor.matmul(dst, a_hi, b_lo, start=False, stop=False)
                return nc.tensor.matmul(dst, a_lo, b_hi, start=False, stop=stop)

            def prep(q, bank=misc_bank):
                wait(pe, "xhat_ok", q * 2 + 2)
                wait(pe, "ctx_ok", q + 1)
                for w in range(2):
                    for j in range(2):
                        last = nc.tensor.transpose(bank[:, (2 * w + j) * P:(2 * w + j + 1) * P], xhat[:, w, j, :], ident[:, :])
                last.then_inc(s["prep_mm"], 1)

            def project_qk(q, par, t, bank=qk_bank):
                which, blk = (t % 4) // 2, 4 * (t // 4) + 2 * (t % 2)
                src = slice(which * 256, which * 256 + 256)
                if isinstance(q, int) and q == 0:
                    wait(pe, "qk_split", t - 1)
                elif isinstance(q, int) and q == 1 and t == 0:
                    wait(pe, "qk_split", 8)
                else:
                    wait(pe, "qk_copied", q * 8 + t - 8)
                for i in range(2):
                    col = which * INNER + (blk + i) * P
                    last = three(bank[:, i * 256:i * 256 + 256], w_qkv[:, HI, col:col + P], w_qkv[:, LO, col:col + P],
                                 xT[:, par, HI, src], xT[:, par, LO, src])
                last.then_inc(s["qk_mm"], 1)

            def project_v(par, k, bank=misc_bank):
                tok = slice(256 + (k // 2) * P, 256 + (k // 2) * P + P)
                cols = slice(2 * INNER + (k % 2) * 512, 2 * INNER + (k % 2) * 512 + 512)
                three(bank[:, :], xT[:, par, HI, tok], xT[:, par, LO, tok], w_qkv[:, HI, cols], w_qkv[:, LO, cols]
                      ).then_inc(s["v_mm"], 1)

            pe.wait_ge(s["consts"], 7)
            pe.wait_ge(s["in_small"], 16 * 5)
            nc.tensor.transpose(out_bank[:, 0:NE], wg_nat[:, :], ident[0:NE, 0:NE]).then_inc(s["wgT_mm"], 1)
            prep(0)
            wait(pe, "misc_free", 1)
            for t in range(8):
                pe.wait_ge(s["w_lo"], min(t // 2 + 1, 3))
                project_qk(0, 0, t, first_bank[t % 2])
                if t >= 4:
                    wait(pe, "misc_free", max(t - 4, 1))
                    project_v(0, t - 4, first_v_bank[t % 2])
                if t == 5:
                    prep(1, ot_bank)
            pe.wait_ge(s["ones_v"], 2)

            def scores(par, r, n):
                j, half, odd = r // 4, (r // 2) % 2, r % 2
                rows, tok = slice(64 * odd, 64 * odd + 64), slice(j * P, j * P + P)
                wait(pe, "exp_ok", n - 1)
                for k in range(4):
                    a = [qk[rows, par, 0, h, 4 * half + k, tok] for h in range(2)]
                    b = [qk[rows, par, 1, h, 4 * half + k, tok] for h in range(2)]
                    last = three(score_bank[r % 2][:, k * P:(k + 1) * P], a[HI], a[LO], b[HI], b[LO])
                last.then_inc(s["score_mm"], 1)

            def steps(p, par):
                for r in range(STEPS):
                    if isinstance(p, int) and (p, r) == (1, 0):
                        pe.wait_ge(s["wgT_ok"], 1)
                    n = p * STEPS + r
                    if live(p, r, 0):
                        if r in (0, 2):
                            wait(pe, "qk_split", p * 8 + 4 + 2 * r)
                        scores(par, r, n)
                    if live(p, r, 2):
                        wait(pe, "exp_ok", n - 1)
                        wait(pe, "pt_lo", n - 2)
                        for k in range(4):
                            last = nc.tensor.transpose(pt_bank[:, k * P:(k + 1) * P], probs[:, r % 2, k, :], ident[:, :])
                        last.then_inc(s["pt_mm"], 1)
                    if pair_live(p + 1):
                        project_qk(p + 1, 1 - par, r)
                    item = ORDER[r]
                    if pair_live(p + USES[item]):
                        wait(pe, "misc_free", misc_before(p, item))
                        if item[0] == "V":
                            project_v(1 - par, int(item[1]))
                        elif item == "PREP":
                            prep(p + 2)
                        elif item == "RANK":
                            wait(pe, "chosen_ok", p - 1)
                            c0, c1 = chosen16[:, 0, :], chosen16[:, 1, :]
                            nc.tensor.matmul(misc_bank[:, 0:NE], before16[:, :], c0, start=True, stop=True)
                            for at, first in ((NE, before16), (2 * NE, ones16)):
                                nc.tensor.matmul(misc_bank[:, at:at + NE], first[:, :], c1, start=True, stop=False)
                                last = nc.tensor.matmul(misc_bank[:, at:at + NE], ones16[:, :], c0, start=False, stop=True)
                            last.then_inc(s["rank_mm"], 1)
                        elif item == "YT":
                            wait(pe, "y_ok", p * 2 - 2)
                            for j in range(2):
                                last = nc.tensor.transpose(misc_bank[:, j * P:(j + 1) * P], y[:, j, :], ident[:, :])
                            last.then_inc(s["yT_mm"], 1)
                        else:
                            for j in range(2):
                                last = nc.tensor.matmul(misc_bank[:, j * NE:(j + 1) * NE], yT[:, j * P:(j + 1) * P], wg_T[:, :],
                                                        start=True, stop=True)
                            last.then_inc(s["lg_mm"], 1)
                    if live(p, r, 3):
                        vp = par if r >= 3 else 1 - par
                        rr = (r - 3) % STEPS
                        j, half, odd = rr // 4, (rr // 2) % 2, rr % 2
                        wait(pe, "pt_lo", n - 2)
                        wait(pe, "o_ok", n - 3)
                        if r == 3 and isinstance(p, int) and p < 2:
                            wait(pe, "misc_free", 6 if p == 0 else misc_before(0, "V3") + 1)
                        for k in range(4):
                            head, tok = 8 * half + 2 * k + odd, slice(k * P, k * P + P)
                            last = three(o_bank[:, k * (DH + 1):(k + 1) * (DH + 1)], pT[:, (r + 1) % 2, HI, tok], pT[:, (r + 1) % 2, LO, tok],
                                         v[:, vp, HI, j, head, 0:DH + 1], v[:, vp, LO, j, head, 0:DH + 1])
                        last.then_inc(s["pv_mm"], 1)
                    if live(p, r, 5):
                        wait(pe, "o_ok", n - 4)
                        wait(pe, "ot_lo", n - 5)
                        for k in range(2):
                            last = nc.tensor.transpose(ot_bank[:, k * P:(k + 1) * P], o_nat[:, (r - 5) % 4, k * P:(k + 1) * P], ident[:, :])
                        last.then_inc(s["ot_mm"], 1)
                    if live(p, r, 6):
                        wait(pe, "ot_lo", n - 5)
                        if isinstance(p, int) and (p, r) == (0, 6):
                            pe.wait_ge(s["wo_lo"], 1)
                        if r % 4 == 2:
                            wait(pe, "x1_ok", p * 2 - 1 + r // 4)
                        for k in range(2):
                            blk = 2 * ((r - 6) % 4) + k
                            last = three(out_bank[:, 0:P], oT[:, r % 2, HI, k * P:(k + 1) * P], oT[:, r % 2, LO, k * P:(k + 1) * P],
                                         w_out[:, HI, blk, :], w_out[:, LO, blk, :], start=(blk == 0), stop=(blk == 7))
                        last.then_inc(s["out_mm"], 1)

            over_pairs(pe, steps)

            pe.wait_ge(s["table_cols"], 1)
            for c in range(2):
                last = nc.tensor.matmul(table_bank[0:1, c * P:(c + 1) * P], table_f[:, c:c + 1], ident[:, :], start=True, stop=True)
            last.then_inc(s["table_mm"], 1)
            pe.wait_ge(s["table_ok"], 2)
            pe.wait_ge(s["gu_lo"], 8)
            pe.wait_ge(s["bias_in"], 16 * 4)

            def plus_bias(dst, a_hi, a_lo, b_hi, b_lo, bias):
                nc.tensor.matmul(dst, ones16[0:2, :], bias, start=True, stop=False)
                return three(dst, a_hi, a_lo, b_hi, b_lo, start=False)

            known = {}

            def load_experts(v, i):
                g = (v + 1) // 3
                if g not in known:
                    six = pe.value_load(expert_groups[0:1, bass.ds(i * (NBUF // 3) + g, 1)], min_val=0, max_val=NE ** 6 - 1)
                    known[g] = [six // NE ** k % NE for k in range(6)]

            def experts_of(v):
                g, at = (v + 1) // 3, 2 * ((v + 1) % 3)
                return known[g][at:at + 2]

            def expert_steps(q, u, i):
                if u == 0:
                    known.clear()
                if block_live(q, 1):
                    load_experts(u - 1, i)
                if block_live(q, 0):
                    pe.wait_ge(block_in[u], i * 32 + 32)
                    wait(pe, "t_ok", q - 1)
                    for t in range(2):
                        for h in range(2):
                            at = (2 * t + h) * P
                            last = nc.tensor.transpose(t_bank[u % 2][:, at:at + P], rows16[:, u, t, h * P:(h + 1) * P], ident16[:, :])
                    last.then_inc(s["t_mm"], 1)
                if block_live(q, 1):
                    wait(pe, "t_ok", q)
                    wait(pe, "up_ok", q - 2)
                    b = (u + 1) % 2
                    for t, e in enumerate(experts_of(u - 1)):
                        last = plus_bias(gu_bank[b][:, t * 256:(t + 1) * 256], bT[:, b, t, HI, :], bT[:, b, t, LO, :],
                                         w_gu[:, HI, e, :], w_gu[:, LO, e, :], bias_gu[:, e, :])
                    last.then_inc(s["gu_mm"], 1)
                if block_live(q, 0) and u + 1 < NBUF:
                    load_experts(u, i)
                if block_live(q, 4):
                    load_experts(u - 4, i)
                if block_live(q, 3):
                    wait(pe, "h_ok", q - 2)
                    wait(pe, "ht_lo", q - 4)
                    for t in range(2):
                        last = nc.tensor.transpose(ht_bank[(u + 1) % 2][:, t * P:(t + 1) * P], hidden[:, (u + 1) % 2, t, :], ident[:, :])
                    last.then_inc(s["ht_mm"], 1)
                if block_live(q, 4):
                    wait(pe, "ht_lo", q - 3)
                    wait(pe, "z_ok", q * 2 - 10)
                    b = u % 2
                    for t, e in enumerate(experts_of(u - 4)):
                        last = plus_bias(d_bank[b][:, t * P:(t + 1) * P], hT[:, b, HI, t * P:(t + 1) * P], hT[:, b, LO, t * P:(t + 1) * P],
                                         w_d[:, HI, e, :], w_d[:, LO, e, :], bias_d[:, e, :])
                    last.then_inc(s["d_mm"], 1)

            over_blocks(pe, expert_steps)


_INS = ["x", "ctx_1024", "L0_xattn_W_qkv", "L0_xattn_W_out", "L0_xattn_b_out", "L0_ffn_Wg", "L0_ffn_bg",
        "L0_ffn_Wgu", "L0_ffn_bgu", "L0_ffn_Wd", "L0_ffn_bd"]


def kernel(**inputs):
    import numpy as _np
    import concourse.bacc as _bacc
    from concourse import mybir as _mybir
    from concourse.bass_utils import run_bass_kernel_spmd as _run

    nc = _bacc.Bacc("TRN2", target_bir_lowering=False, num_devices=1)
    arrays, args = {}, []
    for name in _INS:
        a = _np.ascontiguousarray(inputs[name])
        arrays[f"in_{name}_dram"] = a
        args.append(nc.dram_tensor(f"in_{name}_dram", a.shape, _mybir.dt.from_np(a.dtype), kind="ExternalInput").ap())
    shape = inputs["x"].shape
    args.append(nc.dram_tensor("out_0_dram", shape, _mybir.dt.float32, kind="ExternalOutput").ap())
    xattn_moe_kernel(nc, *args)
    r = _run(nc, [arrays], core_ids=[0])
    return r.results[0]["out_0_dram"]
```
